# Optimizing a Trainium2 kernel written in Bass

```python
import numpy as np
import jax
import jax.numpy as jnp

def _softmax(x, axis=-1):
    return jax.nn.softmax(x, axis=axis)

def _gelu(x):
    return jax.nn.gelu(x, approximate=True)

def _silu(x):
    return jax.nn.silu(x)

def _sigmoid(x):
    return jax.nn.sigmoid(x)

def _layernorm(x, axis=-1, eps=1e-05):
    m = jnp.mean(x, axis=axis, keepdims=True)
    v = jnp.var(x, axis=axis, keepdims=True)
    return (x - m) / jnp.sqrt(v + eps)

def _scatter_add(tgt, idx, src, axis=0):
    return tgt.at[idx].add(src)

def _segment_sum(src, seg, n):
    return jax.ops.segment_sum(src, seg, n)
kernel_name = 'mk_flamingo_gated_d1_seqx_r4_fc3242'

def setup_inputs(seed: int=0):
    np.random.seed(seed)
    _w = jnp.asarray

    def _rec_inputs():
        import jax
        import jax.numpy as jnp
        _rk = jax.random.key(seed)
        x = -0.0002928 + 1 * jax.random.normal(jax.random.fold_in(_rk, 1), (8, 256, 256), jnp.float32)
        _lenS = 256 - jax.random.randint(jax.random.fold_in(_rk, 7), (8,), 0, max(1, 256 // 4) + 1, jnp.int32)
        _lenS2 = 256 - jax.random.randint(jax.random.fold_in(_rk, 8), (8,), 0, max(1, 256 // 4) + 1, jnp.int32)
        _ctx_1024P = jax.random.normal(jax.random.fold_in(_rk, 11), (8, 16, 256), jnp.float32)
        _ctx_1024c = jax.random.dirichlet(jax.random.fold_in(_rk, 511), 0.3 * jnp.ones((16,), jnp.float32), (8, 256))
        _ctx_1024t = jnp.einsum('bsk,bkd->bsd', _ctx_1024c, _ctx_1024P)
        _ctx_1024t = _ctx_1024t * jax.lax.rsqrt(jnp.mean(jnp.square(_ctx_1024t)) + 1e-12) * 0.953939
        ctx_1024 = -1.39393e-06 + 0.999914 * (_ctx_1024t + 0.3 * jax.random.normal(jax.random.fold_in(_rk, 611), (8, 256, 256), jnp.float32))
        _g = jax.random.normal(jax.random.fold_in(_rk, 9001), (2, 1), jnp.float32)
        _g = jnp.sign(_g) * jnp.maximum(jnp.abs(_g), 1.0) + (_g == 0) * 1.0
        g_xattn = _g[0]
        g_ffn = _g[1]
        return (x, ctx_1024, g_xattn, g_ffn)
    x, ctx_1024, g_xattn, g_ffn = _rec_inputs()

    def _L0_xattn_setup():
        import jax, jax.numpy as jnp
        import numpy as np
        B, S, D, NH = (2, 512, 256, 8)
        DH = D // NH
        EPS = 1e-06
        LN_EPS = 1e-05

        def _mlstm_cell(q, k, v, igate_w, igate_b, fgate_w, fgate_b, ln_scale):
            Slen = q.shape[0]
            ifg = jnp.concatenate([q, k, v], axis=-1)
            ig = (ifg @ igate_w.T + igate_b).T
            fg = (ifg @ fgate_w.T + fgate_b).T
            qh = q.reshape(Slen, NH, DH).transpose(1, 0, 2)
            kh = k.reshape(Slen, NH, DH).transpose(1, 0, 2)
            vh = v.reshape(Slen, NH, DH).transpose(1, 0, 2)
            log_f = jax.nn.log_sigmoid(fg)
            cs = jnp.cumsum(log_f, axis=1)
            fg_mat = cs[:, :, None] - cs[:, None, :]
            mask = jnp.tril(jnp.ones((Slen, Slen), dtype=bool))
            log_fg_mat = jnp.where(mask, fg_mat, -jnp.inf)
            log_D = log_fg_mat + ig[:, None, :]
            max_log_D = jnp.max(log_D, axis=-1, keepdims=True)
            D_mat = jnp.exp(log_D - max_log_D)
            qk = jnp.einsum('hsd,htd->hst', qh, kh) / np.sqrt(DH)
            C = qk * D_mat
            normalizer = jnp.maximum(jnp.abs(C.sum(axis=-1, keepdims=True)), jnp.exp(-max_log_D))
            h = jnp.einsum('hst,htd->hsd', C / (normalizer + EPS), vh)
            h = h.transpose(1, 0, 2).reshape(Slen, D)
            mu = h.mean(axis=-1, keepdims=True)
            var = h.var(axis=-1, keepdims=True)
            return (h - mu) / jnp.sqrt(var + LN_EPS) * ln_scale
        key = jax.random.key(seed)
        ks = jax.random.split(key, 8)
        rnd = lambda k, sh, s=1.0: jax.random.normal(k, sh, dtype=jnp.float32) * s
        return {'q': rnd(ks[0], (B, S, D)), 'k': rnd(ks[1], (B, S, D)), 'v': rnd(ks[2], (B, S, D)), 'igate_w': rnd(ks[3], (NH, 3 * D), 0.02), 'igate_b': jnp.linspace(3.0, 6.0, NH, dtype=jnp.float32), 'fgate_w': rnd(ks[4], (NH, 3 * D), 0.02), 'fgate_b': rnd(ks[5], (NH,), 0.3162278), 'ln_scale': jnp.ones((D,), dtype=jnp.float32)}
    _L0_xattn_all = _L0_xattn_setup()
    _L0_xattn_in = {k: v for k, v in _L0_xattn_all.items() if k in ('igate_w', 'igate_b', 'fgate_w', 'fgate_b', 'ln_scale')}
    del _L0_xattn_all

    def _L0_ffn_setup():
        import jax, jax.numpy as jnp
        import numpy as np
        D = 256
        H = 16
        HD = D // H
        L = 64
        E = 8
        B, T = (4, 512)
        EPS = 1e-06

        def _glorot(k, shape):
            fan_in, fan_out = (shape[-2], shape[-1])
            lim = np.sqrt(6.0 / (fan_in + fan_out)).astype(np.float32)
            return jax.random.uniform(k, shape, jnp.float32, -lim, lim)

        def _rmsnorm(x, gamma):
            return gamma * x * jax.lax.rsqrt(jnp.mean(x * x, axis=-1, keepdims=True) + EPS)
        key = jax.random.key(seed)
        ks = jax.random.split(key, 8)
        return {'x': jax.random.normal(ks[0], (B, T, D), jnp.float32), 'gamma1': jnp.ones((D,), jnp.float32), 'Wq': _glorot(ks[1], (D, D)), 'bq': jnp.zeros((D,), jnp.float32), 'Wdown': _glorot(ks[2], (D, L)), 'bdown': jnp.zeros((L,), jnp.float32), 'Wup': _glorot(ks[3], (L, 2 * D)), 'bup': jnp.zeros((2 * D,), jnp.float32), 'Wo': _glorot(ks[4], (D, D)), 'bo': jnp.zeros((D,), jnp.float32), 'gamma2': jnp.ones((D,), jnp.float32), 'Wg': _glorot(ks[5], (D, E)), 'bg': jnp.zeros((E,), jnp.float32), 'We': _glorot(ks[6], (E, D, D))}
    _L0_ffn_all = _L0_ffn_setup()
    _L0_ffn_in = {k: v for k, v in _L0_ffn_all.items() if k in ('gamma1', 'Wq', 'bq', 'Wdown', 'bdown', 'Wup', 'bup', 'Wo', 'bo', 'gamma2', 'Wg', 'bg', 'We')}
    del _L0_ffn_all
    return {'x': x, 'ctx_1024': ctx_1024, 'g_xattn': g_xattn, 'g_ffn': g_ffn, 'L0_xattn_igate_w': _L0_xattn_in['igate_w'], 'L0_xattn_igate_b': _L0_xattn_in['igate_b'], 'L0_xattn_fgate_w': _L0_xattn_in['fgate_w'], 'L0_xattn_fgate_b': _L0_xattn_in['fgate_b'], 'L0_xattn_ln_scale': _L0_xattn_in['ln_scale'], 'L0_ffn_gamma1': _L0_ffn_in['gamma1'], 'L0_ffn_Wq': _L0_ffn_in['Wq'], 'L0_ffn_bq': _L0_ffn_in['bq'], 'L0_ffn_Wdown': _L0_ffn_in['Wdown'], 'L0_ffn_bdown': _L0_ffn_in['bdown'], 'L0_ffn_Wup': _L0_ffn_in['Wup'], 'L0_ffn_bup': _L0_ffn_in['bup'], 'L0_ffn_Wo': _L0_ffn_in['Wo'], 'L0_ffn_bo': _L0_ffn_in['bo'], 'L0_ffn_gamma2': _L0_ffn_in['gamma2'], 'L0_ffn_Wg': _L0_ffn_in['Wg'], 'L0_ffn_bg': _L0_ffn_in['bg'], 'L0_ffn_We': _L0_ffn_in['We']}

def reference(x, ctx_1024, g_xattn, g_ffn, L0_xattn_igate_w, L0_xattn_igate_b, L0_xattn_fgate_w, L0_xattn_fgate_b, L0_xattn_ln_scale, L0_ffn_gamma1, L0_ffn_Wq, L0_ffn_bq, L0_ffn_Wdown, L0_ffn_bdown, L0_ffn_Wup, L0_ffn_bup, L0_ffn_Wo, L0_ffn_bo, L0_ffn_gamma2, L0_ffn_Wg, L0_ffn_bg, L0_ffn_We):
    import jax
    import jax.numpy as jnp

    def _L0_xattn_ref(q, k, v, igate_w, igate_b, fgate_w, fgate_b, ln_scale):
        import jax, jax.numpy as jnp
        import numpy as np
        B, S, D, NH = (2, 512, 256, 8)
        DH = D // NH
        EPS = 1e-06
        LN_EPS = 1e-05

        def _mlstm_cell(q, k, v, igate_w, igate_b, fgate_w, fgate_b, ln_scale):
            Slen = q.shape[0]
            ifg = jnp.concatenate([q, k, v], axis=-1)
            ig = (ifg @ igate_w.T + igate_b).T
            fg = (ifg @ fgate_w.T + fgate_b).T
            qh = q.reshape(Slen, NH, DH).transpose(1, 0, 2)
            kh = k.reshape(Slen, NH, DH).transpose(1, 0, 2)
            vh = v.reshape(Slen, NH, DH).transpose(1, 0, 2)
            log_f = jax.nn.log_sigmoid(fg)
            cs = jnp.cumsum(log_f, axis=1)
            fg_mat = cs[:, :, None] - cs[:, None, :]
            mask = jnp.tril(jnp.ones((Slen, Slen), dtype=bool))
            log_fg_mat = jnp.where(mask, fg_mat, -jnp.inf)
            log_D = log_fg_mat + ig[:, None, :]
            max_log_D = jnp.max(log_D, axis=-1, keepdims=True)
            D_mat = jnp.exp(log_D - max_log_D)
            qk = jnp.einsum('hsd,htd->hst', qh, kh) / np.sqrt(DH)
            C = qk * D_mat
            normalizer = jnp.maximum(jnp.abs(C.sum(axis=-1, keepdims=True)), jnp.exp(-max_log_D))
            h = jnp.einsum('hst,htd->hsd', C / (normalizer + EPS), vh)
            h = h.transpose(1, 0, 2).reshape(Slen, D)
            mu = h.mean(axis=-1, keepdims=True)
            var = h.var(axis=-1, keepdims=True)
            return (h - mu) / jnp.sqrt(var + LN_EPS) * ln_scale
        return jax.vmap(lambda qq, kk, vv: _mlstm_cell(qq, kk, vv, igate_w, igate_b, fgate_w, fgate_b, ln_scale))(q, k, v)

    def _L0_ffn_ref(x, gamma1, Wq, bq, Wdown, bdown, Wup, bup, Wo, bo, gamma2, Wg, bg, We):
        import jax, jax.numpy as jnp
        import numpy as np
        D = 256
        H = 16
        HD = D // H
        L = 64
        E = 8
        B, T = (4, 512)
        EPS = 1e-06

        def _glorot(k, shape):
            fan_in, fan_out = (shape[-2], shape[-1])
            lim = np.sqrt(6.0 / (fan_in + fan_out)).astype(np.float32)
            return jax.random.uniform(k, shape, jnp.float32, -lim, lim)

        def _rmsnorm(x, gamma):
            return gamma * x * jax.lax.rsqrt(jnp.mean(x * x, axis=-1, keepdims=True) + EPS)
        b, t = (x.shape[0], x.shape[1])
        h = _rmsnorm(x, gamma1)
        q = (h @ Wq + bq).reshape(b, t, H, HD)
        kv = ((h @ Wdown + bdown) @ Wup + bup).reshape(b, t, H, 2 * HD)
        k, v = jnp.split(kv, 2, axis=-1)
        att = jnp.einsum('bthd,btgd->bthg', q, k) / np.sqrt(HD).astype(np.float32)
        att = jax.nn.softmax(att, axis=-1)
        out = jnp.einsum('bthg,btgd->bthd', att, v).reshape(b, t, D)
        x = x + (out @ Wo + bo)
        h2 = _rmsnorm(x, gamma2)
        gate = jax.nn.softmax(h2 @ Wg + bg, axis=-1)
        combined = jnp.einsum('btd,edf,bte->btf', h2, We, gate)
        return x + combined
    x = x + jnp.tanh(g_xattn[0]) * _L0_xattn_ref(_layernorm(x, axis=-1), ctx_1024, ctx_1024, L0_xattn_igate_w, L0_xattn_igate_b, L0_xattn_fgate_w, L0_xattn_fgate_b, L0_xattn_ln_scale)
    x = x + jnp.tanh(g_ffn[0]) * _L0_ffn_ref(_layernorm(x, axis=-1), L0_ffn_gamma1, L0_ffn_Wq, L0_ffn_bq, L0_ffn_Wdown, L0_ffn_bdown, L0_ffn_Wup, L0_ffn_bup, L0_ffn_Wo, L0_ffn_bo, L0_ffn_gamma2, L0_ffn_Wg, L0_ffn_bg, L0_ffn_We)
    return x

_drawn_inputs = setup_inputs


def setup_inputs(seed=0):
    import zlib

    import numpy as np

    out = dict(_drawn_inputs(seed))
    spreads = {'L0_xattn_ln_scale': (1.0, 0.2),
     'L0_ffn_gamma1': (1.0, 0.2),
     'L0_ffn_bq': (0.0, 0.412),
     'L0_ffn_bdown': (0.0, 0.392),
     'L0_ffn_bup': (0.0, 0.1),
     'L0_ffn_bo': (0.0, 0.1),
     'L0_ffn_gamma2': (1.0, 0.2),
     'L0_ffn_bg': (0.0, 0.1)}
    factors = {}
    for name, (base, spread) in spreads.items():
        noise = np.random.default_rng([zlib.crc32(name.encode()), seed]).standard_normal(out[name].shape)
        drawn = base * np.exp(spread * noise) if base else spread * noise
        out[name] = jnp.asarray(drawn.astype(out[name].dtype))
    for name, factor in factors.items():
        out[name] = (out[name] * factor).astype(out[name].dtype)
    return out
```

```python
from contextlib import ExitStack

import concourse.bass as bass
from concourse import mybir

F32 = mybir.dt.float32
F32R = mybir.dt.float32r
BF16 = mybir.dt.bfloat16
F16 = mybir.dt.float16
ALU = mybir.AluOpType
ACT = mybir.ActivationFunctionType
AX = mybir.AxisListType

P = 128
MASK = 1e30
LN_EPS = 1e-5
RMS_EPS = 1e-6
CELL_EPS = 1e-6

SLOTS = ["F_norm", "F_turn", "X0", "F_down", "M0", "F_qkv", "M1", "X1", "M2", "X2", "M3",
         "F_scores", "M4", "F_max", "X3", "F_shift", "F_split", "X4", "F_values", "M5", "F_o", "X5",
         "M6", "X6", "F_turn_o", "X7", "F_wo", "M7", "F_turn_h2", "M8", "F_gate"]


class Chain:

    def __init__(self, eng, sem, base, per_round):
        self.eng, self.sem, self.base, self.per_round, self.n = eng, sem, base, per_round, 0

    def step(self, ins):
        ins.then_inc(self.sem, 1)
        self.n += 1
        assert self.n <= self.per_round
        self.eng.wait_ge(self.sem, self.base + self.n)


def wait(eng, sem, value):
    if isinstance(value, int) and value <= 0:
        return
    eng.wait_ge(sem, value)


def build(nc, x, ctx_in, g_xattn, g_ffn, igate_w, igate_b, fgate_w, fgate_b, ln_scale,
          gamma1, Wq, bq, Wdown, bdown, Wup, bup, Wo, bo, gamma2, Wg, bg, We, out):
    B, S, D = x.shape
    NH = igate_w.shape[0]
    DH = D // NH
    H = 16
    HD = D // H
    L = Wdown.shape[1]
    E = Wg.shape[1]
    NJ = S // P
    NC = D // P
    T8 = P // HD
    NG = S // T8
    R = NH * B
    VW = DH + 1
    TRI = P + S
    GP = 32 + NH
    EC = 512 // D
    NX = NJ * E // EC
    QSCALE = float(DH) ** -0.5
    HSCALE = float(HD) ** -0.5
    BIAS = {"q": (0, D), "up": (D, 2 * D), "o": (3 * D, D), "g": (4 * D, 32)}
    NB = 4 * D + 32
    assert (NJ, NC, T8, NG, R) == (2, 2, 8, 32, 64) and NX == 8 and L == 64 and NH == 8

    with ExitStack() as es:
        def sb(name, shape, dt=F32):
            return es.enter_context(nc.sbuf_tensor(name, shape, dt))

        def psum(name):
            return es.enter_context(nc.psum_tensor(name, [P, 512], F32))

        def sem(name):
            return es.enter_context(nc.semaphore(name))

        es.enter_context(nc.allow_non_contiguous_dma(reason="small vectors, once"))

        ident = sb("ident", [P, P])
        neg_ident = sb("neg_ident", [P, P])
        ident_bf = sb("ident_bf", [P, P], BF16)
        mask_bf = sb("mask_bf", [P, P], BF16)
        head_sel = sb("head_sel", [3 * NH, NH, P], BF16)
        block_ones = sb("block_ones", [P, P], F16)
        ones3 = sb("ones3", [3, P], BF16)
        minus_half = sb("minus_half", [P, 4])
        we_hi = sb("we_hi", [P, NC, E * D], F32R)
        we_lo = sb("we_lo", [P, NC, E * D], F32R)
        wq_raw = sb("wq_raw", [P, NC, D])
        wq_hi = sb("wq_hi", [P, NC, D], F32R)
        wq_lo = sb("wq_lo", [P, NC, D], F32R)
        wo_raw = sb("wo_raw", [P, NC, D])
        wo_hi = sb("wo_hi", [P, NC, D], F32R)
        wo_lo = sb("wo_lo", [P, NC, D], F32R)
        wd_raw = sb("wd_raw", [P, NC, L])
        wd_hi = sb("wd_hi", [P, NC, 2, L], F32R)
        wd_lo = sb("wd_lo", [P, NC, 2, L], F32R)
        wu_raw = sb("wu_raw", [P, 2 * D])
        wu_hi = sb("wu_hi", [P, 2 * D], F32R)
        wu_lo = sb("wu_lo", [L, 2 * D], F32R)
        wg_raw = sb("wg_raw", [P, NC, 32])
        wg_hi = sb("wg_hi", [P, NC, 32], F32R)
        wg_lo = sb("wg_lo", [P, NC, 32], F32R)
        bias3 = sb("bias3", [3, NB], BF16)
        bd_col = sb("bd_col", [P, 1])
        g1_col = sb("g1_col", [P, NC])
        g2_col = sb("g2_col", [P, NC])
        gx_col = sb("gx_col", [P, 1])
        gf_col = sb("gf_col", [P, 1])
        tx_col = sb("tx_col", [P, 1])
        tf_col = sb("tf_col", [P, 1])
        ls_row = sb("ls_row", [P, D])
        lst_row = sb("lst_row", [P, D])
        gw_raw = sb("gw_raw", [GP, 3 * D])
        gw_kv = sb("gw_kv", [GP, D])
        gw_t = sb("gw_t", [P, 2 * NC, GP])
        gb_col = sb("gb_col", [GP, 1])
        bs = [sb(f"bs{i}", [P, NJ, 6]) for i in range(2)]
        mv = [sb(f"mv{i}", [P, NJ, 2]) for i in range(2)]
        rstd = [sb(f"rstd{i}", [P, NJ]) for i in range(2)]
        qt_all = sb("qt_all", [P, NC, B * S])
        ct_all = sb("ct_all", [P, NC, B * S])
        m_part = sb("m_part", [R, 3, S], BF16)
        a_t = sb("a_t", [P, NJ, R])
        en_t = sb("en_t", [P, NJ, R])
        qt = sb("qt", [P, NC, S])
        ct = sb("ct", [P, NC, S])
        vals = sb("vals", [P, NJ, NH, VW])
        m_rows = sb("m_rows", [3 * NH, S], BF16)
        a_b = sb("a_b", [P, NJ, NH])
        decay = sb("decay", [P, 2, TRI])
        cell = sb("cell", [P, 2, TRI])
        hm = sb("hm", [P, NJ, NH, VW])
        en_b = sb("en_b", [P, NJ, NH])
        nrm = sb("nrm", [P, NJ, NH])
        fbs = sb("fbs", [P, NJ, 6])
        fmv = sb("fmv", [P, NJ, 2])
        frs = sb("frs", [P, 2, NJ])
        fpw = sb("fpw", [P, 2, NJ])
        ht_hi = sb("ht_hi", [P, NC, S], F32R)
        ht_lo = sb("ht_lo", [P, NC, S], F32R)
        dt = sb("dt", [P, S], F32R)
        q_nat = sb("q_nat", [P, NJ, HD, 2 * H], F16)
        kv_nat = sb("kv_nat", [P, NJ, H, 4 * H], F16)
        q_grp = sb("q_grp", [P, NG, 2 * H], F16)
        smax = sb("smax", [P, 4 * T8])
        smax_x = sb("smax_x", [P, 4 * T8, H])
        prob_hi = sb("prob_hi", [P, NG * H], F16)
        prob_lo = sb("prob_lo", [P, NG * H], F16)
        ot_hi = sb("ot_hi", [P, NC, S], F32R)
        ot_lo = sb("ot_lo", [P, NC, S], F32R)
        h2_hi = sb("h2_hi", [P, NC, S], F32R)
        h2_lo = sb("h2_lo", [P, NC, S], F32R)
        lg = sb("lg", [P, NJ, E])
        gmax = sb("gmax", [P, NJ])
        gate = sb("gate", [P, NJ, E])
        work = sb("work", [P, 14 * NJ * D])

        def part(k, parts=P):
            return work[0:parts, k * NJ * D:(k + 1) * NJ * D]

        xb, cb, xn = ([part(2 * k + i).rearrange("p (j d) -> p j d", j=NJ) for i in range(2)] for k in range(3))
        gates = work[0:GP, 6 * NJ * D:10 * NJ * D].rearrange("p (b s) -> p b s", b=B)
        ig, fg, row_a, row_b, row_c, row_m, en_row, zeros = (
            work[0:R, 10 * NJ * D + k * S:10 * NJ * D + (k + 1) * S] for k in range(8))
        we_raw = work[:, 0:NC * E * D].rearrange("p (c e n) -> p c e n", c=NC, e=E)
        x1, y, hn, o_nat, x2, base, h2, acc, xf, hcell = (
            part(k).rearrange("p (j d) -> p j d", j=NJ) for k in range(10))
        sc_sb, prob, rsum, o_grp = (part(k) for k in range(10, 14))
        kv_all = sb("kv_all", [P, NG * T8 * 4 * H], F16)
        kv_grp = kv_all[:, :].rearrange("p (i t c) -> p i t c", i=NG, t=T8)
        bias_row = kv_all[0:1, 0:6 * NB].bitcast(F32).rearrange("p (k n) -> p k n", k=3)
        bias_part = kv_all[0:1, 6 * NB:9 * NB].bitcast(BF16).rearrange("p (k n) -> p k n", k=3)
        m_dram = nc.dram_tensor("m_dram", [3, R, S], BF16, kind="Internal").ap()
        q_dram = nc.dram_tensor("q_dram", [S, HD * 2 * H], F16, kind="Internal").ap()
        kv_dram = nc.dram_tensor("kv_dram", [S, H * 4 * H], F16, kind="Internal").ap()
        o_dram = nc.dram_tensor("o_dram", [S, D], F32, kind="Internal").ap()
        w0, w1, w2, bank_m, bank_s, bank_o, bank_x0, bank_x1 = (
            psum(n) for n in ("w0", "w1", "w2", "bank_m", "bank_s", "bank_o", "bank_x0", "bank_x1"))

        gwload, grp_zeroed, zeroed_dve = sem("gwload"), sem("grp_zeroed"), sem("zeroed_dve")
        wload = sem("wload")
        eload = sem("eload")
        bload = sem("bload")
        xin = [sem(f"xin{i}") for i in range(2)]
        cin = [sem(f"cin{i}") for i in range(2)]
        gload = sem("gload")
        mstore = sem("mstore")
        mload = sem("mload")
        xload = sem("xload")
        qkv_stored, grp_loaded = sem("qkv_stored"), sem("grp_loaded")
        o_stored, o_loaded = sem("o_stored"), sem("o_loaded")
        stored = sem("stored")
        alone = {e: sem(f"alone_{e.name}") for e in (mybir.EngineType.SP, mybir.EngineType.Pool, mybir.EngineType.DVE)}
        const_chain, consts = sem("const_chain"), sem("consts")
        zeroed = sem("zeroed")
        gw_sum, gw_turned, gw_ready = sem("gw_sum"), sem("gw_turned"), sem("gw_ready")
        prep_chain, bias_ready = sem("prep_chain"), sem("bias_ready")
        tanh_ready, scale_ready = sem("tanh_ready"), sem("scale_ready")
        w_hi_ready, w_lo_ready = sem("w_hi_ready"), sem("w_lo_ready")
        e_hi_ready, e_lo_ready = sem("e_hi_ready"), sem("e_lo_ready")

        def pair(name):
            return [sem(f"{name}{i}") for i in range(2)]

        p_bs, p_stat, p_var, p_rstd, p_xn = pair("p_bs"), pair("p_stat"), pair("p_var"), pair("p_rstd"), pair("p_xn")
        p_qT, p_cT, p_qe, p_ce, p_g, p_ge = pair("p_qT"), pair("p_cT"), pair("p_qe"), pair("p_ce"), pair("p_g"), pair("p_ge")
        row_dve, row_act, rows_turned, rows_ready = sem("row_dve"), sem("row_act"), sem("rows_turned"), sem("rows_ready")
        m_split = sem("m_split")
        a_ready = sem("a_ready")
        mb_ready, d_ready, s_ready, c_ready = sem("mb_ready"), sem("d_ready"), sem("s_ready"), sem("c_ready")
        pv_done, o_evict = sem("pv_done"), sem("o_evict")
        en_ready, hm_read = sem("en_ready"), sem("hm_read")
        f_chain, g_chain = sem("f_chain"), sem("g_chain")
        stat1, rs_a, stat2, rs_b = sem("stat1"), sem("rs_a"), sem("stat2"), sem("rs_b")
        y_ready, hn_ready = sem("y_ready"), sem("hn_ready")
        hT, hT_hi, hT_lo = sem("hT"), sem("hT_hi"), sem("hT_lo")
        dn, dn_hi, dn_lo = sem("dn"), sem("dn_hi"), sem("dn_lo")
        q_done, q_hi, q_lo = sem("q_done"), sem("q_hi"), sem("q_lo")
        kv_done, kv_hi, kv_lo = sem("kv_done"), sem("kv_hi"), sem("kv_lo")
        sc_done, sc_copied, scT, max_ready = sem("sc_done"), sem("sc_copied"), sem("scT"), sem("max_ready")
        shifted, e_ready, e_hi, e_lo = sem("shifted"), sem("e_ready"), sem("e_hi"), sem("e_lo")
        sums, values, r_ready, o_ready = sem("sums"), sem("values"), sem("r_ready"), sem("o_ready")
        oT, oT_hi, oT_lo = sem("oT"), sem("oT_hi"), sem("oT_lo")
        wo_done, x2_ready, stat3, rs_c, h2_ready = sem("wo_done"), sem("x2_ready"), sem("stat3"), sem("rs_c"), sem("h2_ready")
        h2T, h2T_hi, h2T_lo = sem("h2T"), sem("h2T_hi"), sem("h2T_lo")
        lg_done, lg_ready, eg_ready, gate_ready = sem("lg_done"), sem("lg_ready"), sem("eg_ready"), sem("gate_ready")
        base_ready = sem("base_ready")
        mix_done, mix_acc, acc_ready = sem("mix_done"), sem("mix_acc"), sem("acc_ready")

        def steps(eng, run):
            run(0, True, False, False)
            run(1, True, True, False)
            run(2, True, True, True)
            with eng.Fori(3, B) as s:
                run(s, True, True, True)
            run(B, False, True, True)
            run(B + 1, False, False, True)

        def apart(eng):
            eng.sem_inc(alone[eng.engine], 1)

        def first_steps(eng, run):
            run(0)
            with eng.Fori(1, B // 2) as i:
                run(i)

        def f32(ap):
            return ap.bitcast(F32)

        def tok(dram):
            return dram.rearrange("(j p) d -> p j d", p=P)

        k_hi, k_lo, v_hi, v_lo = (
            [kv_all[:, i * T8 * 4 * H + k:(i + 1) * T8 * 4 * H:4] for i in range(NG)] for k in range(4))
        kv_src = kv_dram.rearrange("(i t) (r c) -> t r i c", t=T8, r=H)
        q_src = q_dram.rearrange("(i t) (r c) -> (t r) i c", t=T8, r=HD)
        o_dst = o_dram.rearrange("(i t) (r c) -> (t r) i c", t=T8, r=HD)
        NKV = T8 + 1
        W_LOADS = 16 * (13 + NC * P // H)
        F_CHAIN = 13
        bank_x = [bank_x0, bank_x1]
        turned = [(w0, w1, w2), (bank_m, bank_s, bank_o)]

        def kv_part(j, part):
            return kv_nat[:, j, :, :].rearrange("p r (n l) -> p (r n) l", l=2)[:, :, part]


        block = es.enter_context(nc.Block())

        @block.sync
        def _(sp):
            def first_pass(i):
                for p in range(2):
                    one = bass.ds(2 * i + p, 1)
                    wait(sp, p_xn[p], i)
                    sp.dma_start(xb[p][:, :, :], tok(x[one].rearrange("a s d -> (a s) d")))\
                      .then_inc(xin[p], 16)
                    wait(sp, p_cT[p], i)
                    sp.dma_start(cb[p][:, :, :], tok(ctx_in[one].rearrange("a s d -> (a s) d")))\
                      .then_inc(cin[p], 16)

            first_steps(sp, first_pass)
            sp.wait_ge(zeroed_dve, 1)
            for dst, src in (
                    (wq_raw[:, :, :], Wq.rearrange("(c p) n -> p c n", p=P)),
                    (wd_raw[:, :, :], Wdown.rearrange("(c p) n -> p c n", p=P)),
                    (wu_raw[0:L, :], Wup), (wu_raw[L:2 * L, :], Wup),
                    (wg_raw[:, :, 0:E], Wg.rearrange("(c p) n -> p c n", p=P)),
                    (bd_col[0:L, :], bdown.rearrange("(p a) -> p a", a=1)),
                    (bd_col[L:2 * L, :], bdown.rearrange("(p a) -> p a", a=1)),
                    (g1_col[:, :], gamma1.rearrange("(c p) -> p c", p=P)),
                    (g2_col[:, :], gamma2.rearrange("(c p) -> p c", p=P)),
                    (bias_row[:, 0, 0:D], bq.rearrange("(a n) -> a n", a=1)),
                    (bias_row[:, 0, D:3 * D], bup.rearrange("(a n) -> a n", a=1)),
                    (bias_row[:, 0, 3 * D:4 * D], bo.rearrange("(a n) -> a n", a=1)),
                    (bias_row[:, 0, 4 * D:4 * D + E], bg.rearrange("(a n) -> a n", a=1))):
                sp.dma_start(dst, src).then_inc(wload, 16)
            rows = P // H
            for c in range(NC):
                for r in range(rows):
                    sp.dma_start(wo_raw[r * H:(r + 1) * H, c, :],
                                 Wo.rearrange("(h d) n -> d h n", d=HD)[c * rows + r]).then_inc(wload, 16)
            for p in range(2):
                sp.wait_ge(p_ge[p], B // 2)
            sp.dma_start(ig[:, :], gates[0:NH, :, :]).then_inc(gload, 16)
            sp.dma_start(fg[:, :], gates[32:GP, :, :]).then_inc(gload, 16)
            sp.wait_ge(bias_ready, 1)
            sp.dma_start(bias3[:, :], bias_part[:, :, :]).then_inc(bload, 16)
            sp.wait_ge(m_split, 1)
            sp.dma_start(m_dram.rearrange("k r s -> r k s"), m_part[:, :, :]).then_inc(mstore, 16)
            sp.wait_ge(mstore, 16)

            def load_m(b):
                wait(sp, pv_done, NH * b)
                cols = bass.ds(b * S, S)
                sp.dma_start(qt[:, :, :], qt_all[:, :, cols]).then_inc(mload, 16)
                sp.dma_start(ct[:, :, :], ct_all[:, :, cols]).then_inc(mload, 16)
                sp.dma_start(m_rows[:, :],
                             m_dram.rearrange("k (h b) s -> b (k h) s", b=B)[bass.ds(b, 1)]
                             .rearrange("a r s -> (a r) s")).then_inc(mload, 16)
                for j in range(NJ):
                    sp.dma_start(vals[:, j, :, 0:DH],
                                 ctx_in[bass.ds(b, 1), j * P:(j + 1) * P, :]
                                 .rearrange("a p (h e) -> (a p) h e", e=DH)).then_inc(mload, 16)

            def run(s, m, f_on, x_on, more):
                f, e = s - 1, s - 2
                if f_on:
                    if isinstance(s, int) and s == 1:
                        sp.wait_ge(grp_zeroed, 1)
                    sp.wait_ge(q_lo, f + 1)
                    wait(sp, grp_loaded, 16 * NKV * f)
                    sp.dma_start(tok(q_dram), q_nat[:, :, :, :].rearrange("p j r c -> p j (r c)"))\
                      .then_inc(qkv_stored, 16)
                    sp.wait_ge(kv_lo, NJ * (f + 1))
                    sp.dma_start(tok(kv_dram), kv_nat[:, :, :, :].rearrange("p j r c -> p j (r c)"))\
                      .then_inc(qkv_stored, 16)
                    sp.wait_ge(qkv_stored, 32 * (f + 1))
                    wait(sp, values, f)
                    for t in range(T8):
                        sp.dma_start(kv_grp[t * H:(t + 1) * H, :, t, :], kv_src[t]).then_inc(grp_loaded, 16)
                    sp.dma_start(q_grp[:, :, :], q_src).then_inc(grp_loaded, 16)
                    sp.wait_ge(o_ready, f + 1)
                    apart(sp)
                    wait(sp, o_loaded, 16 * f)
                    sp.dma_start(o_dst, o_grp[:, :].rearrange("p (i c) -> p i c", c=H)).then_inc(o_stored, 16)
                    sp.wait_ge(o_stored, 16 * (f + 1))
                    wait(sp, oT, f)
                    sp.dma_start(o_nat[:, :, :], tok(o_dram)).then_inc(o_loaded, 16)
                if x_on:
                    sp.wait_ge(acc_ready, e + 1)
                    sp.dma_start(tok(out[bass.ds(e, 1)].rearrange("a s d -> (a s) d")), acc[:, :, :])\
                      .then_inc(stored, 16)
                if m:
                    wait(sp, stat2, s)
                    sp.dma_start(xf[:, :, :], tok(x[bass.ds(s, 1)].rearrange("a s d -> (a s) d")))\
                      .then_inc(xload, 16)
                if more:
                    load_m(s + 1)

            load_m(0)
            run(0, True, False, False, True)
            run(1, True, True, False, True)
            run(2, True, True, True, True)
            with sp.Fori(3, B - 1) as s:
                run(s, True, True, True, True)
            run(B - 1, True, True, True, False)
            run(B, False, True, True, False)
            run(B + 1, False, False, True, False)
            sp.wait_ge(stored, 16 * B)

        @block.gpsimd
        def _(pool):
            n = 0

            def made(ins):
                nonlocal n
                ins.then_inc(const_chain, 1)
                n += 1

            for buf, v in ((gw_raw, 0.0), (gb_col, 0.0)):
                pool.memset(buf[:, :], v).then_inc(zeroed, 1) if buf is gb_col else made(pool.memset(buf[:, :], v))
            for buf, v in ((ident, 0.0), (neg_ident, 0.0), (ident_bf, 0.0), (mask_bf, 0.0),
                           (block_ones, 1.0), (ones3, 1.0), (minus_half, -0.5), (zeros, 0.0)):
                made(pool.memset(buf[:, :], v))
            made(pool.memset(head_sel[:, :, :], 0.0))
            pool.wait_ge(const_chain, n)
            for m, fill in ((ident, 1.0), (neg_ident, -1.0), (ident_bf, 1.0)):
                made(pool.affine_select(out=m[:, :], in_=m[:, :], compare_op=ALU.not_equal, fill=fill,
                                        base=0, pattern=[[-1, P]], channel_multiplier=1))
            made(pool.affine_select(out=mask_bf[:, :], in_=mask_bf[:, :], compare_op=ALU.is_ge, fill=MASK,
                                    base=0, pattern=[[1, P]], channel_multiplier=-1))
            for k in range(3):
                pool.wait_ge(const_chain, n)
                made(pool.affine_select(out=head_sel[:, :, :], in_=head_sel[:, :, :],
                                        compare_op=ALU.not_equal, fill=1.0, base=-NH * k,
                                        pattern=[[-1, NH], [0, P]], channel_multiplier=1))
            bo_v = block_ones[:, :].rearrange("p (u c) -> p u c", c=HD)
            made(pool.affine_select(out=bo_v, in_=bo_v, compare_op=ALU.is_ge, fill=0.0, base=0,
                                    pattern=[[-HD, T8], [0, HD]], channel_multiplier=1))
            pool.wait_ge(const_chain, n)
            made(pool.affine_select(out=bo_v, in_=bo_v, compare_op=ALU.is_ge, fill=0.0, base=HD - 1,
                                    pattern=[[HD, T8], [0, HD]], channel_multiplier=-1))
            pool.wait_ge(const_chain, n)
            pool.memset(vals[:, :, :, :], 1.0).then_inc(consts, 1)

            def first_pass(i):
                for p in range(2):
                    pool.wait_ge(p_stat[p], i + 1)
                    wait(pool, p_xn[p], i)
                    apart(pool)
                    pool.tensor_scalar(rstd[p][:, :], mv[p][:, :, 1], LN_EPS, None, ALU.add).then_inc(p_var[p], 1)
                    pool.wait_ge(p_var[p], i + 1)
                    pool.tensor_tensor(rstd[p][:, :], rstd[p][:, :], minus_half[:, 0:NJ], ALU.pow)\
                        .then_inc(p_rstd[p], 1)

            first_steps(pool, first_pass)

            def run(s, m, f_on, x_on):
                f = s - 1
                ch = Chain(pool, g_chain, 6 * f, 6)
                for slot in SLOTS:
                    if slot == "F_norm" and f_on:
                        wait(pool, hm_read, f)
                        apart(pool)
                        pool.tensor_copy(en_b[:, :, :], en_t[:, :, bass.ds(f, NH, B)]).then_inc(en_ready, 1)
                        pool.wait_ge(stat1, f + 1)
                        apart(pool)
                        ch.step(pool.tensor_scalar(fpw[:, 0, :], fmv[:, :, 1], LN_EPS, None, ALU.add))
                        pool.tensor_tensor(frs[:, 0, :], fpw[:, 0, :], minus_half[:, 0:NJ], ALU.pow)\
                            .then_inc(rs_a, 1)
                        pool.wait_ge(rs_a, f + 1)
                        pool.wait_ge(stat2, f + 1)
                        apart(pool)
                        ch.step(pool.tensor_scalar(fpw[:, 0, :], fmv[:, :, 1], LN_EPS, None, ALU.add))
                        apart(pool)
                        ch.step(pool.tensor_scalar(fpw[:, 1, :], fmv[:, :, 1], 1.0 + RMS_EPS, LN_EPS * RMS_EPS,
                                                   ALU.mult, ALU.add))
                        pool.tensor_tensor(frs[:, :, :], fpw[:, :, :],
                                           minus_half[:, :].rearrange("p (a b) -> p a b", a=2), ALU.pow)\
                            .then_inc(rs_b, 1)
                        pool.wait_ge(rs_b, f + 1)
                        wait(pool, x2_ready, f)
                        for j in range(NJ):
                            apart(pool)
                            pool.tensor_scalar(y[:, j, :], x1[:, j, :], fmv[:, j, 0:1], frs[:, 0, j:j + 1],
                                               ALU.subtract, ALU.mult).then_inc(y_ready, 1)
                    if slot == "M0" and m:
                        wait(pool, d_ready, NH * s)
                        apart(pool)
                        pool.tensor_copy(a_b[:, :, :], a_t[:, :, bass.ds(s, NH, B)]).then_inc(a_ready, 1)
                        if isinstance(s, int) and s == 0:
                            pool.wait_ge(e_hi_ready, 1)
                            for c in range(NC):
                                ins = pool.tensor_tensor(we_lo[:, c, :],
                                                         we_raw[:, c, :, :].rearrange("p e n -> p (e n)"),
                                                         f32(we_hi[:, c, :]), ALU.subtract)
                            ins.then_inc(e_lo_ready, 1)
                            pool.wait_ge(bload, 16)
                            pool.memset(kv_all[:, :].bitcast(mybir.dt.uint32), 0).then_inc(grp_zeroed, 1)
                    if slot == "F_split" and f_on:
                        pool.wait_ge(e_hi, f + 1)
                        pool.tensor_tensor(prob_lo[:, :], prob[:, :], prob_hi[:, :], ALU.subtract)\
                            .then_inc(e_lo, 1)
                    if slot == "F_wo" and f_on:
                        pool.wait_ge(stat3, f + 1)
                        pool.wait_ge(y_ready, NJ * (f + 1))
                        ch.step(pool.tensor_tensor(fpw[:, 0, :], fmv[:, :, 0], fmv[:, :, 0], ALU.mult))
                        ch.step(pool.tensor_tensor(fpw[:, 0, :], fpw[:, 0, :], fmv[:, :, 1], ALU.add))
                        apart(pool)
                        ch.step(pool.tensor_scalar(fpw[:, 0, :], fpw[:, 0, :], RMS_EPS, None, ALU.add))
                        pool.tensor_tensor(frs[:, 0, :], fpw[:, 0, :], minus_half[:, 0:NJ], ALU.pow)\
                            .then_inc(rs_c, 1)
                        pool.wait_ge(rs_c, f + 1)
                        wait(pool, h2T, f)
                        for j in range(NJ):
                            apart(pool)
                            pool.tensor_scalar(h2[:, j, :], x2[:, j, :], frs[:, 0, j:j + 1], None, ALU.mult)\
                                .then_inc(h2_ready, 1)

            pool.wait_ge(rows_ready, 2)
            steps(pool, run)

        @block.scalar
        def _(act):
            act.wait_ge(zeroed, 1)
            for dst, src in ((gw_raw[0:NH, :], igate_w), (gw_raw[32:GP, :], fgate_w),
                             (gb_col[0:NH, :], igate_b.rearrange("(p a) -> p a", a=1)),
                             (gb_col[32:GP, :], fgate_b.rearrange("(p a) -> p a", a=1)),
                             (gx_col[:, :], g_xattn.rearrange("(a n) -> a n", a=1).to_broadcast([P, 1])),
                             (gf_col[:, :], g_ffn.rearrange("(a n) -> a n", a=1).to_broadcast([P, 1])),
                             (ls_row[:, :], ln_scale.rearrange("(a n) -> a n", a=1).to_broadcast([P, D]))):
                act.dma_start(dst, src).then_inc(gwload, 16)
            act.wait_ge(gwload, 16 * 7)
            act.activation(tx_col[:, :], gx_col[:, :], ACT.Tanh).then_inc(tanh_ready, 1)
            act.activation(tf_col[:, :], gf_col[:, :], ACT.Tanh).then_inc(tanh_ready, 1)
            act.wait_ge(gw_turned, 1)
            act.activation(gw_t[:, :, :].rearrange("p k g -> p (k g)"), bank_x0[:, 0:2 * NC * GP], ACT.Copy)\
               .then_inc(gw_ready, 1)

            def first_pass(i):
                for p in range(2):
                    cols = bass.ds((2 * i + p) * S, S)
                    act.wait_ge(p_qT[p], i + 1)
                    act.activation(qt_all[:, :, cols],
                                   turned[p][0][:, :].rearrange("p (c s) -> p c s", c=NC), ACT.Copy)\
                       .then_inc(p_qe[p], 1)
                    act.wait_ge(p_g[p], i + 1)
                    act.activation(gates[:, bass.ds(2 * i + p, 1), :].rearrange("p a s -> p (a s)"),
                                   turned[p][2][0:GP, 0:S], ACT.Identity, bias=gb_col[:, 0:1])\
                       .then_inc(p_ge[p], 1)

            first_steps(act, first_pass)
            act.wait_ge(gload, 32)
            for c in range(NC):
                act.dma_start(we_raw[:, c, :, :], We.rearrange("e (c p) n -> c p e n", p=P)[c])\
                   .then_inc(eload, 16)

            act.wait_ge(row_dve, 1)
            act.activation(row_b[:, :], row_a[:, :], ACT.Exp, scale=-1.0).then_inc(row_act, 1)
            act.wait_ge(row_act, 1)
            act.activation(row_c[:, :], row_b[:, :], ACT.Ln, bias=1.0).then_inc(row_act, 1)
            act.wait_ge(row_dve, 6)
            act.activation(en_row[:, :], row_a[:, :], ACT.Exp, scale=-1.0).then_inc(row_act, 1)
            act.wait_ge(rows_turned, 1)
            act.activation(a_t[:, :, :].rearrange("p j r -> p (j r)"), w0[:, 0:NJ * R], ACT.Copy)\
               .then_inc(rows_ready, 1)
            act.activation(en_t[:, :, :].rearrange("p j r -> p (j r)"), w0[:, NJ * R:2 * NJ * R], ACT.Copy,
                           bias=CELL_EPS)\
               .then_inc(rows_ready, 1)

            def split_weights():
                act.wait_ge(wload, W_LOADS)
                act.activation(wq_hi[:, :, :].rearrange("p c (d h) -> p c d h", h=H),
                               wq_raw[:, :, :].rearrange("p c (h d) -> p c d h", d=HD), ACT.Copy)
                act.activation(wo_hi[:, :, :], wo_raw[:, :, :], ACT.Copy)
                for k in range(2):
                    act.activation(wd_hi[:, :, k, :], wd_raw[:, :, :], ACT.Copy)
                act.activation(wg_hi[:, :, :], wg_raw[:, :, :], ACT.Copy)
                for k, order in enumerate(("p (h a d) -> p a d h", "p (h a d) -> p a h d")):
                    ins = act.activation(wu_hi[:, :].rearrange("p (r c a) -> p a r c", a=2, c=H)[:, k],
                                         wu_raw[:, :].rearrange(order, a=2, d=HD)[:, k], ACT.Copy)
                ins.then_inc(w_hi_ready, 1)
                act.wait_ge(eload, 16 * NC)
                for c in range(NC):
                    ins = act.activation(we_hi[:, c, :], we_raw[:, c, :, :].rearrange("p e n -> p (e n)"), ACT.Copy)
                ins.then_inc(e_hi_ready, 1)

            def run(s, m, f_on, x_on):
                f = s - 1
                for slot in SLOTS:
                    if slot == "F_turn" and f_on:
                        act.wait_ge(hT, f + 1)
                        wait(act, q_done, f)
                        for c in range(NC):
                            ins = act.activation(ht_hi[:, c, :], w0[:, c * S:(c + 1) * S], ACT.Identity,
                                                 scale=g1_col[:, c:c + 1])
                        ins.then_inc(hT_hi, 1)
                    if slot == "F_down" and f_on:
                        act.wait_ge(dn, f + 1)
                        wait(act, kv_done, NJ * f)
                        act.activation(dt[:, :], w1[:, 0:S], ACT.Identity, bias=bd_col[:, 0:1])\
                           .then_inc(dn_hi, 1)
                    if slot == "F_qkv" and f_on:
                        act.wait_ge(q_done, f + 1)
                        wait(act, qkv_stored, 32 * f)
                        act.activation(q_nat[:, :, :, 0:H].rearrange("p j d c -> p (j d) c"),
                                       w2[:, :].rearrange("p (r c) -> p r c", c=H), ACT.Copy)\
                           .then_inc(q_hi, 1)
                        for j in range(NJ):
                            act.wait_ge(kv_done, NJ * f + j + 1)
                            act.activation(kv_part(j, 0), (w0, w1)[j][:, :], ACT.Copy).then_inc(kv_hi, 1)
                    if slot[0] == "M" and m:
                        h = int(slot[1:])
                        if h in (NH // 2 + 1, NH):
                            k = 0 if h < NH else 1
                            act.wait_ge(pv_done, NH * s + (k + 1) * NH // 2)
                            wait(act, hm_read, s)
                            act.activation(hm[:, :, k * NH // 2:(k + 1) * NH // 2, :],
                                           bank_o[:, 0:NJ * NH // 2 * VW]
                                           .rearrange("p (j h e) -> p j h e", j=NJ, h=NH // 2), ACT.Copy)\
                               .then_inc(o_evict, 1)
                        if h < NH:
                            act.wait_ge(mb_ready, NH * s + h + 1)
                            wait(act, c_ready, NH * s + h - 1)
                            if h == 0:
                                act.wait_ge(a_ready, s + 1)
                            act.activation(decay[:, h % 2, 0:S], bank_m[:, 0:S], ACT.Exp,
                                           bias=a_b[:, 0, h:h + 1], scale=-1.0)
                            act.activation(decay[:, h % 2, S:TRI], bank_m[:, S:TRI], ACT.Exp,
                                           bias=a_b[:, 1, h:h + 1], scale=-1.0).then_inc(d_ready, 1)
                        if h == 2 and isinstance(s, int) and s == 0:
                            split_weights()
                    if slot == "F_scores" and f_on:
                        act.wait_ge(sc_done, f + 1)
                        wait(act, scT, f)
                        act.activation(sc_sb[:, :], w2[:, :], ACT.Copy).then_inc(sc_copied, 1)
                    if slot == "F_shift" and f_on:
                        act.wait_ge(shifted, f + 1)
                        wait(act, e_lo, f)
                        act.activation(prob[:, :], w2[:, :], ACT.Exp, scale=HSCALE).then_inc(e_ready, 1)
                    if slot == "F_turn_o" and f_on:
                        act.wait_ge(oT, f + 1)
                        wait(act, wo_done, f)
                        act.activation(ot_hi[:, :, :].rearrange("p c s -> p (c s)"), w2[:, :], ACT.Copy)\
                           .then_inc(oT_hi, 1)
                    if slot == "F_turn_h2" and f_on:
                        act.wait_ge(h2T, f + 1)
                        wait(act, mix_done, NX * f)
                        wait(act, lg_done, f)
                        for c in range(NC):
                            ins = act.activation(h2_hi[:, c, :], w0[:, c * S:(c + 1) * S], ACT.Identity,
                                                 scale=g2_col[:, c:c + 1])
                        ins.then_inc(h2T_hi, 1)
                    if slot == "F_gate" and f_on:
                        act.wait_ge(lg_ready, f + 1)
                        act.activation(lg[:, :, :], lg[:, :, :], ACT.Exp).then_inc(eg_ready, 1)

            steps(act, run)

        @block.vector
        def _(dve):
            for buf in (wg_raw, bias_row):
                ins = dve.memset(buf[:, :, :], 0.0)
            ins.then_inc(zeroed_dve, 1)
            dve.wait_ge(gwload, 16 * 7)
            dve.tensor_tensor(gw_kv[:, :], gw_raw[:, D:2 * D], gw_raw[:, 2 * D:3 * D], ALU.add).then_inc(gw_sum, 1)
            dve.wait_ge(tanh_ready, 2)
            dve.tensor_scalar(lst_row[:, :], ls_row[:, :], tx_col[:, 0:1], None, ALU.mult).then_inc(scale_ready, 1)
            dve.wait_ge(scale_ready, 1)
            def first_pass(i):
                for p in range(2):
                    dve.wait_ge(xin[p], 16 * (i + 1))
                    for j in range(NJ):
                        ins = dve.bn_stats(bs[p][:, j, :], xb[p][:, j, :])
                    ins.then_inc(p_bs[p], 1)
                    dve.wait_ge(p_bs[p], i + 1)
                    apart(dve)
                    for j in range(NJ):
                        ins = dve.bn_aggr(mv[p][:, j, :], bs[p][:, j, :])
                    ins.then_inc(p_stat[p], 1)
                    dve.wait_ge(p_rstd[p], i + 1)
                    wait(dve, p_qT[p], i)
                    for j in range(NJ):
                        ins = dve.tensor_scalar(xn[p][:, j, :], xb[p][:, j, :], mv[p][:, j, 0:1],
                                                rstd[p][:, j:j + 1], ALU.subtract, ALU.mult)
                    ins.then_inc(p_xn[p], 1)
                    dve.wait_ge(p_cT[p], i + 1)
                    dve.tensor_copy(ct_all[:, :, bass.ds((2 * i + p) * S, S)],
                                    turned[p][1][:, :].rearrange("p (c s) -> p c s", c=NC)).then_inc(p_ce[p], 1)

            first_steps(dve, first_pass)

            rows = Chain(dve, row_dve, 0, 6)
            dve.wait_ge(gload, 32)
            rows.step(dve.scalar_tensor_tensor(out=row_a[:, :], in0=fg[:, :], scalar=-1.0, in1=fg[:, :],
                                               op0=ALU.mult, op1=ALU.max))
            dve.wait_ge(row_act, 2)
            rows.step(dve.scalar_tensor_tensor(out=row_a[:, :], in0=fg[:, :], scalar=0.0, in1=row_c[:, :],
                                               op0=ALU.min, op1=ALU.subtract))
            rows.step(dve.tensor_tensor_scan(row_b[:, :], row_a[:, :], zeros[:, :], 0.0, ALU.add, ALU.add))
            rows.step(dve.tensor_tensor(row_c[:, :], ig[:, :], row_b[:, :], ALU.subtract))
            rows.step(dve.tensor_tensor_scan(row_m[:, :], row_c[:, :], row_c[:, :], -3.0e38, ALU.max, ALU.max))
            rows.step(dve.tensor_tensor(row_a[:, :], row_b[:, :], row_m[:, :], ALU.add))
            parts = Chain(dve, prep_chain, 0, 9)
            parts.step(dve.tensor_copy(m_part[:, 0, :], row_m[:, :]))
            parts.step(dve.tensor_tensor(row_b[:, :], row_m[:, :], m_part[:, 0, :], ALU.subtract))
            parts.step(dve.tensor_copy(m_part[:, 1, :], row_b[:, :]))
            parts.step(dve.tensor_tensor(fg[:, :], row_b[:, :], m_part[:, 1, :], ALU.subtract))
            dve.tensor_copy(m_part[:, 2, :], fg[:, :]).then_inc(m_split, 1)

            dve.wait_ge(wload, W_LOADS)
            for k, order in enumerate(("p (h a d) -> p a d h", "p (h a d) -> p a h d")):
                dve.tensor_copy(bias_row[:, 1, D:3 * D].rearrange("p (r c a) -> p a r c", a=2, c=H)[:, k],
                                bias_row[:, 0, D:3 * D].rearrange(order, a=2, d=HD)[:, k])
            dve.tensor_copy(bias_row[:, 1, 3 * D:NB], bias_row[:, 0, 3 * D:NB])
            parts.step(dve.tensor_copy(bias_row[:, 1, 0:D].rearrange("p (d h) -> p d h", h=H),
                                       bias_row[:, 0, 0:D].rearrange("p (h d) -> p d h", d=HD)))
            parts.step(dve.tensor_copy(bias_part[:, 0, :], bias_row[:, 1, :]))
            parts.step(dve.tensor_tensor(bias_row[:, 2, :], bias_row[:, 1, :], bias_part[:, 0, :], ALU.subtract))
            parts.step(dve.tensor_copy(bias_part[:, 1, :], bias_row[:, 2, :]))
            parts.step(dve.tensor_tensor(bias_row[:, 0, :], bias_row[:, 2, :], bias_part[:, 1, :], ALU.subtract))
            dve.tensor_copy(bias_part[:, 2, :], bias_row[:, 0, :]).then_inc(bias_ready, 1)

            def split_weights():
                dve.wait_ge(w_hi_ready, 1)
                for c in range(NC):
                    dve.tensor_tensor(wq_lo[:, c, :].rearrange("p (d h) -> p d h", h=H),
                                      wq_raw[:, c, :].rearrange("p (h d) -> p d h", d=HD),
                                      f32(wq_hi[:, c, :]).rearrange("p (d h) -> p d h", h=H), ALU.subtract)
                dve.tensor_tensor(wo_lo[:, :, :], wo_raw[:, :, :], f32(wo_hi[:, :, :]), ALU.subtract)
                for k in range(2):
                    dve.tensor_tensor(wd_lo[:, :, k, :], wd_raw[:, :, :], f32(wd_hi[:, :, k, :]), ALU.subtract)
                dve.tensor_tensor(wg_lo[:, :, :], wg_raw[:, :, :], f32(wg_hi[:, :, :]), ALU.subtract)
                for k, order in enumerate(("p (h a d) -> p a d h", "p (h a d) -> p a h d")):
                    ins = dve.tensor_tensor(
                        wu_lo[:, :].rearrange("p (r c a) -> p a r c", a=2, c=H)[:, k],
                        wu_raw[0:L, :].rearrange(order, a=2, d=HD)[:, k],
                        f32(wu_hi[0:L, :]).rearrange("p (r c a) -> p a r c", a=2, c=H)[:, k], ALU.subtract)
                ins.then_inc(w_lo_ready, 1)

            def run(s, m, f_on, x_on):
                f, e = s - 1, s - 2
                ch = Chain(dve, f_chain, F_CHAIN * f, F_CHAIN)
                for slot in SLOTS:
                    if slot == "F_norm" and f_on:
                        if isinstance(s, int) and s == 1:
                            dve.wait_ge(e_lo_ready, 1)
                        dve.wait_ge(o_evict, 2 * (f + 1))
                        dve.wait_ge(en_ready, f + 1)
                        ch.step(dve.scalar_tensor_tensor(out=nrm[:, :, :], in0=hm[:, :, :, DH], scalar=-1.0,
                                                         in1=hm[:, :, :, DH], op0=ALU.mult, op1=ALU.max))
                        ch.step(dve.scalar_tensor_tensor(out=nrm[:, :, :], in0=nrm[:, :, :], scalar=CELL_EPS,
                                                         in1=en_b[:, :, :], op0=ALU.add, op1=ALU.max))
                        ch.step(dve.reciprocal(nrm[:, :, :], nrm[:, :, :]))
                        dve.tensor_tensor(hcell[:, :, :].rearrange("p j (h e) -> p (j h) e", e=DH),
                                          hm[:, :, :, 0:DH].rearrange("p j h e -> p (j h) e"),
                                          nrm[:, :, :].rearrange("p j h -> p (j h)").unsqueeze(2)
                                          .to_broadcast([P, NJ * NH, DH]), ALU.mult).then_inc(hm_read, 1)
                        dve.wait_ge(hm_read, f + 1)
                        stats(ch, hcell, stat1, f)
                        for j in range(NJ):
                            ins = dve.scalar_tensor_tensor(out=hcell[:, j, :], in0=hcell[:, j, :],
                                                           scalar=fmv[:, j, 0:1], in1=lst_row[:, :],
                                                           op0=ALU.subtract, op1=ALU.mult)
                        ch.step(ins)
                        dve.wait_ge(rs_a, f + 1)
                        dve.wait_ge(xload, 16 * (f + 1))
                        wait(dve, y_ready, NJ * f)
                        for j in range(NJ):
                            ins = dve.scalar_tensor_tensor(out=x1[:, j, :], in0=hcell[:, j, :],
                                                           scalar=frs[:, 0, j:j + 1], in1=xf[:, j, :],
                                                           op0=ALU.mult, op1=ALU.add)
                        ch.step(ins)
                        stats(ch, x1, stat2, f)
                        dve.wait_ge(rs_b, f + 1)
                        wait(dve, hT, f)
                        for j in range(NJ):
                            ins = dve.tensor_scalar(hn[:, j, :], x1[:, j, :], fmv[:, j, 0:1], frs[:, 1, j:j + 1],
                                                    ALU.subtract, ALU.mult)
                        ins.then_inc(hn_ready, 1)
                    if slot == "F_turn" and f_on:
                        dve.wait_ge(hT_hi, f + 1)
                        wait(dve, q_done, f)
                        for c in range(NC):
                            ins = dve.scalar_tensor_tensor(out=ht_lo[:, c, :], in0=w0[:, c * S:(c + 1) * S],
                                                           scalar=g1_col[:, c:c + 1], in1=f32(ht_hi[:, c, :]),
                                                           op0=ALU.mult, op1=ALU.subtract)
                        ins.then_inc(hT_lo, 1)
                    if slot == "F_down" and f_on:
                        dve.wait_ge(dn_hi, f + 1)
                        dve.scalar_tensor_tensor(out=dt[L:P, :], in0=w1[L:P, 0:S], scalar=bd_col[L:P, 0:1],
                                                 in1=f32(dt[L:P, :]), op0=ALU.add, op1=ALU.subtract)\
                           .then_inc(dn_lo, 1)
                    if slot == "F_qkv" and f_on:
                        dve.wait_ge(q_hi, f + 1)
                        q_v = q_nat[:, :, :, :].rearrange("p j d c -> p (j d) c")
                        dve.tensor_tensor(q_v[:, :, H:2 * H], w2[:, :].rearrange("p (r c) -> p r c", c=H),
                                          q_v[:, :, 0:H], ALU.subtract).then_inc(q_lo, 1)
                        for j in range(NJ):
                            dve.wait_ge(kv_hi, NJ * f + j + 1)
                            dve.tensor_tensor(kv_part(j, 1), (w0, w1)[j][:, :], kv_part(j, 0), ALU.subtract).then_inc(kv_lo, 1)
                    if slot[0] == "M" and m and int(slot[1:]) < NH:
                        h = int(slot[1:])
                        dve.wait_ge(s_ready, NH * s + h + 1)
                        dve.wait_ge(d_ready, NH * s + h + 1)
                        wait(dve, pv_done, NH * s + h - 1)
                        dve.scalar_tensor_tensor(out=cell[:, h % 2, :], in0=bank_s[:, 0:TRI], scalar=QSCALE,
                                                 in1=decay[:, h % 2, :], op0=ALU.mult, op1=ALU.mult)\
                           .then_inc(c_ready, 1)
                        if h == 3 and isinstance(s, int) and s == 0:
                            split_weights()
                    if slot == "F_max" and f_on:
                        dve.wait_ge(scT, f + 1)
                        wait(dve, shifted, f)
                        ch.step(dve.tensor_reduce(smax[:, :], w0[:, :].rearrange("p (r g) -> p r g", g=H),
                                                  AX.X, ALU.max))
                        dve.tensor_copy(smax_x[:, :, :], smax[:, :].unsqueeze(2).to_broadcast([P, 4 * T8, H]))\
                           .then_inc(max_ready, 1)
                    if slot == "F_split" and f_on:
                        dve.wait_ge(e_ready, f + 1)
                        wait(dve, values, f)
                        dve.tensor_copy(prob_hi[:, :], prob[:, :]).then_inc(e_hi, 1)
                    if slot == "F_o" and f_on:
                        dve.wait_ge(sums, f + 1)
                        dve.reciprocal(rsum[:, :], w1[:, :]).then_inc(r_ready, 1)
                        dve.wait_ge(r_ready, f + 1)
                        dve.wait_ge(values, f + 1)
                        wait(dve, o_stored, 16 * f)
                        dve.tensor_tensor(o_grp[:, :], w0[:, :], rsum[:, :], ALU.mult).then_inc(o_ready, 1)
                    if slot == "F_turn_o" and f_on:
                        dve.wait_ge(oT_hi, f + 1)
                        wait(dve, wo_done, f)
                        dve.tensor_tensor(ot_lo[:, :, :].rearrange("p c s -> p (c s)"), w2[:, :],
                                          f32(ot_hi[:, :, :]).rearrange("p c s -> p (c s)"), ALU.subtract)\
                           .then_inc(oT_lo, 1)
                    if slot == "F_wo" and f_on:
                        dve.wait_ge(wo_done, f + 1)
                        dve.wait_ge(y_ready, NJ * (f + 1))
                        wait(dve, h2_ready, NJ * f)
                        dve.tensor_tensor(x2[:, :, :].rearrange("p j d -> p (j d)"), w1[:, :],
                                          y[:, :, :].rearrange("p j d -> p (j d)"), ALU.add).then_inc(x2_ready, 1)
                        dve.wait_ge(x2_ready, f + 1)
                        stats(ch, x2, stat3, f)
                        dve.scalar_tensor_tensor(out=base[:, :, :], in0=x2[:, :, :], scalar=tf_col[:, 0:1],
                                                 in1=x1[:, :, :], op0=ALU.mult, op1=ALU.add)\
                           .then_inc(base_ready, 1)
                        dve.wait_ge(base_ready, f + 1)
                    if slot == "F_turn_h2" and f_on:
                        dve.wait_ge(h2T_hi, f + 1)
                        for c in range(NC):
                            ins = dve.scalar_tensor_tensor(out=h2_lo[:, c, :], in0=w0[:, c * S:(c + 1) * S],
                                                           scalar=g2_col[:, c:c + 1], in1=f32(h2_hi[:, c, :]),
                                                           op0=ALU.mult, op1=ALU.subtract)
                        ins.then_inc(h2T_lo, 1)
                    if slot == "F_gate" and f_on:
                        logits = w1[:, 0:NJ * 32].rearrange("p (j n) -> p j n", j=NJ)[:, :, 0:E]
                        dve.wait_ge(lg_done, f + 1)
                        ch.step(dve.tensor_reduce(gmax[:, :], logits, AX.X, ALU.max))
                        dve.tensor_tensor(lg[:, :, :], logits, gmax[:, :].unsqueeze(2).to_broadcast([P, NJ, E]),
                                          ALU.subtract).then_inc(lg_ready, 1)
                        dve.wait_ge(eg_ready, f + 1)
                        ch.step(dve.tensor_reduce(gmax[:, :], lg[:, :, :], AX.X, ALU.add))
                        ch.step(dve.reciprocal(gmax[:, :], gmax[:, :]))
                        ch.step(dve.tensor_scalar(gmax[:, :], gmax[:, :], tf_col[:, 0:1], None, ALU.mult))
                        dve.tensor_tensor(gate[:, :, :], lg[:, :, :],
                                          gmax[:, :].unsqueeze(2).to_broadcast([P, NJ, E]), ALU.mult)\
                           .then_inc(gate_ready, 1)
                        dve.wait_ge(gate_ready, f + 1)
                        assert ch.n == F_CHAIN, ch.n
                    if slot[0] == "X" and x_on:
                        k = int(slot[1:])
                        j, n = divmod(k, E // EC)
                        dve.wait_ge(mix_done, NX * e + k + 1)
                        if k == 0:
                            wait(dve, stored, 16 * e)
                        for u in range(EC):
                            ex = EC * n + u
                            dve.scalar_tensor_tensor(out=acc[:, j, :], in0=bank_x[k % 2][:, u * D:(u + 1) * D],
                                                     scalar=gate[:, j, ex:ex + 1],
                                                     in1=(base if ex == 0 else acc)[:, j, :],
                                                     op0=ALU.mult, op1=ALU.add).then_inc(mix_acc, 1)
                            dve.wait_ge(mix_acc, NX * EC * e + EC * k + u + 1)
                        if k == NX - 1:
                            dve.tensor_copy(gmax[:, 0:1], gmax[:, 1:2]).then_inc(acc_ready, 1)

            def stats(ch, src, done, f):
                for j in range(NJ):
                    ins = dve.bn_stats(fbs[:, j, :], src[:, j, :])
                ch.step(ins)
                apart(dve)
                for j in range(NJ):
                    ins = dve.bn_aggr(fmv[:, j, :], fbs[:, j, :])
                ins.then_inc(done, 1)
                dve.wait_ge(done, f + 1)

            steps(dve, run)

        @block.tensor
        def _(pe):
            def split_mm(dst, a_hi, a_lo, b_hi, b_lo, start, stop):
                pe.matmul(dst, a_hi, b_hi, start=start, stop=False, skip_group_check=True)
                pe.matmul(dst, a_hi, b_lo, start=False, stop=False, skip_group_check=True)
                return pe.matmul(dst, a_lo, b_hi, start=False, stop=stop, skip_group_check=True)

            def bias_mm(dst, name):
                off, size = BIAS[name]
                return pe.matmul(dst, ones3[:, :], bias3[:, off:off + size], start=False, stop=True,
                                 skip_group_check=True)

            pe.wait_ge(consts, 1)
            pe.wait_ge(gw_sum, 1)
            for k in range(2 * NC):
                src = gw_raw[:, k * P:(k + 1) * P] if k < NC else gw_kv[:, (k - NC) * P:(k - NC + 1) * P]
                ins = pe.transpose(bank_x0[:, k * GP:(k + 1) * GP], src, ident[0:GP, 0:GP])
            ins.then_inc(gw_turned, 1)
            pe.wait_ge(gw_ready, 1)

            def first_pass(i):
                for p in range(2):
                    pe.wait_ge(cin[p], 16 * (i + 1))
                    wait(pe, p_ce[p], i)
                    for c in range(NC):
                        for j in range(NJ):
                            ins = pe.transpose(turned[p][1][:, c * S + j * P:c * S + (j + 1) * P],
                                               cb[p][:, j, c * P:(c + 1) * P], ident[:, :])
                    ins.then_inc(p_cT[p], 1)
                    pe.wait_ge(p_xn[p], i + 1)
                    wait(pe, p_qe[p], i)
                    for c in range(NC):
                        for j in range(NJ):
                            ins = pe.transpose(turned[p][0][:, c * S + j * P:c * S + (j + 1) * P],
                                               xn[p][:, j, c * P:(c + 1) * P], ident[:, :])
                    ins.then_inc(p_qT[p], 1)
                    pe.wait_ge(p_qe[p], i + 1)
                    pe.wait_ge(p_ce[p], i + 1)
                    wait(pe, p_ge[p], i)
                    cols = bass.ds((2 * i + p) * S, S)
                    for k in range(2 * NC):
                        src = (qt_all if k < NC else ct_all)[:, k % NC, cols]
                        ins = pe.matmul(turned[p][2][0:GP, 0:S], gw_t[:, k, :], src,
                                        start=(k == 0), stop=(k == 2 * NC - 1))
                    ins.then_inc(p_g[p], 1)

            first_steps(pe, first_pass)

            pe.wait_ge(row_act, 3)
            pe.wait_ge(p_qe[0], B // 2)
            for k, src in enumerate((row_c, en_row)):
                for j in range(NJ):
                    ins = pe.transpose(w0[:, (k * NJ + j) * R:(k * NJ + j + 1) * R], src[:, j * P:(j + 1) * P],
                                       ident[0:R, 0:R])
            ins.then_inc(rows_turned, 1)

            def run(s, m, f_on, x_on):
                f, e = s - 1, s - 2
                first_f = isinstance(s, int) and s == 1
                for slot in SLOTS:
                    if slot == "F_turn" and f_on:
                        pe.wait_ge(hn_ready, f + 1)
                        wait(pe, h2T_lo, f)
                        for c in range(NC):
                            for j in range(NJ):
                                ins = pe.transpose(w0[:, c * S + j * P:c * S + (j + 1) * P],
                                                   hn[:, j, c * P:(c + 1) * P], ident[:, :])
                        ins.then_inc(hT, 1)
                    if slot == "F_down" and f_on:
                        if first_f:
                            pe.wait_ge(w_lo_ready, 1)
                            pe.wait_ge(bload, 16)
                        pe.wait_ge(hT_lo, f + 1)
                        wait(pe, lg_ready, f)
                        for c in range(NC):
                            ins = split_mm(w1[:, 0:S], wd_hi[:, c, :, :].rearrange("p a l -> p (a l)"),
                                           wd_lo[:, c, :, :].rearrange("p a l -> p (a l)"),
                                           ht_hi[:, c, :], ht_lo[:, c, :], c == 0, c == NC - 1)
                        ins.then_inc(dn, 1)
                    if slot == "F_qkv" and f_on:
                        wait(pe, oT_lo, f)
                        for j in range(NJ):
                            dst = w2[:, j * D:(j + 1) * D]
                            for c in range(NC):
                                split_mm(dst, ht_hi[:, c, j * P:(j + 1) * P], ht_lo[:, c, j * P:(j + 1) * P],
                                         wq_hi[:, c, :], wq_lo[:, c, :], c == 0, False)
                            ins = bias_mm(dst, "q")
                        ins.then_inc(q_done, 1)
                        pe.wait_ge(dn_lo, f + 1)
                        for j in range(NJ):
                            dst = (w0, w1)[j][:, :]
                            tk = slice(j * P, (j + 1) * P)
                            pe.matmul(dst, dt[:, tk], wu_hi[:, :], start=True, stop=False, skip_group_check=True)
                            pe.matmul(dst, dt[0:L, tk], wu_lo[:, :], start=False, stop=False, skip_group_check=True)
                            bias_mm(dst, "up").then_inc(kv_done, 1)
                    if slot[0] == "M" and m:
                        h = int(slot[1:])
                        if h == 0:
                            pe.wait_ge(mload, 16 * 5 * (s + 1))
                        if h < NH:
                            wait(pe, d_ready, NH * s + h)
                            sel = head_sel[:, h, :]
                            pe.matmul(bank_m[:, 0:S], sel, m_rows[:, :], start=True, stop=False, skip_group_check=True)
                            pe.matmul(bank_m[:, S:TRI], sel, m_rows[:, P:S], start=False, stop=False,
                                      skip_group_check=True)
                            pe.matmul(bank_m[:, 0:P], ident_bf[:, :], mask_bf[:, :], start=False, stop=False,
                                      skip_group_check=True)
                            pe.matmul(bank_m[:, S:TRI], ident_bf[:, :], mask_bf[:, :], start=False, stop=True,
                                      skip_group_check=True).then_inc(mb_ready, 1)
                            wait(pe, c_ready, NH * s + h)
                            per = P // DH
                            r = slice((h % per) * DH, (h % per + 1) * DH)
                            pe.matmul(bank_s[:, 0:S], ct[r, h // per, 0:P], qt[r, h // per, :], start=True,
                                      stop=False, skip_group_check=True)
                            pe.matmul(bank_s[:, S:TRI], ct[r, h // per, P:S], qt[r, h // per, P:S], start=False,
                                      stop=True, skip_group_check=True).then_inc(s_ready, 1)
                        if h > 0:
                            g = h - 1
                            pe.wait_ge(c_ready, NH * s + h)
                            if g % (NH // 2) == 0:
                                wait(pe, o_evict, 2 * s + g // (NH // 2))
                            for j in range(NJ):
                                col = (j * NH // 2 + g % (NH // 2)) * VW
                                dst = bank_o[:, col:col + VW]
                                if j == 0:
                                    pe.matmul(dst, cell[:, g % 2, 0:P], vals[:, 0, g, :], start=True, stop=True)
                                else:
                                    pe.matmul(dst, cell[:, g % 2, P:S], vals[:, 0, g, :], start=True, stop=False)
                                    pe.matmul(dst, cell[:, g % 2, S:TRI], vals[:, 1, g, :], start=False, stop=True)\
                                      .then_inc(pv_done, 1)
                    if slot == "F_scores" and f_on:
                        if first_f:
                            pe.wait_ge(grp_zeroed, 1)
                        pe.wait_ge(grp_loaded, 16 * NKV * (f + 1))
                        pe.wait_ge(q_lo, f + 1)
                        for i in range(NG):
                            dst = w2[:, i * H:(i + 1) * H]
                            ins = split_mm(dst, k_hi[i], k_lo[i], q_grp[:, i, 0:H], q_grp[:, i, H:2 * H],
                                           i == 0, i == NG - 1)
                        ins.then_inc(sc_done, 1)
                    if slot == "F_max" and f_on:
                        pe.wait_ge(sc_copied, f + 1)
                        pe.wait_ge(kv_lo, NJ * (f + 1))
                        for a in range(4):
                            ins = pe.transpose(w0[:, a * P:(a + 1) * P], sc_sb[:, a * P:(a + 1) * P], ident[:, :])
                        ins.then_inc(scT, 1)
                    if slot == "F_shift" and f_on:
                        pe.wait_ge(max_ready, f + 1)
                        for a in range(4):
                            ins = pe.matmul(w2[:, a * P:(a + 1) * P],
                                            smax_x[:, a * T8:(a + 1) * T8, :].rearrange("p t g -> p (t g)"), neg_ident[:, :],
                                            start=False, stop=(a == 3), skip_group_check=True)
                        ins.then_inc(shifted, 1)
                    if slot == "F_values" and f_on:
                        pe.wait_ge(e_hi, f + 1)
                        pe.wait_ge(e_lo, f + 1)
                        pe.matmul(w1[:, :], block_ones[:, :], prob_hi[:, :], start=True, stop=False)
                        pe.matmul(w1[:, :], block_ones[:, :], prob_lo[:, :], start=False, stop=True).then_inc(sums, 1)
                        for i in range(NG):
                            c = slice(i * H, (i + 1) * H)
                            ins = split_mm(w0[:, c], v_hi[i], v_lo[i], prob_hi[:, c], prob_lo[:, c],
                                           i == 0, i == NG - 1)
                        ins.then_inc(values, 1)
                    if slot == "F_turn_o" and f_on:
                        pe.wait_ge(o_loaded, 16 * (f + 1))
                        pe.wait_ge(e_ready, f + 1)
                        for c in range(NC):
                            for j in range(NJ):
                                ins = pe.transpose(w2[:, c * S + j * P:c * S + (j + 1) * P],
                                                   o_nat[:, j, c * P:(c + 1) * P], ident[:, :])
                        ins.then_inc(oT, 1)
                    if slot == "F_wo" and f_on:
                        pe.wait_ge(oT_lo, f + 1)
                        pe.wait_ge(r_ready, f + 1)
                        for j in range(NJ):
                            dst = w1[:, j * D:(j + 1) * D]
                            for c in range(NC):
                                split_mm(dst, ot_hi[:, c, j * P:(j + 1) * P], ot_lo[:, c, j * P:(j + 1) * P],
                                         wo_hi[:, c, :], wo_lo[:, c, :], c == 0, False)
                            ins = bias_mm(dst, "o")
                        ins.then_inc(wo_done, 1)
                    if slot == "F_turn_h2" and f_on:
                        pe.wait_ge(h2_ready, NJ * (f + 1))
                        pe.wait_ge(o_ready, f + 1)
                        for c in range(NC):
                            for j in range(NJ):
                                ins = pe.transpose(w0[:, c * S + j * P:c * S + (j + 1) * P],
                                                   h2[:, j, c * P:(c + 1) * P], ident[:, :])
                        ins.then_inc(h2T, 1)
                    if slot == "F_gate" and f_on:
                        pe.wait_ge(h2T_lo, f + 1)
                        pe.wait_ge(x2_ready, f + 1)
                        for j in range(NJ):
                            dst = w1[:, j * 32:(j + 1) * 32]
                            for c in range(NC):
                                split_mm(dst, h2_hi[:, c, j * P:(j + 1) * P], h2_lo[:, c, j * P:(j + 1) * P],
                                         wg_hi[:, c, :], wg_lo[:, c, :], c == 0, False)
                            ins = bias_mm(dst, "g")
                        ins.then_inc(lg_done, 1)
                    if slot[0] == "X" and x_on:
                        k = int(slot[1:])
                        j, n = divmod(k, E // EC)
                        if k < 2:
                            if isinstance(s, int) and s == 2:
                                pe.wait_ge(e_lo_ready, 1)
                            wait(pe, acc_ready, e)
                        else:
                            pe.wait_ge(mix_acc, NX * EC * e + EC * (k - 1))
                        cols = slice(n * 512, (n + 1) * 512)
                        for c in range(NC):
                            ins = split_mm(bank_x[k % 2][:, :], h2_hi[:, c, j * P:(j + 1) * P],
                                           h2_lo[:, c, j * P:(j + 1) * P], we_hi[:, c, cols], we_lo[:, c, cols],
                                           c == 0, c == NC - 1)
                        ins.then_inc(mix_done, 1)

            pe.wait_ge(rows_ready, 2)
            for p in range(2):
                pe.wait_ge(p_ge[p], B // 2)
                pe.wait_ge(p_ce[p], B // 2)
            steps(pe, run)


_INS = ["x", "ctx_1024", "g_xattn", "g_ffn", "L0_xattn_igate_w", "L0_xattn_igate_b", "L0_xattn_fgate_w",
        "L0_xattn_fgate_b", "L0_xattn_ln_scale", "L0_ffn_gamma1", "L0_ffn_Wq", "L0_ffn_bq", "L0_ffn_Wdown",
        "L0_ffn_bdown", "L0_ffn_Wup", "L0_ffn_bup", "L0_ffn_Wo", "L0_ffn_bo", "L0_ffn_gamma2", "L0_ffn_Wg",
        "L0_ffn_bg", "L0_ffn_We"]


def kernel(**inputs):
    import numpy as np
    import concourse.bacc as bacc
    from concourse.bass_utils import run_bass_kernel_spmd

    nc = bacc.Bacc("TRN2", target_bir_lowering=False, num_devices=1)
    arrays, args = {}, []
    for name in _INS:
        a = np.ascontiguousarray(inputs[name])
        arrays[f"in_{name}"] = a
        args.append(nc.dram_tensor(f"in_{name}", a.shape, mybir.dt.from_np(a.dtype), kind="ExternalInput").ap())
    out = nc.dram_tensor("out", arrays["in_x"].shape, F32, kind="ExternalOutput").ap()
    build(nc, *args, out)
    r = run_bass_kernel_spmd(nc, [arrays], core_ids=[0])
    return r.results[0]["out"]
```

```python
from contextlib import ExitStack

import concourse.bass as bass
from concourse import mybir

F32 = mybir.dt.float32
F32R = mybir.dt.float32r
BF16 = mybir.dt.bfloat16
F16 = mybir.dt.float16
ALU = mybir.AluOpType
ACT = mybir.ActivationFunctionType
AX = mybir.AxisListType

P = 128
MASK = 1e30
LN_EPS = 1e-5
RMS_EPS = 1e-6
CELL_EPS = 1e-6

SLOTS = ["A_cell", "B_scores", "X0", "B_max", "M0", "A_x1", "B_shift", "M1", "X1", "B_split", "A_rms",
         "B_values", "X2", "A_norm", "M2", "A_turn", "M3", "X3", "A_down", "X4", "A_q", "A_kv", "B_o", "X5",
         "B_turn_o", "M4", "B_wo", "X6", "M5", "X7", "B_rms", "M6", "B_turn_h2", "M7", "B_gate", "M8"]


class Chain:

    def __init__(self, eng, sem, base, per_round):
        self.eng, self.sem, self.base, self.per_round, self.n = eng, sem, base, per_round, 0

    def step(self, ins):
        ins.then_inc(self.sem, 1)
        self.n += 1
        assert self.n <= self.per_round
        self.eng.wait_ge(self.sem, self.base + self.n)


def at(s, step):
    return isinstance(s, int) and s == step


def wait(eng, sem, value):
    if isinstance(value, int) and value <= 0:
        return
    eng.wait_ge(sem, value)


def build(nc, x, ctx_in, g_xattn, g_ffn, igate_w, igate_b, fgate_w, fgate_b, ln_scale,
          gamma1, Wq, bq, Wdown, bdown, Wup, bup, Wo, bo, gamma2, Wg, bg, We, out):
    B, S, D = x.shape
    NH = igate_w.shape[0]
    DH = D // NH
    H = 16
    HD = D // H
    L = Wdown.shape[1]
    E = Wg.shape[1]
    NJ = S // P
    NC = D // P
    T8 = P // HD
    NG = S // T8
    R = NH * B
    VW = DH + 1
    TRI = P + S
    GP = 32 + NH
    EC = 512 // D
    NX = NJ * E // EC
    QSCALE = float(DH) ** -0.5
    HSCALE = float(HD) ** -0.5
    BIAS = {"q": (0, D), "up": (D, 2 * D), "o": (3 * D, D), "g": (4 * D, 32)}
    NB = 4 * D + 32
    assert (NJ, NC, T8, NG, R) == (2, 2, 8, 32, 64) and NX == 8 and L == 64 and NH == 8

    with ExitStack() as es:
        def sb(name, shape, dt=F32):
            return es.enter_context(nc.sbuf_tensor(name, shape, dt))

        def psum(name):
            return es.enter_context(nc.psum_tensor(name, [P, 512], F32))

        def sem(name):
            return es.enter_context(nc.semaphore(name))

        es.enter_context(nc.allow_non_contiguous_dma(reason="small vectors, once"))

        ident = sb("ident", [P, P])
        neg_ident = sb("neg_ident", [P, P])
        ident_bf = sb("ident_bf", [P, P], BF16)
        mask_bf = sb("mask_bf", [P, P], BF16)
        head_sel = sb("head_sel", [3 * NH, NH, P], BF16)
        block_ones = sb("block_ones", [P, P], F16)
        ones3 = sb("ones3", [3, P], BF16)
        minus_half = sb("minus_half", [P, 4])
        we_hi = sb("we_hi", [P, NC, E * D], F32R)
        we_lo = sb("we_lo", [P, NC, E * D], F32R)
        wq_raw = sb("wq_raw", [P, NC, D])
        wq_hi = sb("wq_hi", [P, NC, D], F32R)
        wq_lo = sb("wq_lo", [P, NC, D], F32R)
        wo_raw = sb("wo_raw", [P, NC, D])
        wo_hi = sb("wo_hi", [P, NC, D], F32R)
        wo_lo = sb("wo_lo", [P, NC, D], F32R)
        wd_raw = sb("wd_raw", [P, NC, L])
        wd_hi = sb("wd_hi", [P, NC, 2, L], F32R)
        wd_lo = sb("wd_lo", [P, NC, 2, L], F32R)
        wu_raw = sb("wu_raw", [P, 2 * D])
        wu_hi = sb("wu_hi", [P, 2 * D], F32R)
        wu_lo = sb("wu_lo", [L, 2 * D], F32R)
        wg_raw = sb("wg_raw", [P, NC, 32])
        wg_hi = sb("wg_hi", [P, NC, 32], F32R)
        wg_lo = sb("wg_lo", [P, NC, 32], F32R)
        bias3 = sb("bias3", [3, NB], BF16)
        bd_col = sb("bd_col", [P, 1])
        g1_col = sb("g1_col", [P, NC])
        g2_col = sb("g2_col", [P, NC])
        gx_col = sb("gx_col", [P, 1])
        gf_col = sb("gf_col", [P, 1])
        tx_col = sb("tx_col", [P, 1])
        tf_col = sb("tf_col", [P, 1])
        ls_row = sb("ls_row", [P, D])
        lst_row = sb("lst_row", [P, D])
        gw_raw = sb("gw_raw", [GP, 3 * D])
        gw_kv = sb("gw_kv", [GP, D])
        gw_t = sb("gw_t", [P, 2 * NC, GP])
        gb_col = sb("gb_col", [GP, 1])
        bs = [sb(f"bs{i}", [P, NJ, 6]) for i in range(2)]
        mv = [sb(f"mv{i}", [P, NJ, 2]) for i in range(2)]
        rstd = [sb(f"rstd{i}", [P, NJ]) for i in range(2)]
        qt_all = sb("qt_all", [P, NC, B * S])
        ct_all = sb("ct_all", [P, NC, B * S])
        m_part = sb("m_part", [R, 3, S], BF16)
        a_t = sb("a_t", [P, NJ, R])
        en_t = sb("en_t", [P, NJ, R])
        qt = sb("qt", [P, NC, S])
        ct = sb("ct", [P, NC, S])
        vals = sb("vals", [P, NJ, NH, VW])
        m_rows = sb("m_rows", [3 * NH, S], BF16)
        a_b = sb("a_b", [P, NJ, NH])
        decay = sb("decay", [P, 2, TRI])
        cell = sb("cell", [P, 2, TRI])
        hm = sb("hm", [P, NJ, NH, VW])
        en_b = sb("en_b", [P, NJ, NH])
        nrm = sb("nrm", [P, NJ, NH])
        fbs = sb("fbs", [P, NJ, 6])
        fmv = sb("fmv", [P, NJ, 2])
        frs = sb("frs", [P, 2, NJ])
        fpw = sb("fpw", [P, 2, NJ])
        gbs = sb("gbs", [P, NJ, 6])
        gmv = sb("gmv", [P, NJ, 2])
        grs = sb("grs", [P, NJ])
        gpw = sb("gpw", [P, NJ])
        sum_nat = sb("sum_nat", [P, NJ, H])
        rsum = sb("rsum", [P, NJ, H])
        ht_hi = sb("ht_hi", [P, NC, S], F32R)
        ht_lo = sb("ht_lo", [P, NC, S], F32R)
        dt = sb("dt", [P, S], F32R)
        q_nat = sb("q_nat", [P, NJ, HD, 2 * H], F16)
        kv_nat = sb("kv_nat", [P, NJ, H, 4 * H], F16)
        q_grp = sb("q_grp", [P, NG, 2 * H], F16)
        smax = sb("smax", [P, 4 * T8])
        smax_x = sb("smax_x", [P, 4 * T8, H])
        prob_hi = sb("prob_hi", [P, NG * H], F16)
        prob_lo = sb("prob_lo", [P, NG * H], F16)
        ot_hi = sb("ot_hi", [P, NC, S], F32R)
        ot_lo = sb("ot_lo", [P, NC, S], F32R)
        h2_hi = sb("h2_hi", [P, NC, S], F32R)
        h2_lo = sb("h2_lo", [P, NC, S], F32R)
        lg = sb("lg", [P, NJ, E])
        gmax = sb("gmax", [P, NJ])
        gate = sb("gate", [P, NJ, E])
        work = sb("work", [P, 14 * NJ * D])

        def part(k, parts=P):
            return work[0:parts, k * NJ * D:(k + 1) * NJ * D]

        xb, cb, xn = ([part(2 * k + i).rearrange("p (j d) -> p j d", j=NJ) for i in range(2)] for k in range(3))
        gates = work[0:GP, 6 * NJ * D:10 * NJ * D].rearrange("p (b s) -> p b s", b=B)
        ig, fg, row_a, row_b, row_c, row_m, en_row, zeros = (
            work[0:R, 10 * NJ * D + k * S:10 * NJ * D + (k + 1) * S] for k in range(8))
        we_raw = work[:, 0:NC * E * D].rearrange("p (c e n) -> p c e n", c=NC, e=E)
        x1, y, hn, x2, base, h2, acc, hcell, xf = (
            part(k).rearrange("p (j d) -> p j d", j=NJ) for k in range(9))
        sc_sb, prob, o_grp = (part(k) for k in range(9, 12))
        sum_grp = part(12, T8)
        o_nat = part(13).rearrange("p (j d) -> p j d", j=NJ)
        x1_old = wo_raw
        kv_all = sb("kv_all", [P, NG * T8 * 4 * H], F16)
        kv_grp = kv_all[:, :].rearrange("p (i t c) -> p i t c", i=NG, t=T8)
        bias_row = kv_all[0:1, 0:6 * NB].bitcast(F32).rearrange("p (k n) -> p k n", k=3)
        bias_part = kv_all[0:1, 6 * NB:9 * NB].bitcast(BF16).rearrange("p (k n) -> p k n", k=3)
        m_dram = nc.dram_tensor("m_dram", [3, R, S], BF16, kind="Internal").ap()
        q_dram = nc.dram_tensor("q_dram", [S, HD * 2 * H], F16, kind="Internal").ap()
        kv_dram = nc.dram_tensor("kv_dram", [S, H * 4 * H], F16, kind="Internal").ap()
        o_dram = nc.dram_tensor("o_dram", [S, D], F32, kind="Internal").ap()
        sum_dram = nc.dram_tensor("sum_dram", [S, H], F32, kind="Internal").ap()
        w0, w1, w2, bank_m, bank_s, bank_o, bank_x0, bank_x1 = (
            psum(n) for n in ("w0", "w1", "w2", "bank_m", "bank_s", "bank_o", "bank_x0", "bank_x1"))

        gwload, grp_zeroed, zeroed_dve = sem("gwload"), sem("grp_zeroed"), sem("zeroed_dve")
        wload = sem("wload")
        woload = sem("woload")
        eload = sem("eload")
        bload = sem("bload")
        xin = [sem(f"xin{i}") for i in range(2)]
        cin = [sem(f"cin{i}") for i in range(2)]
        gload = sem("gload")
        mstore = sem("mstore")
        mload = sem("mload")
        vload = sem("vload")
        xload = sem("xload")
        qkv_stored, grp_loaded = sem("qkv_stored"), sem("grp_loaded")
        o_stored, o_loaded = sem("o_stored"), sem("o_loaded")
        stored = sem("stored")
        alone = {e: sem(f"alone_{e.name}") for e in (mybir.EngineType.SP, mybir.EngineType.Pool, mybir.EngineType.DVE)}
        const_chain, consts = sem("const_chain"), sem("consts")
        zeroed = sem("zeroed")
        gw_sum, gw_turned, gw_ready = sem("gw_sum"), sem("gw_turned"), sem("gw_ready")
        prep_chain, bias_ready = sem("prep_chain"), sem("bias_ready")
        tanh_ready, scale_ready = sem("tanh_ready"), sem("scale_ready")
        w_hi_ready, w_lo_ready = sem("w_hi_ready"), sem("w_lo_ready")
        e_hi_ready, e_lo_ready = sem("e_hi_ready"), sem("e_lo_ready")

        def pair(name):
            return [sem(f"{name}{i}") for i in range(2)]

        p_bs, p_stat, p_var, p_rstd, p_xn = pair("p_bs"), pair("p_stat"), pair("p_var"), pair("p_rstd"), pair("p_xn")
        p_qT, p_cT, p_qe, p_ce, p_g, p_ge = pair("p_qT"), pair("p_cT"), pair("p_qe"), pair("p_ce"), pair("p_g"), pair("p_ge")
        row_dve, row_act, rows_turned, rows_ready = sem("row_dve"), sem("row_act"), sem("rows_turned"), sem("rows_ready")
        m_split = sem("m_split")
        a_ready = sem("a_ready")
        mb_ready, d_ready, s_ready, c_ready = sem("mb_ready"), sem("d_ready"), sem("s_ready"), sem("c_ready")
        pv_done, o_evict = sem("pv_done"), sem("o_evict")
        en_ready, hm_read = sem("en_ready"), sem("hm_read")
        a_chain, b_chain = sem("a_chain"), sem("b_chain")
        a_pool, b_pool = sem("a_pool"), sem("b_pool")
        x1_kept = sem("x1_kept")
        stat1, rs_a, stat2, rs_b = sem("stat1"), sem("rs_a"), sem("stat2"), sem("rs_b")
        y_ready, hn_ready = sem("y_ready"), sem("hn_ready")
        hT, hT_hi, hT_lo = sem("hT"), sem("hT_hi"), sem("hT_lo")
        dn, dn_hi, dn_lo = sem("dn"), sem("dn_hi"), sem("dn_lo")
        q_done, q_hi, q_lo = sem("q_done"), sem("q_hi"), sem("q_lo")
        kv_done, kv_hi, kv_lo = sem("kv_done"), sem("kv_hi"), sem("kv_lo")
        sc_done, sc_copied, scT, max_ready = sem("sc_done"), sem("sc_copied"), sem("scT"), sem("max_ready")
        shifted, e_hi, e_lo = sem("shifted"), sem("e_hi"), sem("e_lo")
        sums, values, sum_ready, o_ready = sem("sums"), sem("values"), sem("sum_ready"), sem("o_ready")
        o_normed = sem("o_normed")
        oT, oT_hi, oT_lo = sem("oT"), sem("oT_hi"), sem("oT_lo")
        wo_done, x2_ready, stat3, rs_c, h2_ready = sem("wo_done"), sem("x2_ready"), sem("stat3"), sem("rs_c"), sem("h2_ready")
        h2T, h2T_hi, h2T_lo = sem("h2T"), sem("h2T_hi"), sem("h2T_lo")
        lg_done, lg_ready, eg_ready, gate_ready = sem("lg_done"), sem("lg_ready"), sem("eg_ready"), sem("gate_ready")
        base_ready = sem("base_ready")
        mix_done, mix_acc = sem("mix_done"), sem("mix_acc")

        def steps(eng, run):
            run(0, True, False, False, False)
            run(1, True, True, False, False)
            run(2, True, True, True, False)
            run(3, True, True, True, True)
            with eng.Fori(4, B) as s:
                run(s, True, True, True, True)
            run(B, False, True, True, True)
            run(B + 1, False, False, True, True)
            run(B + 2, False, False, False, True)

        def apart(eng):
            eng.sem_inc(alone[eng.engine], 1)

        def first_steps(eng, run):
            run(0)
            with eng.Fori(1, B // 2) as i:
                run(i)

        def f32(ap):
            return ap.bitcast(F32)

        def tok(dram):
            return dram.rearrange("(j p) d -> p j d", p=P)

        k_hi, k_lo, v_hi, v_lo = (
            [kv_all[:, i * T8 * 4 * H + k:(i + 1) * T8 * 4 * H:4] for i in range(NG)] for k in range(4))
        kv_src = kv_dram.rearrange("(i t) (r c) -> t r i c", t=T8, r=H)
        q_src = q_dram.rearrange("(i t) (r c) -> (t r) i c", t=T8, r=HD)
        o_dst = o_dram.rearrange("(i t) (r c) -> (t r) i c", t=T8, r=HD)
        sum_dst = sum_dram.rearrange("(i t) c -> t i c", t=T8)
        NKV = T8 + 1
        W_LOADS = 16 * 13
        A_CHAIN, B_CHAIN, AB_POOL = 7, 7, 3
        bank_x = [bank_x0, bank_x1]
        turned = [(w0, w1, w2), (bank_m, bank_s, bank_o)]

        def kv_part(j, part):
            return kv_nat[:, j, :, :].rearrange("p r (n l) -> p (r n) l", l=2)[:, :, part]


        block = es.enter_context(nc.Block())

        @block.sync
        def _(sp):
            def first_pass(i):
                for p in range(2):
                    one = bass.ds(2 * i + p, 1)
                    wait(sp, p_xn[p], i)
                    sp.dma_start(xb[p][:, :, :], tok(x[one].rearrange("a s d -> (a s) d")))\
                      .then_inc(xin[p], 16)
                    wait(sp, p_cT[p], i)
                    sp.dma_start(cb[p][:, :, :], tok(ctx_in[one].rearrange("a s d -> (a s) d")))\
                      .then_inc(cin[p], 16)

            first_steps(sp, first_pass)
            sp.wait_ge(zeroed_dve, 1)
            for dst, src in (
                    (wq_raw[:, :, :], Wq.rearrange("(c p) n -> p c n", p=P)),
                    (wd_raw[:, :, :], Wdown.rearrange("(c p) n -> p c n", p=P)),
                    (wu_raw[0:L, :], Wup), (wu_raw[L:2 * L, :], Wup),
                    (wg_raw[:, :, 0:E], Wg.rearrange("(c p) n -> p c n", p=P)),
                    (bd_col[0:L, :], bdown.rearrange("(p a) -> p a", a=1)),
                    (bd_col[L:2 * L, :], bdown.rearrange("(p a) -> p a", a=1)),
                    (g1_col[:, :], gamma1.rearrange("(c p) -> p c", p=P)),
                    (g2_col[:, :], gamma2.rearrange("(c p) -> p c", p=P)),
                    (bias_row[:, 0, 0:D], bq.rearrange("(a n) -> a n", a=1)),
                    (bias_row[:, 0, D:3 * D], bup.rearrange("(a n) -> a n", a=1)),
                    (bias_row[:, 0, 3 * D:4 * D], bo.rearrange("(a n) -> a n", a=1)),
                    (bias_row[:, 0, 4 * D:4 * D + E], bg.rearrange("(a n) -> a n", a=1))):
                sp.dma_start(dst, src).then_inc(wload, 16)
            for p in range(2):
                sp.wait_ge(p_ge[p], B // 2)
            sp.dma_start(ig[:, :], gates[0:NH, :, :]).then_inc(gload, 16)
            sp.dma_start(fg[:, :], gates[32:GP, :, :]).then_inc(gload, 16)
            rows = P // H
            for c in range(NC):
                for r in range(rows):
                    sp.dma_start(wo_raw[r * H:(r + 1) * H, c, :],
                                 Wo.rearrange("(h d) n -> d h n", d=HD)[c * rows + r]).then_inc(woload, 16)
            sp.wait_ge(m_split, 1)
            sp.dma_start(m_dram.rearrange("k r s -> r k s"), m_part[:, :, :]).then_inc(mstore, 16)
            sp.wait_ge(mstore, 16)

            def load_m(b):
                wait(sp, s_ready, NH * b)
                cols = bass.ds(b * S, S)
                sp.dma_start(qt[:, :, :], qt_all[:, :, cols]).then_inc(mload, 16)
                sp.dma_start(ct[:, :, :], ct_all[:, :, cols]).then_inc(mload, 16)
                sp.dma_start(m_rows[:, :],
                             m_dram.rearrange("k (h b) s -> b (k h) s", b=B)[bass.ds(b, 1)]
                             .rearrange("a r s -> (a r) s")).then_inc(mload, 16)
                wait(sp, pv_done, NH * b)
                for j in range(NJ):
                    sp.dma_start(vals[:, j, :, 0:DH],
                                 ctx_in[bass.ds(b, 1), j * P:(j + 1) * P, :]
                                 .rearrange("a p (h e) -> (a p) h e", e=DH)).then_inc(vload, 16)

            def run(s, m, a, b, x_on, more):
                f, g, e = s - 1, s - 2, s - 3
                if m:
                    wait(sp, stat2, s)
                    sp.dma_start(xf[:, :, :], tok(x[bass.ds(s, 1)].rearrange("a s d -> (a s) d")))\
                      .then_inc(xload, 16)
                if b:
                    sp.wait_ge(o_ready, g + 1)
                    apart(sp)
                    wait(sp, o_loaded, 32 * g)
                    sp.dma_start(o_dst, o_grp[:, :].rearrange("p (i c) -> p i c", c=H)).then_inc(o_stored, 16)
                    sp.wait_ge(sum_ready, g + 1)
                    sp.dma_start(sum_dst, sum_grp[:, :].rearrange("p (i c) -> p i c", c=H)).then_inc(o_stored, 16)
                    sp.wait_ge(o_stored, 32 * (g + 1))
                    wait(sp, oT, g)
                    sp.dma_start(o_nat[:, :, :], tok(o_dram)).then_inc(o_loaded, 16)
                    sp.dma_start(sum_nat[:, :, :], tok(sum_dram)).then_inc(o_loaded, 16)
                if a:
                    if at(s, 1):
                        sp.wait_ge(grp_zeroed, 1)
                    sp.wait_ge(q_lo, f + 1)
                    apart(sp)
                    wait(sp, grp_loaded, 16 * NKV * f)
                    sp.dma_start(tok(q_dram), q_nat[:, :, :, :].rearrange("p j r c -> p j (r c)"))\
                      .then_inc(qkv_stored, 16)
                    sp.wait_ge(kv_lo, NJ * (f + 1))
                    sp.dma_start(tok(kv_dram), kv_nat[:, :, :, :].rearrange("p j r c -> p j (r c)"))\
                      .then_inc(qkv_stored, 16)
                    sp.wait_ge(qkv_stored, 32 * (f + 1))
                    wait(sp, values, f)
                    for t in range(T8):
                        sp.dma_start(kv_grp[t * H:(t + 1) * H, :, t, :], kv_src[t]).then_inc(grp_loaded, 16)
                    sp.dma_start(q_grp[:, :, :], q_src).then_inc(grp_loaded, 16)
                if x_on:
                    sp.wait_ge(mix_acc, NX * EC * (e + 1))
                    sp.dma_start(tok(out[bass.ds(e, 1)].rearrange("a s d -> (a s) d")), acc[:, :, :])\
                      .then_inc(stored, 16)
                if more:
                    load_m(s + 1)

            load_m(0)
            sp.wait_ge(bias_ready, 1)
            sp.dma_start(bias3[:, :], bias_part[:, :, :]).then_inc(bload, 16)
            run(0, True, False, False, False, True)
            run(1, True, True, False, False, True)
            run(2, True, True, True, False, True)
            run(3, True, True, True, True, True)
            with sp.Fori(4, B - 1) as s:
                run(s, True, True, True, True, True)
            run(B - 1, True, True, True, True, False)
            run(B, False, True, True, True, False)
            run(B + 1, False, False, True, True, False)
            run(B + 2, False, False, False, True, False)
            sp.wait_ge(stored, 16 * B)

        @block.gpsimd
        def _(pool):
            n = 0

            def made(ins):
                nonlocal n
                ins.then_inc(const_chain, 1)
                n += 1

            for buf, v in ((gw_raw, 0.0), (gb_col, 0.0)):
                pool.memset(buf[:, :], v).then_inc(zeroed, 1) if buf is gb_col else made(pool.memset(buf[:, :], v))
            for buf, v in ((ident, 0.0), (neg_ident, 0.0), (ident_bf, 0.0), (mask_bf, 0.0),
                           (block_ones, 1.0), (ones3, 1.0), (minus_half, -0.5), (zeros, 0.0)):
                made(pool.memset(buf[:, :], v))
            made(pool.memset(head_sel[:, :, :], 0.0))
            pool.wait_ge(const_chain, n)
            for m, fill in ((ident, 1.0), (neg_ident, -1.0), (ident_bf, 1.0)):
                made(pool.affine_select(out=m[:, :], in_=m[:, :], compare_op=ALU.not_equal, fill=fill,
                                        base=0, pattern=[[-1, P]], channel_multiplier=1))
            made(pool.affine_select(out=mask_bf[:, :], in_=mask_bf[:, :], compare_op=ALU.is_ge, fill=MASK,
                                    base=0, pattern=[[1, P]], channel_multiplier=-1))
            for k in range(3):
                pool.wait_ge(const_chain, n)
                made(pool.affine_select(out=head_sel[:, :, :], in_=head_sel[:, :, :],
                                        compare_op=ALU.not_equal, fill=1.0, base=-NH * k,
                                        pattern=[[-1, NH], [0, P]], channel_multiplier=1))
            bo_v = block_ones[:, :].rearrange("p (u c) -> p u c", c=HD)
            made(pool.affine_select(out=bo_v, in_=bo_v, compare_op=ALU.is_ge, fill=0.0, base=0,
                                    pattern=[[-HD, T8], [0, HD]], channel_multiplier=1))
            pool.wait_ge(const_chain, n)
            made(pool.affine_select(out=bo_v, in_=bo_v, compare_op=ALU.is_ge, fill=0.0, base=HD - 1,
                                    pattern=[[HD, T8], [0, HD]], channel_multiplier=-1))
            pool.wait_ge(const_chain, n)
            pool.memset(vals[:, :, :, :], 1.0).then_inc(consts, 1)

            def first_pass(i):
                for p in range(2):
                    pool.wait_ge(p_stat[p], i + 1)
                    wait(pool, p_xn[p], i)
                    apart(pool)
                    pool.tensor_scalar(rstd[p][:, :], mv[p][:, :, 1], LN_EPS, None, ALU.add).then_inc(p_var[p], 1)
                    pool.wait_ge(p_var[p], i + 1)
                    pool.tensor_tensor(rstd[p][:, :], rstd[p][:, :], minus_half[:, 0:NJ], ALU.pow)\
                        .then_inc(p_rstd[p], 1)

            first_steps(pool, first_pass)

            def run(s, m, a, b, x_on):
                f, g = s - 1, s - 2
                ch_a, ch_b = Chain(pool, a_pool, AB_POOL * f, AB_POOL), Chain(pool, b_pool, AB_POOL * g, AB_POOL)
                for slot in SLOTS:
                    if slot == "A_cell":
                        if a:
                            wait(pool, hm_read, f)
                            apart(pool)
                            pool.tensor_copy(en_b[:, :, :], en_t[:, :, bass.ds(f, NH, B)]).then_inc(en_ready, 1)
                        if m:
                            wait(pool, d_ready, NH * s)
                            apart(pool)
                            pool.tensor_copy(a_b[:, :, :], a_t[:, :, bass.ds(s, NH, B)]).then_inc(a_ready, 1)
                        if at(s, 0):
                            pool.wait_ge(bload, 16)
                            pool.memset(kv_all[:, :].bitcast(mybir.dt.uint32), 0).then_inc(grp_zeroed, 1)
                        if a:
                            pool.wait_ge(stat1, f + 1)
                            apart(pool)
                            ch_a.step(pool.tensor_scalar(fpw[:, 0, :], fmv[:, :, 1], LN_EPS, None, ALU.add))
                            pool.tensor_tensor(frs[:, 0, :], fpw[:, 0, :], minus_half[:, 0:NJ], ALU.pow)\
                                .then_inc(rs_a, 1)
                    if slot == "A_rms" and a:
                        pool.wait_ge(rs_a, f + 1)
                        pool.wait_ge(stat2, f + 1)
                        apart(pool)
                        ch_a.step(pool.tensor_scalar(fpw[:, 0, :], fmv[:, :, 1], LN_EPS, None, ALU.add))
                        apart(pool)
                        ch_a.step(pool.tensor_scalar(fpw[:, 1, :], fmv[:, :, 1], 1.0 + RMS_EPS, LN_EPS * RMS_EPS,
                                                     ALU.mult, ALU.add))
                        pool.tensor_tensor(frs[:, :, :], fpw[:, :, :],
                                           minus_half[:, :].rearrange("p (a b) -> p a b", a=2), ALU.pow)\
                            .then_inc(rs_b, 1)
                        pool.wait_ge(rs_b, f + 1)
                    if slot == "B_split" and b:
                        pool.wait_ge(e_hi, g + 1)
                        wait(pool, values, g)
                        pool.tensor_tensor(prob_lo[:, :], prob[:, :], prob_hi[:, :], ALU.subtract)\
                            .then_inc(e_lo, 1)
                    if slot == "B_rms" and b:
                        pool.wait_ge(stat3, g + 1)
                        wait(pool, h2_ready, g)
                        ch_b.step(pool.tensor_tensor(gpw[:, :], gmv[:, :, 0], gmv[:, :, 0], ALU.mult))
                        ch_b.step(pool.tensor_tensor(gpw[:, :], gpw[:, :], gmv[:, :, 1], ALU.add))
                        apart(pool)
                        ch_b.step(pool.tensor_scalar(gpw[:, :], gpw[:, :], RMS_EPS, None, ALU.add))
                        pool.tensor_tensor(grs[:, :], gpw[:, :], minus_half[:, 0:NJ], ALU.pow).then_inc(rs_c, 1)
                    if slot == "B_turn_h2" and a:
                        wait(pool, x2_ready, f)
                        apart(pool)
                        for j in range(NJ):
                            pool.tensor_scalar(y[:, j, :], x1[:, j, :], fmv[:, j, 0:1], frs[:, 0, j:j + 1],
                                               ALU.subtract, ALU.mult).then_inc(y_ready, 1)

            pool.wait_ge(rows_ready, 2)
            pool.wait_ge(e_hi_ready, 1)
            for c in range(NC):
                ins = pool.tensor_tensor(we_lo[:, c, :], we_raw[:, c, :, :].rearrange("p e n -> p (e n)"),
                                         f32(we_hi[:, c, :]), ALU.subtract)
            ins.then_inc(e_lo_ready, 1)
            steps(pool, run)

        @block.scalar
        def _(act):
            act.wait_ge(zeroed, 1)
            for dst, src in ((gw_raw[0:NH, :], igate_w), (gw_raw[32:GP, :], fgate_w),
                             (gb_col[0:NH, :], igate_b.rearrange("(p a) -> p a", a=1)),
                             (gb_col[32:GP, :], fgate_b.rearrange("(p a) -> p a", a=1)),
                             (gx_col[:, :], g_xattn.rearrange("(a n) -> a n", a=1).to_broadcast([P, 1])),
                             (gf_col[:, :], g_ffn.rearrange("(a n) -> a n", a=1).to_broadcast([P, 1])),
                             (ls_row[:, :], ln_scale.rearrange("(a n) -> a n", a=1).to_broadcast([P, D]))):
                act.dma_start(dst, src).then_inc(gwload, 16)
            act.wait_ge(gwload, 16 * 7)
            act.activation(tx_col[:, :], gx_col[:, :], ACT.Tanh).then_inc(tanh_ready, 1)
            act.activation(tf_col[:, :], gf_col[:, :], ACT.Tanh).then_inc(tanh_ready, 1)
            act.wait_ge(gw_turned, 1)
            act.activation(gw_t[:, :, :].rearrange("p k g -> p (k g)"), bank_x0[:, 0:2 * NC * GP], ACT.Copy)\
               .then_inc(gw_ready, 1)

            def first_pass(i):
                for p in range(2):
                    cols = bass.ds((2 * i + p) * S, S)
                    act.wait_ge(p_qT[p], i + 1)
                    act.activation(qt_all[:, :, cols],
                                   turned[p][0][:, :].rearrange("p (c s) -> p c s", c=NC), ACT.Copy)\
                       .then_inc(p_qe[p], 1)
                    act.wait_ge(p_g[p], i + 1)
                    act.activation(gates[:, bass.ds(2 * i + p, 1), :].rearrange("p a s -> p (a s)"),
                                   turned[p][2][0:GP, 0:S], ACT.Identity, bias=gb_col[:, 0:1])\
                       .then_inc(p_ge[p], 1)

            first_steps(act, first_pass)
            act.wait_ge(gload, 32)
            for c in range(NC):
                act.dma_start(we_raw[:, c, :, :], We.rearrange("e (c p) n -> c p e n", p=P)[c])\
                   .then_inc(eload, 16)

            act.wait_ge(row_dve, 1)
            act.activation(row_b[:, :], row_a[:, :], ACT.Exp, scale=-1.0).then_inc(row_act, 1)
            act.wait_ge(row_act, 1)
            act.activation(row_c[:, :], row_b[:, :], ACT.Ln, bias=1.0).then_inc(row_act, 1)
            act.wait_ge(row_dve, 6)
            act.activation(en_row[:, :], row_a[:, :], ACT.Exp, scale=-1.0).then_inc(row_act, 1)
            act.wait_ge(rows_turned, 1)
            act.activation(a_t[:, :, :].rearrange("p j r -> p (j r)"), w0[:, 0:NJ * R], ACT.Copy)\
               .then_inc(rows_ready, 1)
            act.activation(en_t[:, :, :].rearrange("p j r -> p (j r)"), w0[:, NJ * R:2 * NJ * R], ACT.Copy,
                           bias=CELL_EPS)\
               .then_inc(rows_ready, 1)

            def split_weights():
                act.wait_ge(eload, 16 * NC)
                for c in range(NC):
                    ins = act.activation(we_hi[:, c, :], we_raw[:, c, :, :].rearrange("p e n -> p (e n)"), ACT.Copy)
                ins.then_inc(e_hi_ready, 1)
                act.wait_ge(wload, W_LOADS)
                act.wait_ge(woload, 16 * NC * P // H)
                act.activation(wq_hi[:, :, :].rearrange("p c (d h) -> p c d h", h=H),
                               wq_raw[:, :, :].rearrange("p c (h d) -> p c d h", d=HD), ACT.Copy)
                act.activation(wo_hi[:, :, :], wo_raw[:, :, :], ACT.Copy)
                for k in range(2):
                    act.activation(wd_hi[:, :, k, :], wd_raw[:, :, :], ACT.Copy)
                act.activation(wg_hi[:, :, :], wg_raw[:, :, :], ACT.Copy)
                for k, order in enumerate(("p (h a d) -> p a d h", "p (h a d) -> p a h d")):
                    ins = act.activation(wu_hi[:, :].rearrange("p (r c a) -> p a r c", a=2, c=H)[:, k],
                                         wu_raw[:, :].rearrange(order, a=2, d=HD)[:, k], ACT.Copy)
                ins.then_inc(w_hi_ready, 1)

            def run(s, m, a, b, x_on):
                f, g, e = s - 1, s - 2, s - 3
                for slot in SLOTS:
                    if slot == "A_turn" and a:
                        act.wait_ge(hT, f + 1)
                        wait(act, q_done, f)
                        for c in range(NC):
                            ins = act.activation(ht_hi[:, c, :], w0[:, c * S:(c + 1) * S], ACT.Identity,
                                                 scale=g1_col[:, c:c + 1])
                        ins.then_inc(hT_hi, 1)
                    if slot == "A_down" and a:
                        act.wait_ge(dn, f + 1)
                        wait(act, kv_done, NJ * f)
                        act.activation(dt[:, :], w1[:, 0:S], ACT.Identity, bias=bd_col[:, 0:1])\
                           .then_inc(dn_hi, 1)
                    if slot == "A_q" and a:
                        act.wait_ge(q_done, f + 1)
                        wait(act, qkv_stored, 32 * f)
                        act.activation(q_nat[:, :, :, 0:H].rearrange("p j d c -> p (j d) c"),
                                       w2[:, :].rearrange("p (r c) -> p r c", c=H), ACT.Copy)\
                           .then_inc(q_hi, 1)
                    if slot == "A_kv" and a:
                        for j in range(NJ):
                            act.wait_ge(kv_done, NJ * f + j + 1)
                            act.activation(kv_part(j, 0), (w0, w1)[j][:, :], ACT.Copy).then_inc(kv_hi, 1)
                    if slot[0] == "M" and m:
                        h = int(slot[1:])
                        if h in (NH // 2 + 1, NH):
                            k = 0 if h < NH else 1
                            act.wait_ge(pv_done, NH * s + (k + 1) * NH // 2)
                            wait(act, hm_read, s)
                            act.activation(hm[:, :, k * NH // 2:(k + 1) * NH // 2, :],
                                           bank_o[:, 0:NJ * NH // 2 * VW]
                                           .rearrange("p (j h e) -> p j h e", j=NJ, h=NH // 2), ACT.Copy)\
                               .then_inc(o_evict, 1)
                        if h < NH:
                            act.wait_ge(mb_ready, NH * s + h + 1)
                            wait(act, c_ready, NH * s + h - 1)
                            if h == 0:
                                act.wait_ge(a_ready, s + 1)
                            act.activation(decay[:, h % 2, 0:S], bank_m[:, 0:S], ACT.Exp,
                                           bias=a_b[:, 0, h:h + 1], scale=-1.0)
                            act.activation(decay[:, h % 2, S:TRI], bank_m[:, S:TRI], ACT.Exp,
                                           bias=a_b[:, 1, h:h + 1], scale=-1.0).then_inc(d_ready, 1)
                    if slot == "B_scores" and b:
                        act.wait_ge(sc_done, g + 1)
                        wait(act, scT, g)
                        act.activation(sc_sb[:, :], w2[:, :], ACT.Copy).then_inc(sc_copied, 1)
                    if slot == "B_shift" and b:
                        act.wait_ge(shifted, g + 1)
                        wait(act, e_lo, g)
                        wait(act, values, g)
                        act.activation(prob_hi[:, :], w2[:, :], ACT.Exp, scale=HSCALE)
                        act.activation(prob[:, :], w2[:, :], ACT.Exp, scale=HSCALE).then_inc(e_hi, 1)
                    if slot == "B_values" and b:
                        act.wait_ge(sums, g + 1)
                        wait(act, o_stored, 32 * g)
                        act.activation(sum_grp[:, :], w1[0:T8, :], ACT.Copy).then_inc(sum_ready, 1)
                        act.wait_ge(values, g + 1)
                        act.activation(o_grp[:, :], w0[:, :], ACT.Copy).then_inc(o_ready, 1)
                    if slot == "B_turn_o" and b:
                        act.wait_ge(oT, g + 1)
                        wait(act, wo_done, g)
                        act.activation(ot_hi[:, :, :].rearrange("p c s -> p (c s)"), w2[:, :], ACT.Copy)\
                           .then_inc(oT_hi, 1)
                    if slot == "B_rms" and b:
                        act.wait_ge(rs_c, g + 1)
                        wait(act, h2T, g)
                        for j in range(NJ):
                            ins = act.activation(h2[:, j, :], x2[:, j, :], ACT.Identity, scale=grs[:, j:j + 1])
                        ins.then_inc(h2_ready, 1)
                    if slot == "B_turn_h2":
                        if b:
                            act.wait_ge(h2T, g + 1)
                            wait(act, mix_done, NX * g)
                            wait(act, lg_done, g)
                            for c in range(NC):
                                ins = act.activation(h2_hi[:, c, :], w0[:, c * S:(c + 1) * S], ACT.Identity,
                                                     scale=g2_col[:, c:c + 1])
                            ins.then_inc(h2T_hi, 1)
                        if a:
                            if at(s, 1):
                                act.wait_ge(w_lo_ready, 1)
                            wait(act, base_ready, f)
                            act.wait_ge(stat2, f + 1)
                            act.activation(x1_old[:, :, :], x1[:, :, :], ACT.Copy).then_inc(x1_kept, 1)
                    if slot == "B_gate" and b:
                        act.wait_ge(lg_ready, g + 1)
                        act.activation(lg[:, :, :], lg[:, :, :], ACT.Exp).then_inc(eg_ready, 1)

            split_weights()
            steps(act, run)

        @block.vector
        def _(dve):
            for buf in (wg_raw, bias_row):
                ins = dve.memset(buf[:, :, :], 0.0)
            ins.then_inc(zeroed_dve, 1)
            dve.wait_ge(gwload, 16 * 7)
            dve.tensor_tensor(gw_kv[:, :], gw_raw[:, D:2 * D], gw_raw[:, 2 * D:3 * D], ALU.add).then_inc(gw_sum, 1)
            dve.wait_ge(tanh_ready, 2)
            dve.tensor_scalar(lst_row[:, :], ls_row[:, :], tx_col[:, 0:1], None, ALU.mult).then_inc(scale_ready, 1)
            dve.wait_ge(scale_ready, 1)
            def first_pass(i):
                for p in range(2):
                    dve.wait_ge(xin[p], 16 * (i + 1))
                    for j in range(NJ):
                        ins = dve.bn_stats(bs[p][:, j, :], xb[p][:, j, :])
                    ins.then_inc(p_bs[p], 1)
                    dve.wait_ge(p_bs[p], i + 1)
                    apart(dve)
                    for j in range(NJ):
                        ins = dve.bn_aggr(mv[p][:, j, :], bs[p][:, j, :])
                    ins.then_inc(p_stat[p], 1)
                    dve.wait_ge(p_rstd[p], i + 1)
                    wait(dve, p_qT[p], i)
                    for j in range(NJ):
                        ins = dve.tensor_scalar(xn[p][:, j, :], xb[p][:, j, :], mv[p][:, j, 0:1],
                                                rstd[p][:, j:j + 1], ALU.subtract, ALU.mult)
                    ins.then_inc(p_xn[p], 1)
                    dve.wait_ge(p_cT[p], i + 1)
                    dve.tensor_copy(ct_all[:, :, bass.ds((2 * i + p) * S, S)],
                                    turned[p][1][:, :].rearrange("p (c s) -> p c s", c=NC)).then_inc(p_ce[p], 1)

            first_steps(dve, first_pass)

            rows = Chain(dve, row_dve, 0, 6)
            dve.wait_ge(gload, 32)
            rows.step(dve.scalar_tensor_tensor(out=row_a[:, :], in0=fg[:, :], scalar=-1.0, in1=fg[:, :],
                                               op0=ALU.mult, op1=ALU.max))
            dve.wait_ge(row_act, 2)
            rows.step(dve.scalar_tensor_tensor(out=row_a[:, :], in0=fg[:, :], scalar=0.0, in1=row_c[:, :],
                                               op0=ALU.min, op1=ALU.subtract))
            rows.step(dve.tensor_tensor_scan(row_b[:, :], row_a[:, :], zeros[:, :], 0.0, ALU.add, ALU.add))
            rows.step(dve.tensor_tensor(row_c[:, :], ig[:, :], row_b[:, :], ALU.subtract))
            rows.step(dve.tensor_tensor_scan(row_m[:, :], row_c[:, :], row_c[:, :], -3.0e38, ALU.max, ALU.max))
            rows.step(dve.tensor_tensor(row_a[:, :], row_b[:, :], row_m[:, :], ALU.add))
            parts = Chain(dve, prep_chain, 0, 9)
            parts.step(dve.tensor_copy(m_part[:, 0, :], row_m[:, :]))
            parts.step(dve.tensor_tensor(row_b[:, :], row_m[:, :], m_part[:, 0, :], ALU.subtract))
            parts.step(dve.tensor_copy(m_part[:, 1, :], row_b[:, :]))
            parts.step(dve.tensor_tensor(fg[:, :], row_b[:, :], m_part[:, 1, :], ALU.subtract))
            dve.tensor_copy(m_part[:, 2, :], fg[:, :]).then_inc(m_split, 1)

            dve.wait_ge(wload, W_LOADS)
            for k, order in enumerate(("p (h a d) -> p a d h", "p (h a d) -> p a h d")):
                dve.tensor_copy(bias_row[:, 1, D:3 * D].rearrange("p (r c a) -> p a r c", a=2, c=H)[:, k],
                                bias_row[:, 0, D:3 * D].rearrange(order, a=2, d=HD)[:, k])
            dve.tensor_copy(bias_row[:, 1, 3 * D:NB], bias_row[:, 0, 3 * D:NB])
            parts.step(dve.tensor_copy(bias_row[:, 1, 0:D].rearrange("p (d h) -> p d h", h=H),
                                       bias_row[:, 0, 0:D].rearrange("p (h d) -> p d h", d=HD)))
            parts.step(dve.tensor_copy(bias_part[:, 0, :], bias_row[:, 1, :]))
            parts.step(dve.tensor_tensor(bias_row[:, 2, :], bias_row[:, 1, :], bias_part[:, 0, :], ALU.subtract))
            parts.step(dve.tensor_copy(bias_part[:, 1, :], bias_row[:, 2, :]))
            parts.step(dve.tensor_tensor(bias_row[:, 0, :], bias_row[:, 2, :], bias_part[:, 1, :], ALU.subtract))
            dve.tensor_copy(bias_part[:, 2, :], bias_row[:, 0, :]).then_inc(bias_ready, 1)

            def split_weights():
                dve.wait_ge(w_hi_ready, 1)
                for c in range(NC):
                    dve.tensor_tensor(wq_lo[:, c, :].rearrange("p (d h) -> p d h", h=H),
                                      wq_raw[:, c, :].rearrange("p (h d) -> p d h", d=HD),
                                      f32(wq_hi[:, c, :]).rearrange("p (d h) -> p d h", h=H), ALU.subtract)
                dve.tensor_tensor(wo_lo[:, :, :], wo_raw[:, :, :], f32(wo_hi[:, :, :]), ALU.subtract)
                for k in range(2):
                    dve.tensor_tensor(wd_lo[:, :, k, :], wd_raw[:, :, :], f32(wd_hi[:, :, k, :]), ALU.subtract)
                dve.tensor_tensor(wg_lo[:, :, :], wg_raw[:, :, :], f32(wg_hi[:, :, :]), ALU.subtract)
                for k, order in enumerate(("p (h a d) -> p a d h", "p (h a d) -> p a h d")):
                    ins = dve.tensor_tensor(
                        wu_lo[:, :].rearrange("p (r c a) -> p a r c", a=2, c=H)[:, k],
                        wu_raw[0:L, :].rearrange(order, a=2, d=HD)[:, k],
                        f32(wu_hi[0:L, :]).rearrange("p (r c a) -> p a r c", a=2, c=H)[:, k], ALU.subtract)
                ins.then_inc(w_lo_ready, 1)

            def stats(ch, src, done, index, bn, mean_var):
                for j in range(NJ):
                    ins = dve.bn_stats(bn[:, j, :], src[:, j, :])
                ch.step(ins)
                apart(dve)
                for j in range(NJ):
                    ins = dve.bn_aggr(mean_var[:, j, :], bn[:, j, :])
                ins.then_inc(done, 1)

            def run(s, m, a, b, x_on):
                f, g, e = s - 1, s - 2, s - 3
                ch_a, ch_b = Chain(dve, a_chain, A_CHAIN * f, A_CHAIN), Chain(dve, b_chain, B_CHAIN * g, B_CHAIN)
                for slot in SLOTS:
                    if slot == "A_cell" and a:
                        if at(s, 1):
                            dve.wait_ge(e_lo_ready, 1)
                        dve.wait_ge(o_evict, 2 * (f + 1))
                        dve.wait_ge(en_ready, f + 1)
                        ch_a.step(dve.scalar_tensor_tensor(out=nrm[:, :, :], in0=hm[:, :, :, DH], scalar=-1.0,
                                                           in1=hm[:, :, :, DH], op0=ALU.mult, op1=ALU.max))
                        ch_a.step(dve.scalar_tensor_tensor(out=nrm[:, :, :], in0=nrm[:, :, :], scalar=CELL_EPS,
                                                           in1=en_b[:, :, :], op0=ALU.add, op1=ALU.max))
                        ch_a.step(dve.reciprocal(nrm[:, :, :], nrm[:, :, :]))
                        dve.tensor_tensor(hcell[:, :, :].rearrange("p j (h e) -> p (j h) e", e=DH),
                                          hm[:, :, :, 0:DH].rearrange("p j h e -> p (j h) e"),
                                          nrm[:, :, :].rearrange("p j h -> p (j h)").unsqueeze(2)
                                          .to_broadcast([P, NJ * NH, DH]), ALU.mult).then_inc(hm_read, 1)
                        dve.wait_ge(hm_read, f + 1)
                        wait(dve, y_ready, NJ * f)
                        stats(ch_a, hcell, stat1, f, fbs, fmv)
                    if slot == "A_x1" and a:
                        dve.wait_ge(stat1, f + 1)
                        for j in range(NJ):
                            ins = dve.scalar_tensor_tensor(out=hcell[:, j, :], in0=hcell[:, j, :],
                                                           scalar=fmv[:, j, 0:1], in1=lst_row[:, :],
                                                           op0=ALU.subtract, op1=ALU.mult)
                        ch_a.step(ins)
                        dve.wait_ge(rs_a, f + 1)
                        dve.wait_ge(xload, 16 * (f + 1))
                        wait(dve, x1_kept, f)
                        for j in range(NJ):
                            ins = dve.scalar_tensor_tensor(out=x1[:, j, :], in0=hcell[:, j, :],
                                                           scalar=frs[:, 0, j:j + 1], in1=xf[:, j, :],
                                                           op0=ALU.mult, op1=ALU.add)
                        ch_a.step(ins)
                        stats(ch_a, x1, stat2, f, fbs, fmv)
                    if slot == "A_norm" and a:
                        dve.wait_ge(stat2, f + 1)
                        dve.wait_ge(rs_b, f + 1)
                        wait(dve, hT, f)
                        for j in range(NJ):
                            ins = dve.tensor_scalar(hn[:, j, :], x1[:, j, :], fmv[:, j, 0:1], frs[:, 1, j:j + 1],
                                                    ALU.subtract, ALU.mult)
                        ins.then_inc(hn_ready, 1)
                        assert ch_a.n == A_CHAIN
                    if slot == "A_turn" and a:
                        dve.wait_ge(hT_hi, f + 1)
                        wait(dve, q_done, f)
                        for c in range(NC):
                            ins = dve.scalar_tensor_tensor(out=ht_lo[:, c, :], in0=w0[:, c * S:(c + 1) * S],
                                                           scalar=g1_col[:, c:c + 1], in1=f32(ht_hi[:, c, :]),
                                                           op0=ALU.mult, op1=ALU.subtract)
                        ins.then_inc(hT_lo, 1)
                    if slot == "A_down" and a:
                        dve.wait_ge(dn_hi, f + 1)
                        dve.scalar_tensor_tensor(out=dt[L:P, :], in0=w1[L:P, 0:S], scalar=bd_col[L:P, 0:1],
                                                 in1=f32(dt[L:P, :]), op0=ALU.add, op1=ALU.subtract)\
                           .then_inc(dn_lo, 1)
                    if slot == "A_q" and a:
                        dve.wait_ge(q_hi, f + 1)
                        q_v = q_nat[:, :, :, :].rearrange("p j d c -> p (j d) c")
                        dve.tensor_tensor(q_v[:, :, H:2 * H], w2[:, :].rearrange("p (r c) -> p r c", c=H),
                                          q_v[:, :, 0:H], ALU.subtract).then_inc(q_lo, 1)
                    if slot == "A_kv" and a:
                        for j in range(NJ):
                            dve.wait_ge(kv_hi, NJ * f + j + 1)
                            dve.tensor_tensor(kv_part(j, 1), (w0, w1)[j][:, :], kv_part(j, 0), ALU.subtract)\
                               .then_inc(kv_lo, 1)
                    if slot[0] == "M" and m and int(slot[1:]) < NH:
                        h = int(slot[1:])
                        dve.wait_ge(s_ready, NH * s + h + 1)
                        dve.wait_ge(d_ready, NH * s + h + 1)
                        wait(dve, pv_done, NH * s + h - 1)
                        dve.scalar_tensor_tensor(out=cell[:, h % 2, :], in0=bank_s[:, 0:TRI], scalar=QSCALE,
                                                 in1=decay[:, h % 2, :], op0=ALU.mult, op1=ALU.mult)\
                           .then_inc(c_ready, 1)
                        if h == 3 and at(s, 0):
                            split_weights()
                    if slot == "B_max" and b:
                        dve.wait_ge(scT, g + 1)
                        wait(dve, shifted, g)
                        ch_b.step(dve.tensor_reduce(smax[:, :], w0[:, :].rearrange("p (r g) -> p r g", g=H),
                                                    AX.X, ALU.max))
                        dve.tensor_copy(smax_x[:, :, :], smax[:, :].unsqueeze(2).to_broadcast([P, 4 * T8, H]))\
                           .then_inc(max_ready, 1)
                    if slot == "B_o" and b:
                        dve.wait_ge(o_loaded, 32 * (g + 1))
                        ch_b.step(dve.reciprocal(rsum[:, :, :], sum_nat[:, :, :]))
                        dve.tensor_tensor(o_nat[:, :, :].rearrange("p j (d h) -> p j d h", h=H),
                                          o_nat[:, :, :].rearrange("p j (d h) -> p j d h", h=H),
                                          rsum[:, :, :].unsqueeze(2).to_broadcast([P, NJ, HD, H]), ALU.mult)\
                           .then_inc(o_normed, 1)
                    if slot == "B_turn_o" and b:
                        dve.wait_ge(oT_hi, g + 1)
                        wait(dve, wo_done, g)
                        dve.tensor_tensor(ot_lo[:, :, :].rearrange("p c s -> p (c s)"), w2[:, :],
                                          f32(ot_hi[:, :, :]).rearrange("p c s -> p (c s)"), ALU.subtract)\
                           .then_inc(oT_lo, 1)
                    if slot == "B_wo" and b:
                        dve.wait_ge(wo_done, g + 1)
                        dve.wait_ge(y_ready, NJ * (g + 1))
                        wait(dve, h2_ready, g)
                        dve.tensor_tensor(x2[:, :, :].rearrange("p j d -> p (j d)"), w1[:, :],
                                          y[:, :, :].rearrange("p j d -> p (j d)"), ALU.add).then_inc(x2_ready, 1)
                        dve.wait_ge(x2_ready, g + 1)
                        stats(ch_b, x2, stat3, g, gbs, gmv)
                    if slot == "X7" and b:
                        dve.wait_ge(x1_kept, g + 1)
                        dve.scalar_tensor_tensor(out=base[:, :, :], in0=x2[:, :, :], scalar=tf_col[:, 0:1],
                                                 in1=x1_old[:, :, :], op0=ALU.mult, op1=ALU.add)\
                           .then_inc(base_ready, 1)
                    if slot == "B_turn_h2" and b:
                        dve.wait_ge(h2T_hi, g + 1)
                        for c in range(NC):
                            ins = dve.scalar_tensor_tensor(out=h2_lo[:, c, :], in0=w0[:, c * S:(c + 1) * S],
                                                           scalar=g2_col[:, c:c + 1], in1=f32(h2_hi[:, c, :]),
                                                           op0=ALU.mult, op1=ALU.subtract)
                        ins.then_inc(h2T_lo, 1)
                    if slot == "B_gate" and b:
                        logits = w1[:, 0:NJ * 32].rearrange("p (j n) -> p j n", j=NJ)[:, :, 0:E]
                        dve.wait_ge(lg_done, g + 1)
                        ch_b.step(dve.tensor_reduce(gmax[:, :], logits, AX.X, ALU.max))
                        dve.tensor_tensor(lg[:, :, :], logits, gmax[:, :].unsqueeze(2).to_broadcast([P, NJ, E]),
                                          ALU.subtract).then_inc(lg_ready, 1)
                        dve.wait_ge(eg_ready, g + 1)
                        ch_b.step(dve.tensor_reduce(gmax[:, :], lg[:, :, :], AX.X, ALU.add))
                        ch_b.step(dve.reciprocal(gmax[:, :], gmax[:, :]))
                        ch_b.step(dve.tensor_scalar(gmax[:, :], gmax[:, :], tf_col[:, 0:1], None, ALU.mult))
                        dve.tensor_tensor(gate[:, :, :], lg[:, :, :],
                                          gmax[:, :].unsqueeze(2).to_broadcast([P, NJ, E]), ALU.mult)\
                           .then_inc(gate_ready, 1)
                        assert ch_b.n == B_CHAIN
                    if slot[0] == "X" and x_on:
                        k = int(slot[1:])
                        j, n = divmod(k, E // EC)
                        if k == 0:
                            wait(dve, stored, 16 * e)
                            dve.wait_ge(gate_ready, e + 1)
                            dve.wait_ge(base_ready, e + 1)
                        dve.wait_ge(mix_done, NX * e + k + 1)
                        for u in range(EC):
                            ex = EC * n + u
                            dve.scalar_tensor_tensor(out=acc[:, j, :], in0=bank_x[k % 2][:, u * D:(u + 1) * D],
                                                     scalar=gate[:, j, ex:ex + 1],
                                                     in1=(base if ex == 0 else acc)[:, j, :],
                                                     op0=ALU.mult, op1=ALU.add).then_inc(mix_acc, 1)
                            dve.wait_ge(mix_acc, NX * EC * e + EC * k + u + 1)

            steps(dve, run)

        @block.tensor
        def _(pe):
            def split_mm(dst, a_hi, a_lo, b_hi, b_lo, start, stop):
                pe.matmul(dst, a_hi, b_hi, start=start, stop=False, skip_group_check=True)
                pe.matmul(dst, a_hi, b_lo, start=False, stop=False, skip_group_check=True)
                return pe.matmul(dst, a_lo, b_hi, start=False, stop=stop, skip_group_check=True)

            def bias_mm(dst, name):
                off, size = BIAS[name]
                return pe.matmul(dst, ones3[:, :], bias3[:, off:off + size], start=False, stop=True,
                                 skip_group_check=True)

            pe.wait_ge(consts, 1)
            pe.wait_ge(gw_sum, 1)
            for k in range(2 * NC):
                src = gw_raw[:, k * P:(k + 1) * P] if k < NC else gw_kv[:, (k - NC) * P:(k - NC + 1) * P]
                ins = pe.transpose(bank_x0[:, k * GP:(k + 1) * GP], src, ident[0:GP, 0:GP])
            ins.then_inc(gw_turned, 1)
            pe.wait_ge(gw_ready, 1)

            def first_pass(i):
                for p in range(2):
                    pe.wait_ge(cin[p], 16 * (i + 1))
                    wait(pe, p_ce[p], i)
                    for c in range(NC):
                        for j in range(NJ):
                            ins = pe.transpose(turned[p][1][:, c * S + j * P:c * S + (j + 1) * P],
                                               cb[p][:, j, c * P:(c + 1) * P], ident[:, :])
                    ins.then_inc(p_cT[p], 1)
                    pe.wait_ge(p_xn[p], i + 1)
                    wait(pe, p_qe[p], i)
                    for c in range(NC):
                        for j in range(NJ):
                            ins = pe.transpose(turned[p][0][:, c * S + j * P:c * S + (j + 1) * P],
                                               xn[p][:, j, c * P:(c + 1) * P], ident[:, :])
                    ins.then_inc(p_qT[p], 1)
                    pe.wait_ge(p_qe[p], i + 1)
                    pe.wait_ge(p_ce[p], i + 1)
                    wait(pe, p_ge[p], i)
                    cols = bass.ds((2 * i + p) * S, S)
                    for k in range(2 * NC):
                        src = (qt_all if k < NC else ct_all)[:, k % NC, cols]
                        ins = pe.matmul(turned[p][2][0:GP, 0:S], gw_t[:, k, :], src,
                                        start=(k == 0), stop=(k == 2 * NC - 1))
                    ins.then_inc(p_g[p], 1)

            first_steps(pe, first_pass)

            pe.wait_ge(row_act, 3)
            pe.wait_ge(p_qe[0], B // 2)
            for k, src in enumerate((row_c, en_row)):
                for j in range(NJ):
                    ins = pe.transpose(w0[:, (k * NJ + j) * R:(k * NJ + j + 1) * R], src[:, j * P:(j + 1) * P],
                                       ident[0:R, 0:R])
            ins.then_inc(rows_turned, 1)

            def run(s, m, a, b, x_on):
                f, g, e = s - 1, s - 2, s - 3
                for slot in SLOTS:
                    if slot == "A_turn" and a:
                        pe.wait_ge(hn_ready, f + 1)
                        if b:
                            pe.wait_ge(o_ready, g + 1)
                        for c in range(NC):
                            for j in range(NJ):
                                ins = pe.transpose(w0[:, c * S + j * P:c * S + (j + 1) * P],
                                                   hn[:, j, c * P:(c + 1) * P], ident[:, :])
                        ins.then_inc(hT, 1)
                    if slot == "A_down" and a:
                        if at(s, 1):
                            pe.wait_ge(w_lo_ready, 1)
                            pe.wait_ge(bload, 16)
                        pe.wait_ge(hT_lo, f + 1)
                        if b:
                            pe.wait_ge(sum_ready, g + 1)
                        for c in range(NC):
                            ins = split_mm(w1[:, 0:S], wd_hi[:, c, :, :].rearrange("p a l -> p (a l)"),
                                           wd_lo[:, c, :, :].rearrange("p a l -> p (a l)"),
                                           ht_hi[:, c, :], ht_lo[:, c, :], c == 0, c == NC - 1)
                        ins.then_inc(dn, 1)
                    if slot == "A_q" and a:
                        if b:
                            pe.wait_ge(e_hi, g + 1)
                        for j in range(NJ):
                            dst = w2[:, j * D:(j + 1) * D]
                            for c in range(NC):
                                split_mm(dst, ht_hi[:, c, j * P:(j + 1) * P], ht_lo[:, c, j * P:(j + 1) * P],
                                         wq_hi[:, c, :], wq_lo[:, c, :], c == 0, False)
                            ins = bias_mm(dst, "q")
                        ins.then_inc(q_done, 1)
                    if slot == "A_kv" and a:
                        pe.wait_ge(dn_lo, f + 1)
                        for j in range(NJ):
                            dst = (w0, w1)[j][:, :]
                            tk = slice(j * P, (j + 1) * P)
                            pe.matmul(dst, dt[:, tk], wu_hi[:, :], start=True, stop=False, skip_group_check=True)
                            pe.matmul(dst, dt[0:L, tk], wu_lo[:, :], start=False, stop=False, skip_group_check=True)
                            bias_mm(dst, "up").then_inc(kv_done, 1)
                    if slot[0] == "M" and m:
                        h = int(slot[1:])
                        if h == 0:
                            pe.wait_ge(mload, 16 * 3 * (s + 1))
                        if h < NH:
                            wait(pe, d_ready, NH * s + h)
                            sel = head_sel[:, h, :]
                            pe.matmul(bank_m[:, 0:S], sel, m_rows[:, :], start=True, stop=False, skip_group_check=True)
                            pe.matmul(bank_m[:, S:TRI], sel, m_rows[:, P:S], start=False, stop=False,
                                      skip_group_check=True)
                            pe.matmul(bank_m[:, 0:P], ident_bf[:, :], mask_bf[:, :], start=False, stop=False,
                                      skip_group_check=True)
                            pe.matmul(bank_m[:, S:TRI], ident_bf[:, :], mask_bf[:, :], start=False, stop=True,
                                      skip_group_check=True).then_inc(mb_ready, 1)
                            wait(pe, c_ready, NH * s + h)
                            per = P // DH
                            r = slice((h % per) * DH, (h % per + 1) * DH)
                            pe.matmul(bank_s[:, 0:S], ct[r, h // per, 0:P], qt[r, h // per, :], start=True,
                                      stop=False, skip_group_check=True)
                            pe.matmul(bank_s[:, S:TRI], ct[r, h // per, P:S], qt[r, h // per, P:S], start=False,
                                      stop=True, skip_group_check=True).then_inc(s_ready, 1)
                        if h > 0:
                            done = h - 1
                            if h == 1:
                                pe.wait_ge(vload, 16 * NJ * (s + 1))
                            pe.wait_ge(c_ready, NH * s + h)
                            if done % (NH // 2) == 0:
                                wait(pe, o_evict, 2 * s + done // (NH // 2))
                            for j in range(NJ):
                                col = (j * NH // 2 + done % (NH // 2)) * VW
                                dst = bank_o[:, col:col + VW]
                                if j == 0:
                                    pe.matmul(dst, cell[:, done % 2, 0:P], vals[:, 0, done, :], start=True, stop=True)
                                else:
                                    pe.matmul(dst, cell[:, done % 2, P:S], vals[:, 0, done, :], start=True, stop=False)
                                    pe.matmul(dst, cell[:, done % 2, S:TRI], vals[:, 1, done, :], start=False, stop=True)\
                                      .then_inc(pv_done, 1)
                    if slot == "B_scores" and b:
                        if at(s, 2):
                            pe.wait_ge(grp_zeroed, 1)
                        pe.wait_ge(grp_loaded, 16 * NKV * (g + 1))
                        wait(pe, oT_lo, g)
                        pe.wait_ge(q_lo, g + 1)
                        for i in range(NG):
                            dst = w2[:, i * H:(i + 1) * H]
                            ins = split_mm(dst, k_hi[i], k_lo[i], q_grp[:, i, 0:H], q_grp[:, i, H:2 * H],
                                           i == 0, i == NG - 1)
                        ins.then_inc(sc_done, 1)
                    if slot == "B_max" and b:
                        pe.wait_ge(sc_copied, g + 1)
                        wait(pe, h2T_lo, g)
                        pe.wait_ge(kv_lo, NJ * (g + 1))
                        for col in range(4):
                            ins = pe.transpose(w0[:, col * P:(col + 1) * P], sc_sb[:, col * P:(col + 1) * P], ident[:, :])
                        ins.then_inc(scT, 1)
                    if slot == "B_shift" and b:
                        pe.wait_ge(max_ready, g + 1)
                        for col in range(4):
                            ins = pe.matmul(w2[:, col * P:(col + 1) * P],
                                            smax_x[:, col * T8:(col + 1) * T8, :].rearrange("p t g -> p (t g)"), neg_ident[:, :],
                                            start=False, stop=(col == 3), skip_group_check=True)
                        ins.then_inc(shifted, 1)
                    if slot == "B_values" and b:
                        pe.wait_ge(e_hi, g + 1)
                        pe.wait_ge(e_lo, g + 1)
                        wait(pe, lg_ready, g)
                        pe.matmul(w1[0:T8, :], block_ones[:, 0:P:H], prob_hi[:, :], start=True, stop=False)
                        pe.matmul(w1[0:T8, :], block_ones[:, 0:P:H], prob_lo[:, :], start=False, stop=True)\
                          .then_inc(sums, 1)
                        for i in range(NG):
                            c = slice(i * H, (i + 1) * H)
                            ins = split_mm(w0[:, c], v_hi[i], v_lo[i], prob_hi[:, c], prob_lo[:, c],
                                           i == 0, i == NG - 1)
                        ins.then_inc(values, 1)
                    if slot == "B_turn_o" and b:
                        pe.wait_ge(o_normed, g + 1)
                        if a:
                            pe.wait_ge(q_lo, f + 1)
                        for c in range(NC):
                            for j in range(NJ):
                                ins = pe.transpose(w2[:, c * S + j * P:c * S + (j + 1) * P],
                                                   o_nat[:, j, c * P:(c + 1) * P], ident[:, :])
                        ins.then_inc(oT, 1)
                    if slot == "B_wo" and b:
                        pe.wait_ge(oT_lo, g + 1)
                        if a:
                            pe.wait_ge(kv_lo, NJ * (f + 1))
                        for j in range(NJ):
                            dst = w1[:, j * D:(j + 1) * D]
                            for c in range(NC):
                                split_mm(dst, ot_hi[:, c, j * P:(j + 1) * P], ot_lo[:, c, j * P:(j + 1) * P],
                                         wo_hi[:, c, :], wo_lo[:, c, :], c == 0, False)
                            ins = bias_mm(dst, "o")
                        ins.then_inc(wo_done, 1)
                    if slot == "B_turn_h2" and b:
                        pe.wait_ge(h2_ready, g + 1)
                        if a:
                            pe.wait_ge(kv_lo, NJ * (f + 1))
                        for c in range(NC):
                            for j in range(NJ):
                                ins = pe.transpose(w0[:, c * S + j * P:c * S + (j + 1) * P],
                                                   h2[:, j, c * P:(c + 1) * P], ident[:, :])
                        ins.then_inc(h2T, 1)
                    if slot == "B_gate" and b:
                        pe.wait_ge(h2T_lo, g + 1)
                        pe.wait_ge(x2_ready, g + 1)
                        for j in range(NJ):
                            dst = w1[:, j * 32:(j + 1) * 32]
                            for c in range(NC):
                                split_mm(dst, h2_hi[:, c, j * P:(j + 1) * P], h2_lo[:, c, j * P:(j + 1) * P],
                                         wg_hi[:, c, :], wg_lo[:, c, :], c == 0, False)
                            ins = bias_mm(dst, "g")
                        ins.then_inc(lg_done, 1)
                    if slot[0] == "X" and x_on:
                        k = int(slot[1:])
                        j, n = divmod(k, E // EC)
                        if k < 2:
                            if at(s, 3):
                                pe.wait_ge(e_lo_ready, 1)
                            wait(pe, mix_acc, NX * EC * e)
                        else:
                            pe.wait_ge(mix_acc, NX * EC * e + EC * (k - 1))
                        cols = slice(n * 512, (n + 1) * 512)
                        for c in range(NC):
                            ins = split_mm(bank_x[k % 2][:, :], h2_hi[:, c, j * P:(j + 1) * P],
                                           h2_lo[:, c, j * P:(j + 1) * P], we_hi[:, c, cols], we_lo[:, c, cols],
                                           c == 0, c == NC - 1)
                        ins.then_inc(mix_done, 1)

            pe.wait_ge(rows_ready, 2)
            for p in range(2):
                pe.wait_ge(p_ge[p], B // 2)
                pe.wait_ge(p_ce[p], B // 2)
            steps(pe, run)


_INS = ["x", "ctx_1024", "g_xattn", "g_ffn", "L0_xattn_igate_w", "L0_xattn_igate_b", "L0_xattn_fgate_w",
        "L0_xattn_fgate_b", "L0_xattn_ln_scale", "L0_ffn_gamma1", "L0_ffn_Wq", "L0_ffn_bq", "L0_ffn_Wdown",
        "L0_ffn_bdown", "L0_ffn_Wup", "L0_ffn_bup", "L0_ffn_Wo", "L0_ffn_bo", "L0_ffn_gamma2", "L0_ffn_Wg",
        "L0_ffn_bg", "L0_ffn_We"]


def kernel(**inputs):
    import numpy as np
    import concourse.bacc as bacc
    from concourse.bass_utils import run_bass_kernel_spmd

    nc = bacc.Bacc("TRN2", target_bir_lowering=False, num_devices=1)
    arrays, args = {}, []
    for name in _INS:
        a = np.ascontiguousarray(inputs[name])
        arrays[f"in_{name}"] = a
        args.append(nc.dram_tensor(f"in_{name}", a.shape, mybir.dt.from_np(a.dtype), kind="ExternalInput").ap())
    out = nc.dram_tensor("out", arrays["in_x"].shape, F32, kind="ExternalOutput").ap()
    build(nc, *args, out)
    r = run_bass_kernel_spmd(nc, [arrays], core_ids=[0])
    return r.results[0]["out"]
```

```python
from contextlib import ExitStack

import concourse.bass as bass
from concourse import mybir

F32 = mybir.dt.float32
F32R = mybir.dt.float32r
BF16 = mybir.dt.bfloat16
F16 = mybir.dt.float16
ALU = mybir.AluOpType
ACT = mybir.ActivationFunctionType
AX = mybir.AxisListType

P = 128
MASK = 1e30
LN_EPS = 1e-5
RMS_EPS = 1e-6
CELL_EPS = 1e-6

SLOTS = ["A_cell", "B_scores", "M0", "B_max", "X0", "A_x1", "B_shift", "M1", "X1", "B_split", "A_rms",
         "B_values", "A_norm", "M2", "X2", "A_turn", "X3", "M3", "X4", "A_down", "B_o", "A_q", "X5",
         "A_kv", "B_turn_o", "M4", "B_wo", "X6", "M5", "X7", "B_rms", "M6", "B_turn_h2", "M7", "B_gate",
         "M8", "B_logits"]


class Chain:

    def __init__(self, eng, sem, base, per_round):
        self.eng, self.sem, self.base, self.per_round, self.n = eng, sem, base, per_round, 0

    def step(self, ins):
        ins.then_inc(self.sem, 1)
        self.n += 1
        assert self.n <= self.per_round
        self.eng.wait_ge(self.sem, self.base + self.n)


def at(s, step):
    return isinstance(s, int) and s == step


def wait(eng, sem, value):
    if isinstance(value, int) and value <= 0:
        return
    eng.wait_ge(sem, value)


def build(nc, x, ctx_in, g_xattn, g_ffn, igate_w, igate_b, fgate_w, fgate_b, ln_scale,
          gamma1, Wq, bq, Wdown, bdown, Wup, bup, Wo, bo, gamma2, Wg, bg, We, out):
    B, S, D = x.shape
    NH = igate_w.shape[0]
    DH = D // NH
    H = 16
    HD = D // H
    L = Wdown.shape[1]
    E = Wg.shape[1]
    NJ = S // P
    NC = D // P
    T8 = P // HD
    NG = S // T8
    R = NH * B
    VW = DH + 1
    TRI = P + S
    GP = 32 + NH
    EC = 512 // D
    NX = NJ * E // EC
    QSCALE = float(DH) ** -0.5
    HSCALE = float(HD) ** -0.5
    BIAS = {"q": (0, D), "up": (D, 2 * D)}
    NB = 3 * D
    assert (NJ, NC, T8, NG, R) == (2, 2, 8, 32, 64) and NX == 8 and L == 64 and NH == 8

    with ExitStack() as es:
        def sb(name, shape, dt=F32):
            return es.enter_context(nc.sbuf_tensor(name, shape, dt))

        def psum(name):
            return es.enter_context(nc.psum_tensor(name, [P, 512], F32))

        def sem(name):
            return es.enter_context(nc.semaphore(name))

        es.enter_context(nc.allow_non_contiguous_dma(reason="small vectors, once"))

        ident = sb("ident", [P, P])
        neg_ident = sb("neg_ident", [P, P])
        ident_bf = sb("ident_bf", [P, P], BF16)
        mask_bf = sb("mask_bf", [P, P], BF16)
        head_sel = sb("head_sel", [3 * NH, NH, P], BF16)
        block_ones = sb("block_ones", [P, P], F16)
        ones3 = sb("ones3", [3, P], BF16)
        minus_half = sb("minus_half", [P, 4])
        zero_col = sb("zero_col", [P, 1])
        we_hi = sb("we_hi", [P, NC, E * D], F32R)
        we_lo = sb("we_lo", [P, NC, E * D], F32R)
        wq_hi = sb("wq_hi", [P, NC, D], F32R)
        wq_lo = sb("wq_lo", [P, NC, D], F32R)
        wo_raw = sb("wo_raw", [P, NC, D])
        wo_hi = sb("wo_hi", [P, NC, D], F32R)
        wo_lo = sb("wo_lo", [P, NC, D], F32R)
        wd_raw = sb("wd_raw", [P, NC, L])
        wd_hi = sb("wd_hi", [P, NC, 2, L], F32R)
        wd_lo = sb("wd_lo", [P, NC, 2, L], F32R)
        wu_hi = sb("wu_hi", [P, 2 * D], F32R)
        wu_lo = sb("wu_lo", [L, 2 * D], F32R)
        wg_raw = sb("wg_raw", [P, NC, 32])
        wg_hi = sb("wg_hi", [P, NC, 32], F32R)
        wg_lo = sb("wg_lo", [P, NC, 32], F32R)
        bias3 = sb("bias3", [3, NB], BF16)
        bd_col = sb("bd_col", [P, 1])
        g1_col = sb("g1_col", [P, NC])
        g2_col = sb("g2_col", [P, NC])
        bg_col = sb("bg_col", [32, 1])
        gx_col = sb("gx_col", [P, 1])
        gf_col = sb("gf_col", [P, 1])
        tx_col = sb("tx_col", [P, 1])
        tf_col = sb("tf_col", [P, 1])
        lst_row = sb("lst_row", [P, D])
        bo_row = sb("bo_row", [P, D])
        gw_t = sb("gw_t", [P, 2 * NC, GP])
        gb_col = sb("gb_col", [GP, 1])
        bs = [sb(f"bs{i}", [P, NJ, 6]) for i in range(2)]
        mv = [sb(f"mv{i}", [P, NJ, 2]) for i in range(2)]
        rstd = [sb(f"rstd{i}", [P, NJ]) for i in range(2)]
        qt_all = sb("qt_all", [P, NC, B * S])
        ct_all = sb("ct_all", [P, NC, B * S])
        a_t = sb("a_t", [P, NJ, R])
        en_t = sb("en_t", [P, NJ, R])
        vals = sb("vals", [P, NJ, NH, VW])
        k_parts = sb("k_parts", [P, NH, S], F32R)
        q_parts = sb("q_parts", [P, NH, S], F32R)
        m_rows = sb("m_rows", [3 * NH, S], BF16)
        a_b = sb("a_b", [P, NJ, NH])
        decay = sb("decay", [P, 2, TRI])
        cell = sb("cell", [P, 2, TRI])
        hm = sb("hm", [P, NJ, NH, VW])
        en_b = sb("en_b", [P, NJ, NH])
        nrm = sb("nrm", [P, NJ, NH])
        fbs = sb("fbs", [P, NJ, 6])
        fmv = sb("fmv", [P, NJ, 2])
        frs = sb("frs", [P, 2, NJ])
        fpw = sb("fpw", [P, 2, NJ])
        gbs = sb("gbs", [P, NJ, 6])
        gmv = sb("gmv", [P, NJ, 2])
        grs = sb("grs", [P, NJ])
        gpw = sb("gpw", [P, NJ])
        sum_nat = sb("sum_nat", [P, NJ, H])
        rsum = sb("rsum", [P, NJ, H])
        ht_hi = sb("ht_hi", [P, NC, S], F32R)
        ht_lo = sb("ht_lo", [P, NC, S], F32R)
        dt = sb("dt", [P, S], F32R)
        q_nat = sb("q_nat", [P, NJ, HD, 2 * H], F16)
        kv_nat = sb("kv_nat", [P, NJ, H, 4 * H], F16)
        q_grp = sb("q_grp", [P, NG, 2 * H], F16)
        smax = sb("smax", [P, 4 * T8])
        smax_x = sb("smax_x", [P, 4 * T8, H])
        prob_hi = sb("prob_hi", [P, NG * H], F16)
        prob_lo = sb("prob_lo", [P, NG * H], F16)
        ot_hi = sb("ot_hi", [P, NC, S], F32R)
        ot_lo = sb("ot_lo", [P, NC, S], F32R)
        h2_hi = sb("h2_hi", [P, NC, S], F32R)
        h2_lo = sb("h2_lo", [P, NC, S], F32R)
        lg_t = sb("lg_t", [P, S])
        lg = sb("lg", [P, NJ, E])
        gmax = sb("gmax", [P, NJ])
        gate = sb("gate", [P, NJ, E])
        work = sb("work", [P, 14 * NJ * D])

        def part(k, parts=P):
            return work[0:parts, k * NJ * D:(k + 1) * NJ * D]


        def flat(ap, dt=F32):
            return ap.rearrange("p a b -> p (a b)").bitcast(dt)

        cb = [t[:, 0:NJ * D].rearrange("p (j d) -> p j d", j=NJ)
              for t in (flat(cell[:, :, :]), flat(hm[:, :, :, :].rearrange("p j h e -> p j (h e)")))]
        gw_raw = flat(decay[0:GP, :, :])
        gw_kv = prob_hi[0:GP, :].bitcast(F32)
        ls_row = prob_lo[:, :].bitcast(F32)
        wq_raw = smax_x[:, :, :].rearrange("p a b -> p (a b)").rearrange("p (c n) -> p c n", c=NC)
        wu_raw = q_nat[:, :, :, :].rearrange("p j d c -> p (j d c)").bitcast(F32)
        m_part = kv_nat[0:R, :, :, :].rearrange("p j r c -> p (j r c)")[:, 0:3 * S].bitcast(BF16)\
            .rearrange("p (k s) -> p k s", k=3)
        xn = [part(8 + i).rearrange("p (j d) -> p j d", j=NJ) for i in range(2)]
        gates = work[0:GP, 10 * NJ * D:14 * NJ * D].rearrange("p (b s) -> p b s", b=B)
        we_raw = work[:, 0:NC * E * D].rearrange("p (c e n) -> p c e n", c=NC, e=E)
        x1, y, hn, x2, base, h2, acc, hcell, xf = (
            part(k).rearrange("p (j d) -> p j d", j=NJ) for k in range(9))
        sc_sb, prob, o_grp = (part(k) for k in range(9, 12))
        sum_grp = part(12, T8)
        o_nat = part(13).rearrange("p (j d) -> p j d", j=NJ)
        x1_old = wo_raw
        kv_all = sb("kv_all", [P, NG * T8 * 4 * H], F16)
        kv_grp = kv_all[:, :].rearrange("p (i t c) -> p i t c", i=NG, t=T8)
        bias_row = kv_all[0:1, 0:6 * NB].bitcast(F32).rearrange("p (k n) -> p k n", k=3)
        x0 = NG * T8 * 4 * H - 2 * B * NJ * D
        x_all = kv_all[:, x0:].bitcast(F32).rearrange("p (b j d) -> p b j d", b=B, j=NJ)
        rows0 = NG * T8 * 4 * H - 8 * 2 * S
        ig, fg, row_a, row_b, row_c, row_m, en_row, zeros = (
            kv_all[0:R, rows0 + 2 * k * S:rows0 + 2 * (k + 1) * S].bitcast(F32) for k in range(8))
        assert 6 * NB <= x0 and 9 * NB <= rows0
        bias_part = kv_all[0:1, 6 * NB:9 * NB].bitcast(BF16).rearrange("p (k n) -> p k n", k=3)
        m_dram = nc.dram_tensor("m_dram", [3, R, S], BF16, kind="Internal").ap()
        q_dram = nc.dram_tensor("q_dram", [S, HD * 2 * H], F16, kind="Internal").ap()
        kv_dram = nc.dram_tensor("kv_dram", [S, H * 4 * H], F16, kind="Internal").ap()
        o_dram = nc.dram_tensor("o_dram", [S, D], F32, kind="Internal").ap()
        sum_dram = nc.dram_tensor("sum_dram", [S, H], F32, kind="Internal").ap()
        w0, w1, w2, bank_m, bank_s, bank_o, bank_x0, bank_x1 = (
            psum(n) for n in ("w0", "w1", "w2", "bank_m", "bank_s", "bank_o", "bank_x0", "bank_x1"))

        gwload, vecload = sem("gwload"), sem("vecload")
        grp_zeroed, zeroed_dve = sem("grp_zeroed"), sem("zeroed_dve")
        wload = sem("wload")
        woload = sem("woload")
        eload = sem("eload")
        bload = sem("bload")
        xin = [sem(f"xin{i}") for i in range(2)]
        cin = [sem(f"cin{i}") for i in range(2)]
        gload = sem("gload")
        mstore = sem("mstore")
        mload = sem("mload")
        vload = sem("vload")
        xload = sem("xload")
        qkv_stored, grp_loaded = sem("qkv_stored"), sem("grp_loaded")
        o_stored, o_loaded = sem("o_stored"), sem("o_loaded")
        stored = sem("stored")
        alone = {e: sem(f"alone_{e.name}") for e in (mybir.EngineType.SP, mybir.EngineType.Pool, mybir.EngineType.DVE)}
        const_chain, consts, ident_ready = sem("const_chain"), sem("consts"), sem("ident_ready")
        zeroed = sem("zeroed")
        gw_sum, gw_turned, gw_ready = sem("gw_sum"), sem("gw_turned"), sem("gw_ready")
        prep_chain, bias_ready = sem("prep_chain"), sem("bias_ready")
        tanh_ready, scale_ready = sem("tanh_ready"), sem("scale_ready")
        w_hi_ready, w_lo_ready = sem("w_hi_ready"), sem("w_lo_ready")
        e_hi_ready, e_lo_ready = sem("e_hi_ready"), sem("e_lo_ready")

        def pair(name):
            return [sem(f"{name}{i}") for i in range(2)]

        p_bs, p_stat, p_var, p_rstd, p_xn = pair("p_bs"), pair("p_stat"), pair("p_var"), pair("p_rstd"), pair("p_xn")
        p_qT, p_cT, p_qe, p_ce, p_g, p_ge = pair("p_qT"), pair("p_cT"), pair("p_qe"), pair("p_ce"), pair("p_g"), pair("p_ge")
        row_dve, row_act, rows_turned, rows_ready = sem("row_dve"), sem("row_act"), sem("rows_turned"), sem("rows_ready")
        m_split, zeros_ready = sem("m_split"), sem("zeros_ready")
        parts_zeroed, qk_hi, qk_lo = sem("parts_zeroed"), sem("qk_hi"), sem("qk_lo")
        a_ready = sem("a_ready")
        mb_ready, d_ready, s_ready, c_ready = sem("mb_ready"), sem("d_ready"), sem("s_ready"), sem("c_ready")
        pv_done, o_evict = sem("pv_done"), sem("o_evict")
        en_ready, hm_read = sem("en_ready"), sem("hm_read")
        a_chain, b_chain = sem("a_chain"), sem("b_chain")
        a_pool, b_pool = sem("a_pool"), sem("b_pool")
        x1_kept = sem("x1_kept")
        stat1, rs_a, stat2, rs_b = sem("stat1"), sem("rs_a"), sem("stat2"), sem("rs_b")
        y_normed, y_ready, hn_ready = sem("y_normed"), sem("y_ready"), sem("hn_ready")
        hT, hT_hi, hT_lo = sem("hT"), sem("hT_hi"), sem("hT_lo")
        dn, dn_hi, dn_lo = sem("dn"), sem("dn_hi"), sem("dn_lo")
        q_done, q_hi, q_lo = sem("q_done"), sem("q_hi"), sem("q_lo")
        kv_done, kv_hi, kv_lo = sem("kv_done"), sem("kv_hi"), sem("kv_lo")
        sc_done, sc_copied, scT, max_ready = sem("sc_done"), sem("sc_copied"), sem("scT"), sem("max_ready")
        shifted, e_hi, e_lo = sem("shifted"), sem("e_hi"), sem("e_lo")
        sums, values, sum_ready, o_ready = sem("sums"), sem("values"), sem("sum_ready"), sem("o_ready")
        o_normed = sem("o_normed")
        oT, oT_hi, oT_lo = sem("oT"), sem("oT_hi"), sem("oT_lo")
        wo_done, x2_ready, stat3, rs_c, h2_ready = sem("wo_done"), sem("x2_ready"), sem("stat3"), sem("rs_c"), sem("h2_ready")
        h2T, h2T_hi, h2T_lo = sem("h2T"), sem("h2T_hi"), sem("h2T_lo")
        lgT, lgT_ready = sem("lgT"), sem("lgT_ready")
        lg_done, lg_ready, eg_ready, gate_ready = sem("lg_done"), sem("lg_ready"), sem("eg_ready"), sem("gate_ready")
        base_ready = sem("base_ready")
        mix_done, mix_acc = sem("mix_done"), sem("mix_acc")

        def steps(eng, run):
            run(0, True, False, False, False)
            run(1, True, True, False, False)
            run(2, True, True, True, False)
            run(3, True, True, True, True)
            with eng.Fori(4, B - 1) as s:
                run(s, True, True, True, True)
            run(B - 1, True, True, True, True)
            run(B, False, True, True, True)
            run(B + 1, False, False, True, True)
            run(B + 2, False, False, False, True)

        def apart(eng):
            eng.sem_inc(alone[eng.engine], 1)

        def first_steps(eng, run):
            run(0)
            with eng.Fori(1, B // 2) as i:
                run(i)

        def blocks(h):
            per = P // DH
            return [slice(n % per * DH, (n % per + 1) * DH) for n in (h, h + 1, h + 2, h + 3)]

        def f32(ap):
            return ap.bitcast(F32)

        def tok(dram):
            return dram.rearrange("(j p) d -> p j d", p=P)

        k_hi, k_lo, v_hi, v_lo = (
            [kv_all[:, i * T8 * 4 * H + k:(i + 1) * T8 * 4 * H:4] for i in range(NG)] for k in range(4))
        kv_src = kv_dram.rearrange("(i t) (r c) -> t r i c", t=T8, r=H)
        q_src = q_dram.rearrange("(i t) (r c) -> (t r) i c", t=T8, r=HD)
        o_dst = o_dram.rearrange("(i t) (r c) -> (t r) i c", t=T8, r=HD)
        sum_dst = sum_dram.rearrange("(i t) c -> t i c", t=T8)
        NKV = T8 + 1
        W_LOADS = 16 * 13
        A_CHAIN, B_CHAIN, AB_POOL = 7, 7, 3
        bank_x = [bank_x0, bank_x1]
        turned = [(w0, w1, w2), (bank_m, bank_s, bank_o)]

        def kv_part(j, part):
            return kv_nat[:, j, :, :].rearrange("p r (n l) -> p (r n) l", l=2)[:, :, part]

        block = es.enter_context(nc.Block())

        @block.sync
        def _(sp):
            def load_max(b):
                sp.dma_start(m_rows[:, :],
                             m_dram.rearrange("k (h b) s -> b (k h) s", b=B)[bass.ds(b, 1)]
                             .rearrange("a r s -> (a r) s")).then_inc(mload, 16)

            def load_v(b):
                for j in range(NJ):
                    sp.dma_start(vals[:, j, :, 0:DH],
                                 ctx_in[bass.ds(b, 1), j * P:(j + 1) * P, :]
                                 .rearrange("a p (h e) -> (a p) h e", e=DH)).then_inc(vload, 16)

            sp.wait_ge(zeroed, 1)
            for dst, src in ((gw_raw[0:NH, :], igate_w), (gw_raw[32:GP, :], fgate_w)):
                sp.dma_start(dst, src).then_inc(gwload, 16)

            def load_x(half):
                b = slice(half * B // 2, (half + 1) * B // 2)
                sp.dma_start(x_all[:, b].rearrange("p b j d -> p (b j) d"),
                             x[b].rearrange("b (j p) d -> p (b j) d", p=P)).then_inc(xin[half], 16)

            def load_context(b):
                wait(sp, p_cT[b % 2], b // 2)
                sp.dma_start(cb[b % 2], tok(ctx_in[b])).then_inc(cin[b % 2], 16)

            load_x(0)
            load_context(0)
            load_context(1)
            load_x(1)
            for b in range(2, B):
                load_context(b)
            sp.wait_ge(zeroed_dve, 1)
            for dst, src in (
                    (wq_raw[:, :, :], Wq.rearrange("(c p) n -> p c n", p=P)),
                    (wd_raw[:, :, :], Wdown.rearrange("(c p) n -> p c n", p=P)),
                    (wu_raw[0:L, :], Wup), (wu_raw[L:2 * L, :], Wup),
                    (wg_raw[:, :, 0:E], Wg.rearrange("(c p) n -> p c n", p=P)),
                    (bd_col[0:L, :], bdown.rearrange("(p a) -> p a", a=1)),
                    (bd_col[L:2 * L, :], bdown.rearrange("(p a) -> p a", a=1)),
                    (g1_col[:, :], gamma1.rearrange("(c p) -> p c", p=P)),
                    (g2_col[:, :], gamma2.rearrange("(c p) -> p c", p=P)),
                    (bias_row[:, 0, 0:D], bq.rearrange("(a n) -> a n", a=1)),
                    (bias_row[:, 0, D:3 * D], bup.rearrange("(a n) -> a n", a=1)),
                    (bo_row[:, :], bo.rearrange("(a n) -> a n", a=1).to_broadcast([P, D])),
                    (bg_col[0:E, :], bg.rearrange("(p a) -> p a", a=1))):
                sp.dma_start(dst, src).then_inc(wload, 16)
            for p in range(2):
                sp.wait_ge(p_ge[p], B // 2)
            sp.dma_start(ig[:, :], gates[0:NH, :, :]).then_inc(gload, 16)
            sp.dma_start(fg[:, :], gates[32:GP, :, :]).then_inc(gload, 16)
            load_v(0)
            rows = P // H
            for c in range(NC):
                for r in range(rows):
                    sp.dma_start(wo_raw[r * H:(r + 1) * H, c, :],
                                 Wo.rearrange("(h d) n -> d h n", d=HD)[c * rows + r]).then_inc(woload, 16)
            def run(s, m, a, b, x_on, more):
                f, g, e = s - 1, s - 2, s - 3
                if m:
                    wait(sp, stat2, s)
                    sp.dma_start(xf[:, :, :], tok(x[bass.ds(s, 1)].rearrange("a s d -> (a s) d")))\
                      .then_inc(xload, 16)
                if at(s, 0):
                    sp.wait_ge(bias_ready, 1)
                    sp.dma_start(bias3[:, :], bias_part[:, :, :]).then_inc(bload, 16)
                if b:
                    sp.wait_ge(o_ready, g + 1)
                    apart(sp)
                    wait(sp, o_loaded, 32 * g)
                    sp.dma_start(o_dst, o_grp[:, :].rearrange("p (i c) -> p i c", c=H)).then_inc(o_stored, 16)
                    sp.wait_ge(sum_ready, g + 1)
                    sp.dma_start(sum_dst, sum_grp[:, :].rearrange("p (i c) -> p i c", c=H)).then_inc(o_stored, 16)
                    sp.wait_ge(o_stored, 32 * (g + 1))
                    wait(sp, oT, g)
                    sp.dma_start(o_nat[:, :, :], tok(o_dram)).then_inc(o_loaded, 16)
                    sp.dma_start(sum_nat[:, :, :], tok(sum_dram)).then_inc(o_loaded, 16)
                if a:
                    if at(s, 1):
                        sp.wait_ge(grp_zeroed, 1)
                    sp.wait_ge(q_lo, f + 1)
                    apart(sp)
                    wait(sp, grp_loaded, 16 * NKV * f)
                    sp.dma_start(tok(q_dram), q_nat[:, :, :, :].rearrange("p j r c -> p j (r c)"))\
                      .then_inc(qkv_stored, 16)
                    sp.wait_ge(kv_lo, NJ * (f + 1))
                    sp.dma_start(tok(kv_dram), kv_nat[:, :, :, :].rearrange("p j r c -> p j (r c)"))\
                      .then_inc(qkv_stored, 16)
                    sp.wait_ge(qkv_stored, 32 * (f + 1))
                    wait(sp, values, f)
                    for t in range(T8):
                        sp.dma_start(kv_grp[t * H:(t + 1) * H, :, t, :], kv_src[t]).then_inc(grp_loaded, 16)
                    sp.dma_start(q_grp[:, :, :], q_src).then_inc(grp_loaded, 16)
                if x_on:
                    sp.wait_ge(mix_acc, NX * EC * (e + 1))
                    sp.dma_start(tok(out[bass.ds(e, 1)].rearrange("a s d -> (a s) d")), acc[:, :, :])\
                      .then_inc(stored, 16)
                if more:
                    sp.wait_ge(mb_ready, NH * (s + 1))
                    load_max(s + 1)
                    sp.wait_ge(pv_done, NH * (s + 1))
                    load_v(s + 1)

            sp.wait_ge(m_split, 1)
            sp.dma_start(m_dram.rearrange("k r s -> r k s"), m_part[:, :, :]).then_inc(mstore, 16)
            sp.wait_ge(mstore, 16)
            load_max(0)
            run(0, True, False, False, False, True)
            run(1, True, True, False, False, True)
            run(2, True, True, True, False, True)
            run(3, True, True, True, True, True)
            with sp.Fori(4, B - 1) as s:
                run(s, True, True, True, True, True)
            run(B - 1, True, True, True, True, False)
            run(B, False, True, True, True, False)
            run(B + 1, False, False, True, True, False)
            run(B + 2, False, False, False, True, False)
            sp.wait_ge(stored, 16 * B)

        @block.gpsimd
        def _(pool):
            n = 0

            def made(ins):
                nonlocal n
                ins.then_inc(const_chain, 1)
                n += 1

            for buf, v in ((zero_col, 0.0), (gw_raw, 0.0), (gb_col, 0.0)):
                pool.memset(buf[:, :], v).then_inc(zeroed, 1) if buf is gb_col else made(pool.memset(buf[:, :], v))
            made(pool.memset(ident[:, :], 0.0))
            pool.wait_ge(const_chain, n)
            pool.affine_select(out=ident[:, :], in_=ident[:, :], compare_op=ALU.not_equal, fill=1.0, base=0,
                               pattern=[[-1, P]], channel_multiplier=1).then_inc(ident_ready, 1)
            for buf, v in ((neg_ident, 0.0), (ident_bf, 0.0), (mask_bf, 0.0),
                           (block_ones, 1.0), (ones3, 1.0), (minus_half, -0.5)):
                made(pool.memset(buf[:, :], v))
            made(pool.memset(head_sel[:, :, :], 0.0))
            pool.wait_ge(const_chain, n)
            for m, fill in ((neg_ident, -1.0), (ident_bf, 1.0)):
                made(pool.affine_select(out=m[:, :], in_=m[:, :], compare_op=ALU.not_equal, fill=fill,
                                        base=0, pattern=[[-1, P]], channel_multiplier=1))
            made(pool.affine_select(out=mask_bf[:, :], in_=mask_bf[:, :], compare_op=ALU.is_ge, fill=MASK,
                                    base=0, pattern=[[1, P]], channel_multiplier=-1))
            for k in range(3):
                pool.wait_ge(const_chain, n)
                made(pool.affine_select(out=head_sel[:, :, :], in_=head_sel[:, :, :],
                                        compare_op=ALU.not_equal, fill=1.0, base=-NH * k,
                                        pattern=[[-1, NH], [0, P]], channel_multiplier=1))
            bo_v = block_ones[:, :].rearrange("p (u c) -> p u c", c=HD)
            made(pool.affine_select(out=bo_v, in_=bo_v, compare_op=ALU.is_ge, fill=0.0, base=0,
                                    pattern=[[-HD, T8], [0, HD]], channel_multiplier=1))
            pool.wait_ge(const_chain, n)
            made(pool.affine_select(out=bo_v, in_=bo_v, compare_op=ALU.is_ge, fill=0.0, base=HD - 1,
                                    pattern=[[HD, T8], [0, HD]], channel_multiplier=-1))
            pool.wait_ge(const_chain, n)
            pool.memset(vals[:, :, :, :], 1.0).then_inc(consts, 1)

            def first_pass(i):
                for p in range(2):
                    pool.wait_ge(p_stat[p], i + 1)
                    wait(pool, p_xn[p], i)
                    apart(pool)
                    pool.tensor_scalar(rstd[p][:, :], mv[p][:, :, 1], LN_EPS, None, ALU.add).then_inc(p_var[p], 1)
                    pool.wait_ge(p_var[p], i + 1)
                    pool.tensor_tensor(rstd[p][:, :], rstd[p][:, :], minus_half[:, 0:NJ], ALU.pow)\
                        .then_inc(p_rstd[p], 1)

            first_steps(pool, first_pass)

            def split_weights():
                pool.wait_ge(w_hi_ready, 1)
                for c in range(NC):
                    pool.tensor_tensor(wq_lo[:, c, :].rearrange("p (d h) -> p d h", h=H),
                                      wq_raw[:, c, :].rearrange("p (h d) -> p d h", d=HD),
                                      f32(wq_hi[:, c, :]).rearrange("p (d h) -> p d h", h=H), ALU.subtract)
                pool.tensor_tensor(wo_lo[:, :, :], wo_raw[:, :, :], f32(wo_hi[:, :, :]), ALU.subtract)
                for k in range(2):
                    pool.tensor_tensor(wd_lo[:, :, k, :], wd_raw[:, :, :], f32(wd_hi[:, :, k, :]), ALU.subtract)
                pool.tensor_tensor(wg_lo[:, :, :], wg_raw[:, :, :], f32(wg_hi[:, :, :]), ALU.subtract)
                for k, order in enumerate(("p (h a d) -> p a d h", "p (h a d) -> p a h d")):
                    ins = pool.tensor_tensor(
                        wu_lo[:, :].rearrange("p (r c a) -> p a r c", a=2, c=H)[:, k],
                        wu_raw[0:L, :].rearrange(order, a=2, d=HD)[:, k],
                        f32(wu_hi[0:L, :]).rearrange("p (r c a) -> p a r c", a=2, c=H)[:, k], ALU.subtract)
                ins.then_inc(w_lo_ready, 1)

            def run(s, m, a, b, x_on):
                f, g = s - 1, s - 2
                ch_a, ch_b = Chain(pool, a_pool, AB_POOL * f, AB_POOL), Chain(pool, b_pool, AB_POOL * g, AB_POOL)
                for slot in SLOTS:
                    if slot == "A_cell":
                        if a:
                            wait(pool, hm_read, f)
                            apart(pool)
                            pool.tensor_copy(en_b[:, :, :], en_t[:, :, bass.ds(f, NH, B)]).then_inc(en_ready, 1)
                        if m:
                            wait(pool, d_ready, NH * s)
                            apart(pool)
                            pool.tensor_copy(a_b[:, :, :], a_t[:, :, bass.ds(s, NH, B)]).then_inc(a_ready, 1)
                        if at(s, 0):
                            for c in range(NC):
                                pool.wait_ge(e_hi_ready, c + 1)
                                ins = pool.tensor_tensor(we_lo[:, c, :],
                                                         we_raw[:, c, :, :].rearrange("p e n -> p (e n)"),
                                                         f32(we_hi[:, c, :]), ALU.subtract)
                            ins.then_inc(e_lo_ready, 1)
                            split_weights()
                        if a:
                            pool.wait_ge(stat1, f + 1)
                            apart(pool)
                            ch_a.step(pool.tensor_scalar(fpw[:, 0, :], fmv[:, :, 1], LN_EPS, None, ALU.add))
                            pool.tensor_tensor(frs[:, 0, :], fpw[:, 0, :], minus_half[:, 0:NJ], ALU.pow)\
                                .then_inc(rs_a, 1)
                    if slot == "A_rms" and a:
                        pool.wait_ge(rs_a, f + 1)
                        pool.wait_ge(stat2, f + 1)
                        apart(pool)
                        ch_a.step(pool.tensor_scalar(fpw[:, 0, :], fmv[:, :, 1], LN_EPS, None, ALU.add))
                        apart(pool)
                        ch_a.step(pool.tensor_scalar(fpw[:, 1, :], fmv[:, :, 1], 1.0 + RMS_EPS, LN_EPS * RMS_EPS,
                                                     ALU.mult, ALU.add))
                        pool.tensor_tensor(frs[:, :, :], fpw[:, :, :],
                                           minus_half[:, :].rearrange("p (a b) -> p a b", a=2), ALU.pow)\
                            .then_inc(rs_b, 1)
                        pool.wait_ge(rs_b, f + 1)
                    if slot == "A_norm" and at(s, 1):
                        pool.wait_ge(bload, 16)
                        pool.memset(kv_all[:, :].bitcast(mybir.dt.uint32), 0).then_inc(grp_zeroed, 1)
                    if slot == "B_split" and b:
                        pool.wait_ge(e_hi, g + 1)
                        wait(pool, values, g)
                        pool.tensor_tensor(prob_lo[:, :], prob[:, :], prob_hi[:, :], ALU.subtract)\
                            .then_inc(e_lo, 1)
                    if slot == "B_rms" and b:
                        pool.wait_ge(stat3, g + 1)
                        wait(pool, h2_ready, g)
                        ch_b.step(pool.tensor_tensor(gpw[:, :], gmv[:, :, 0], gmv[:, :, 0], ALU.mult))
                        ch_b.step(pool.tensor_tensor(gpw[:, :], gpw[:, :], gmv[:, :, 1], ALU.add))
                        apart(pool)
                        ch_b.step(pool.tensor_scalar(gpw[:, :], gpw[:, :], RMS_EPS, None, ALU.add))
                        pool.tensor_tensor(grs[:, :], gpw[:, :], minus_half[:, 0:NJ], ALU.pow).then_inc(rs_c, 1)
                    if slot == "B_turn_h2" and a:
                        wait(pool, x2_ready, f)
                        apart(pool)
                        for j in range(NJ):
                            ins = pool.tensor_scalar(y[:, j, :], x1[:, j, :], fmv[:, j, 0:1], frs[:, 0, j:j + 1],
                                                     ALU.subtract, ALU.mult)
                        ins.then_inc(y_normed, 1)
                        if at(s, 1):
                            pool.wait_ge(wload, W_LOADS)
                        pool.wait_ge(y_normed, f + 1)
                        for j in range(NJ):
                            pool.tensor_tensor(y[:, j, :], y[:, j, :], bo_row[:, :], ALU.add).then_inc(y_ready, 1)

            for p in range(2):
                pool.wait_ge(p_xn[p], B // 2)
            pool.memset(zeros[:, :], 0.0).then_inc(zeros_ready, 1)
            pool.wait_ge(rows_ready, 2)
            steps(pool, run)

        @block.scalar
        def _(act):
            act.wait_ge(zeroed, 1)
            for dst, src in ((gb_col[0:NH, :], igate_b.rearrange("(p a) -> p a", a=1)),
                             (gb_col[32:GP, :], fgate_b.rearrange("(p a) -> p a", a=1)),
                             (gx_col[:, :], g_xattn.rearrange("(a n) -> a n", a=1).to_broadcast([P, 1])),
                             (gf_col[:, :], g_ffn.rearrange("(a n) -> a n", a=1).to_broadcast([P, 1])),
                             (ls_row[:, :], ln_scale.rearrange("(a n) -> a n", a=1).to_broadcast([P, D]))):
                act.dma_start(dst, src).then_inc(vecload, 16)
            for c in range(NC):
                act.dma_start(we_raw[:, c, :, :], We.rearrange("e (c p) n -> c p e n", p=P)[c])\
                   .then_inc(eload, 16)
            act.wait_ge(gw_turned, 1)
            act.activation(gw_t[:, :, :].rearrange("p k g -> p (k g)"), bank_x0[:, 0:2 * NC * GP], ACT.Copy)\
               .then_inc(gw_ready, 1)

            def first_pass(i):
                for p in range(2):
                    cols = bass.ds((2 * i + p) * S, S)
                    act.wait_ge(p_qT[p], i + 1)
                    act.activation(qt_all[:, :, cols],
                                   turned[p][0][:, :].rearrange("p (c s) -> p c s", c=NC), ACT.Copy)\
                       .then_inc(p_qe[p], 1)
                act.wait_ge(vecload, 16 * 5)
                for p in range(2):
                    act.wait_ge(p_g[p], i + 1)
                    act.activation(gates[:, bass.ds(2 * i + p, 1), :].rearrange("p a s -> p (a s)"),
                                   turned[p][2][0:GP, 0:S], ACT.Identity, bias=gb_col[:, 0:1])\
                       .then_inc(p_ge[p], 1)

            first_steps(act, first_pass)

            def part_hi(b, h):
                wait(act, s_ready, NH * (b - 1) + h + 1)
                cols, c = bass.ds(b * S, S), h * DH // P
                src, hi_lo, lo_hi, _ = blocks(h)
                for dst, rows in ((k_parts, src), (k_parts, hi_lo), (q_parts, src), (q_parts, lo_hi)):
                    ins = act.activation(dst[rows, h, :], (ct_all if dst is k_parts else qt_all)[src, c, cols],
                                         ACT.Copy)
                ins.then_inc(qk_hi, 1)

            act.activation(tx_col[:, :], gx_col[:, :], ACT.Tanh).then_inc(tanh_ready, 1)
            act.activation(tf_col[:, :], gf_col[:, :], ACT.Tanh).then_inc(tanh_ready, 1)
            act.wait_ge(p_ce[0], B // 2)
            for h in range(2):
                part_hi(0, h)
            act.wait_ge(row_dve, 1)
            act.activation(row_b[:, :], row_a[:, :], ACT.Exp, scale=-1.0).then_inc(row_act, 1)
            act.wait_ge(row_act, 1)
            act.activation(row_c[:, :], row_b[:, :], ACT.Ln, bias=1.0).then_inc(row_act, 1)
            part_hi(0, 2)
            act.wait_ge(row_dve, 6)
            act.activation(en_row[:, :], row_a[:, :], ACT.Exp, scale=-1.0).then_inc(row_act, 1)
            act.wait_ge(rows_turned, 1)
            act.activation(a_t[:, :, :].rearrange("p j r -> p (j r)"), w0[:, 0:NJ * R], ACT.Copy)\
               .then_inc(rows_ready, 1)
            act.activation(en_t[:, :, :].rearrange("p j r -> p (j r)"), w0[:, NJ * R:2 * NJ * R], ACT.Copy,
                           bias=CELL_EPS)\
               .then_inc(rows_ready, 1)

            def split_experts(c):
                act.wait_ge(eload, 16 * NC)
                act.activation(we_hi[:, c, :], we_raw[:, c, :, :].rearrange("p e n -> p (e n)"), ACT.Copy)\
                   .then_inc(e_hi_ready, 1)

            def split_weights():
                act.wait_ge(wload, W_LOADS)
                act.wait_ge(woload, 16 * NC * P // H)
                act.activation(wq_hi[:, :, :].rearrange("p c (d h) -> p c d h", h=H),
                               wq_raw[:, :, :].rearrange("p c (h d) -> p c d h", d=HD), ACT.Copy)
                act.activation(wo_hi[:, :, :], wo_raw[:, :, :], ACT.Copy)
                for k in range(2):
                    act.activation(wd_hi[:, :, k, :], wd_raw[:, :, :], ACT.Copy)
                act.activation(wg_hi[:, :, :], wg_raw[:, :, :], ACT.Copy)
                for k, order in enumerate(("p (h a d) -> p a d h", "p (h a d) -> p a h d")):
                    ins = act.activation(wu_hi[:, :].rearrange("p (r c a) -> p a r c", a=2, c=H)[:, k],
                                         wu_raw[:, :].rearrange(order, a=2, d=HD)[:, k], ACT.Copy)
                ins.then_inc(w_hi_ready, 1)

            def run(s, m, a, b, x_on):
                f, g, e = s - 1, s - 2, s - 3
                for slot in SLOTS:
                    if slot == "A_turn" and a:
                        act.wait_ge(hT, f + 1)
                        wait(act, q_done, f)
                        for c in range(NC):
                            ins = act.activation(ht_hi[:, c, :], w0[:, c * S:(c + 1) * S], ACT.Identity,
                                                 scale=g1_col[:, c:c + 1])
                        ins.then_inc(hT_hi, 1)
                    if slot == "A_down" and a:
                        act.wait_ge(dn, f + 1)
                        wait(act, kv_done, NJ * f)
                        act.activation(dt[:, :], w1[:, 0:S], ACT.Identity, bias=bd_col[:, 0:1])\
                           .then_inc(dn_hi, 1)
                    if slot == "A_q" and a:
                        act.wait_ge(q_done, f + 1)
                        wait(act, qkv_stored, 32 * f)
                        act.activation(q_nat[:, :, :, 0:H].rearrange("p j d c -> p (j d) c"),
                                       w2[:, :].rearrange("p (r c) -> p r c", c=H), ACT.Copy)\
                           .then_inc(q_hi, 1)
                    if slot == "A_kv" and a:
                        for j in range(NJ):
                            act.wait_ge(kv_done, NJ * f + j + 1)
                            act.activation(kv_part(j, 0), (w0, w1)[j][:, :], ACT.Copy).then_inc(kv_hi, 1)
                    if slot[0] == "M" and m:
                        h = int(slot[1:])
                        if h in (NH // 2 + 1, NH):
                            k = 0 if h < NH else 1
                            act.wait_ge(pv_done, NH * s + (k + 1) * NH // 2)
                            wait(act, hm_read, s)
                            act.activation(hm[:, :, k * NH // 2:(k + 1) * NH // 2, :],
                                           bank_o[:, 0:NJ * NH // 2 * VW]
                                           .rearrange("p (j h e) -> p j h e", j=NJ, h=NH // 2), ACT.Copy)\
                               .then_inc(o_evict, 1)
                        if h < NH:
                            act.wait_ge(mb_ready, NH * s + h + 1)
                            wait(act, c_ready, NH * s + h - 1)
                            if h == 0:
                                act.wait_ge(a_ready, s + 1)
                            act.activation(decay[:, h % 2, 0:S], bank_m[:, 0:S], ACT.Exp,
                                           bias=a_b[:, 0, h:h + 1], scale=-1.0)
                            act.activation(decay[:, h % 2, S:TRI], bank_m[:, S:TRI], ACT.Exp,
                                           bias=a_b[:, 1, h:h + 1], scale=-1.0).then_inc(d_ready, 1)
                        if at(s, 0) and h in (1, 2):
                            split_experts(h - 1)
                        if at(s, 0) and h == 4:
                            split_weights()
                        if 0 < h < NH and not at(s, B - 1):
                            part_hi(s + 1, h - 1)
                        if h == 0 and not at(s, 0):
                            part_hi(s, NH - 1)
                    if slot == "B_scores" and b:
                        act.wait_ge(sc_done, g + 1)
                        wait(act, scT, g)
                        act.activation(sc_sb[:, :], w2[:, :], ACT.Copy).then_inc(sc_copied, 1)
                    if slot == "B_shift" and b:
                        act.wait_ge(shifted, g + 1)
                        wait(act, e_lo, g)
                        wait(act, values, g)
                        act.activation(prob_hi[:, :], w2[:, :], ACT.Exp, scale=HSCALE)
                        act.activation(prob[:, :], w2[:, :], ACT.Exp, scale=HSCALE).then_inc(e_hi, 1)
                    if slot == "B_values" and b:
                        act.wait_ge(sums, g + 1)
                        wait(act, o_stored, 32 * g)
                        act.activation(sum_grp[:, :], w1[0:T8, :], ACT.Copy).then_inc(sum_ready, 1)
                        act.wait_ge(values, g + 1)
                        act.activation(o_grp[:, :], w0[:, :], ACT.Copy).then_inc(o_ready, 1)
                    if slot == "B_turn_o" and b:
                        act.wait_ge(oT, g + 1)
                        wait(act, wo_done, g)
                        act.activation(ot_hi[:, :, :].rearrange("p c s -> p (c s)"), w2[:, :], ACT.Copy)\
                           .then_inc(oT_hi, 1)
                    if slot == "B_rms" and b:
                        act.wait_ge(rs_c, g + 1)
                        wait(act, h2T, g)
                        for j in range(NJ):
                            ins = act.activation(h2[:, j, :], x2[:, j, :], ACT.Identity, scale=grs[:, j:j + 1])
                        ins.then_inc(h2_ready, 1)
                    if slot == "B_turn_h2":
                        if b:
                            act.wait_ge(h2T, g + 1)
                            wait(act, mix_done, NX * g)
                            wait(act, lg_done, g)
                            for c in range(NC):
                                ins = act.activation(h2_hi[:, c, :], w0[:, c * S:(c + 1) * S], ACT.Identity,
                                                     scale=g2_col[:, c:c + 1])
                            ins.then_inc(h2T_hi, 1)
                        if a:
                            if at(s, 1):
                                act.wait_ge(w_lo_ready, 1)
                            wait(act, base_ready, f)
                            act.wait_ge(stat2, f + 1)
                            act.activation(x1_old[:, :, :], x1[:, :, :], ACT.Copy).then_inc(x1_kept, 1)
                    if slot == "B_gate" and b:
                        act.wait_ge(lgT, g + 1)
                        wait(act, lg_done, g)
                        act.activation(lg_t[0:32, :], w1[0:32, 0:S], ACT.Identity, bias=bg_col[:, 0:1])\
                           .then_inc(lgT_ready, 1)
                    if slot == "B_logits" and b:
                        act.wait_ge(lg_ready, g + 1)
                        act.activation(lg[:, :, :], lg[:, :, :], ACT.Exp).then_inc(eg_ready, 1)

            for h in range(3, NH):
                part_hi(0, h)
            steps(act, run)

        @block.vector
        def _(dve):
            dve.memset(bg_col[:, :], 0.0)
            dve.memset(lg_t[:, :], 0.0)
            for buf in (wg_raw, bias_row):
                ins = dve.memset(buf[:, :, :], 0.0)
            ins.then_inc(zeroed_dve, 1)
            dve.wait_ge(gwload, 16 * 2)
            dve.tensor_tensor(gw_kv[:, :], gw_raw[:, D:2 * D], gw_raw[:, 2 * D:3 * D], ALU.add).then_inc(gw_sum, 1)
            def first_pass(i):
                dve.wait_ge(xin[0 if at(i, 0) else 1], 16)
                for p in range(2):
                    for j in range(NJ):
                        ins = dve.bn_stats(bs[p][:, j, :], x_all[:, 2 * i + p, j, :])
                    ins.then_inc(p_bs[p], 1)
                    dve.wait_ge(p_bs[p], i + 1)
                    apart(dve)
                    for j in range(NJ):
                        ins = dve.bn_aggr(mv[p][:, j, :], bs[p][:, j, :])
                    ins.then_inc(p_stat[p], 1)
                for p in range(2):
                    dve.wait_ge(p_rstd[p], i + 1)
                    wait(dve, p_qT[p], i)
                    for j in range(NJ):
                        ins = dve.tensor_scalar(xn[p][:, j, :], x_all[:, 2 * i + p, j, :], mv[p][:, j, 0:1],
                                                rstd[p][:, j:j + 1], ALU.subtract, ALU.mult)
                    ins.then_inc(p_xn[p], 1)
                    dve.wait_ge(p_cT[p], i + 1)
                    dve.tensor_copy(ct_all[:, :, bass.ds((2 * i + p) * S, S)],
                                    turned[p][1][:, :].rearrange("p (c s) -> p c s", c=NC)).then_inc(p_ce[p], 1)

            first_steps(dve, first_pass)

            dve.wait_ge(tanh_ready, 2)
            dve.tensor_scalar(lst_row[:, :], ls_row[:, :], tx_col[:, 0:1], None, ALU.mult).then_inc(scale_ready, 1)
            dve.wait_ge(scale_ready, 1)
            for h in range(NH):
                zero = blocks(h)[3]
                for dst in (k_parts, q_parts):
                    ins = dve.tensor_copy(dst[zero, h, :], zero_col[zero, 0:1].to_broadcast([DH, S]))
            ins.then_inc(parts_zeroed, 1)

            rows = Chain(dve, row_dve, 0, 6)
            dve.wait_ge(gload, 32)
            rows.step(dve.scalar_tensor_tensor(out=row_a[:, :], in0=fg[:, :], scalar=-1.0, in1=fg[:, :],
                                               op0=ALU.mult, op1=ALU.max))
            dve.wait_ge(row_act, 2)
            rows.step(dve.scalar_tensor_tensor(out=row_a[:, :], in0=fg[:, :], scalar=0.0, in1=row_c[:, :],
                                               op0=ALU.min, op1=ALU.subtract))
            dve.wait_ge(zeros_ready, 1)
            rows.step(dve.tensor_tensor_scan(row_b[:, :], row_a[:, :], zeros[:, :], 0.0, ALU.add, ALU.add))
            rows.step(dve.tensor_tensor(row_c[:, :], ig[:, :], row_b[:, :], ALU.subtract))
            rows.step(dve.tensor_tensor_scan(row_m[:, :], row_c[:, :], row_c[:, :], -3.0e38, ALU.max, ALU.max))
            rows.step(dve.tensor_tensor(row_a[:, :], row_b[:, :], row_m[:, :], ALU.add))
            parts = Chain(dve, prep_chain, 0, 9)
            parts.step(dve.tensor_copy(m_part[:, 0, :], row_m[:, :]))
            parts.step(dve.tensor_tensor(row_b[:, :], row_m[:, :], m_part[:, 0, :], ALU.subtract))
            parts.step(dve.tensor_copy(m_part[:, 1, :], row_b[:, :]))
            parts.step(dve.tensor_tensor(fg[:, :], row_b[:, :], m_part[:, 1, :], ALU.subtract))
            dve.tensor_copy(m_part[:, 2, :], fg[:, :]).then_inc(m_split, 1)

            def split_biases(n):
                if n == 0:
                    dve.wait_ge(wload, W_LOADS)
                    for k, order in enumerate(("p (h a d) -> p a d h", "p (h a d) -> p a h d")):
                        dve.tensor_copy(bias_row[:, 1, D:3 * D].rearrange("p (r c a) -> p a r c", a=2, c=H)[:, k],
                                        bias_row[:, 0, D:3 * D].rearrange(order, a=2, d=HD)[:, k])
                    parts.step(dve.tensor_copy(bias_row[:, 1, 0:D].rearrange("p (d h) -> p d h", h=H),
                                               bias_row[:, 0, 0:D].rearrange("p (h d) -> p d h", d=HD)))
                elif n in (1, 3):
                    parts.step(dve.tensor_copy(bias_part[:, n // 2, :], bias_row[:, 1 + n // 2, :]))
                elif n in (2, 4):
                    parts.step(dve.tensor_tensor(bias_row[:, 2 if n == 2 else 0, :], bias_row[:, n // 2, :],
                                                 bias_part[:, n // 2 - 1, :], ALU.subtract))
                elif n == 5:
                    dve.tensor_copy(bias_part[:, 2, :], bias_row[:, 0, :]).then_inc(bias_ready, 1)

            def part_lo(b, h):
                dve.wait_ge(qk_hi, NH * b + h + 1)
                cols, c = bass.ds(b * S, S), h * DH // P
                src, hi_lo, lo_hi, _ = blocks(h)
                dve.tensor_tensor(k_parts[lo_hi, h, :], ct_all[src, c, cols], f32(k_parts[src, h, :]), ALU.subtract)
                dve.tensor_tensor(q_parts[hi_lo, h, :], qt_all[src, c, cols], f32(q_parts[src, h, :]), ALU.subtract)\
                   .then_inc(qk_lo, 1)

            def stats(ch, src, done, index, bn, mean_var):
                for j in range(NJ):
                    ins = dve.bn_stats(bn[:, j, :], src[:, j, :])
                ch.step(ins)
                apart(dve)
                for j in range(NJ):
                    ins = dve.bn_aggr(mean_var[:, j, :], bn[:, j, :])
                ins.then_inc(done, 1)

            def run(s, m, a, b, x_on):
                f, g, e = s - 1, s - 2, s - 3
                ch_a, ch_b = Chain(dve, a_chain, A_CHAIN * f, A_CHAIN), Chain(dve, b_chain, B_CHAIN * g, B_CHAIN)
                for slot in SLOTS:
                    if slot == "A_cell" and a:
                        if at(s, 1):
                            dve.wait_ge(e_lo_ready, 1)
                        dve.wait_ge(o_evict, 2 * (f + 1))
                        dve.wait_ge(en_ready, f + 1)
                        ch_a.step(dve.scalar_tensor_tensor(out=nrm[:, :, :], in0=hm[:, :, :, DH], scalar=-1.0,
                                                           in1=hm[:, :, :, DH], op0=ALU.mult, op1=ALU.max))
                        ch_a.step(dve.scalar_tensor_tensor(out=nrm[:, :, :], in0=nrm[:, :, :], scalar=CELL_EPS,
                                                           in1=en_b[:, :, :], op0=ALU.add, op1=ALU.max))
                        ch_a.step(dve.reciprocal(nrm[:, :, :], nrm[:, :, :]))
                        dve.tensor_tensor(hcell[:, :, :].rearrange("p j (h e) -> p (j h) e", e=DH),
                                          hm[:, :, :, 0:DH].rearrange("p j h e -> p (j h) e"),
                                          nrm[:, :, :].rearrange("p j h -> p (j h)").unsqueeze(2)
                                          .to_broadcast([P, NJ * NH, DH]), ALU.mult).then_inc(hm_read, 1)
                        dve.wait_ge(hm_read, f + 1)
                        wait(dve, y_normed, f)
                        stats(ch_a, hcell, stat1, f, fbs, fmv)
                    if slot == "A_x1" and a:
                        dve.wait_ge(stat1, f + 1)
                        for j in range(NJ):
                            ins = dve.scalar_tensor_tensor(out=hcell[:, j, :], in0=hcell[:, j, :],
                                                           scalar=fmv[:, j, 0:1], in1=lst_row[:, :],
                                                           op0=ALU.subtract, op1=ALU.mult)
                        ch_a.step(ins)
                        dve.wait_ge(rs_a, f + 1)
                        dve.wait_ge(xload, 16 * (f + 1))
                        wait(dve, x1_kept, f)
                        for j in range(NJ):
                            ins = dve.scalar_tensor_tensor(out=x1[:, j, :], in0=hcell[:, j, :],
                                                           scalar=frs[:, 0, j:j + 1], in1=xf[:, j, :],
                                                           op0=ALU.mult, op1=ALU.add)
                        ch_a.step(ins)
                        stats(ch_a, x1, stat2, f, fbs, fmv)
                    if slot == "A_norm" and a:
                        dve.wait_ge(stat2, f + 1)
                        dve.wait_ge(rs_b, f + 1)
                        wait(dve, hT, f)
                        for j in range(NJ):
                            ins = dve.tensor_scalar(hn[:, j, :], x1[:, j, :], fmv[:, j, 0:1], frs[:, 1, j:j + 1],
                                                    ALU.subtract, ALU.mult)
                        ins.then_inc(hn_ready, 1)
                        assert ch_a.n == A_CHAIN
                    if slot == "A_turn" and a:
                        dve.wait_ge(hT_hi, f + 1)
                        wait(dve, q_done, f)
                        for c in range(NC):
                            ins = dve.scalar_tensor_tensor(out=ht_lo[:, c, :], in0=w0[:, c * S:(c + 1) * S],
                                                           scalar=g1_col[:, c:c + 1], in1=f32(ht_hi[:, c, :]),
                                                           op0=ALU.mult, op1=ALU.subtract)
                        ins.then_inc(hT_lo, 1)
                    if slot == "A_down" and a:
                        dve.wait_ge(dn_hi, f + 1)
                        dve.scalar_tensor_tensor(out=dt[L:P, :], in0=w1[L:P, 0:S], scalar=bd_col[L:P, 0:1],
                                                 in1=f32(dt[L:P, :]), op0=ALU.add, op1=ALU.subtract)\
                           .then_inc(dn_lo, 1)
                    if slot == "A_q" and a:
                        dve.wait_ge(q_hi, f + 1)
                        q_v = q_nat[:, :, :, :].rearrange("p j d c -> p (j d) c")
                        dve.tensor_tensor(q_v[:, :, H:2 * H], w2[:, :].rearrange("p (r c) -> p r c", c=H),
                                          q_v[:, :, 0:H], ALU.subtract).then_inc(q_lo, 1)
                    if slot == "A_kv" and a:
                        for j in range(NJ):
                            dve.wait_ge(kv_hi, NJ * f + j + 1)
                            dve.tensor_tensor(kv_part(j, 1), (w0, w1)[j][:, :], kv_part(j, 0), ALU.subtract)\
                               .then_inc(kv_lo, 1)
                    if slot[0] == "M" and m and int(slot[1:]) < NH:
                        h = int(slot[1:])
                        dve.wait_ge(s_ready, NH * s + h + 1)
                        dve.wait_ge(d_ready, NH * s + h + 1)
                        wait(dve, pv_done, NH * s + h - 1)
                        dve.scalar_tensor_tensor(out=cell[:, h % 2, :], in0=bank_s[:, 0:TRI], scalar=QSCALE,
                                                 in1=decay[:, h % 2, :], op0=ALU.mult, op1=ALU.mult)\
                           .then_inc(c_ready, 1)
                        if at(s, 0):
                            split_biases(h)
                    if slot[0] == "M" and m:
                        h = int(slot[1:])
                        if 2 <= h < NH and not at(s, B - 1):
                            part_lo(s + 1, h - 2)
                        if h < 2 and not at(s, 0):
                            part_lo(s, NH - 2 + h)
                    if slot == "B_max" and b:
                        dve.wait_ge(scT, g + 1)
                        wait(dve, shifted, g)
                        ch_b.step(dve.tensor_reduce(smax[:, :], w0[:, :].rearrange("p (r g) -> p r g", g=H),
                                                    AX.X, ALU.max))
                        dve.tensor_copy(smax_x[:, :, :], smax[:, :].unsqueeze(2).to_broadcast([P, 4 * T8, H]))\
                           .then_inc(max_ready, 1)
                    if slot == "B_o" and b:
                        dve.wait_ge(o_loaded, 32 * (g + 1))
                        ch_b.step(dve.reciprocal(rsum[:, :, :], sum_nat[:, :, :]))
                        dve.tensor_tensor(o_nat[:, :, :].rearrange("p j (d h) -> p j d h", h=H),
                                          o_nat[:, :, :].rearrange("p j (d h) -> p j d h", h=H),
                                          rsum[:, :, :].unsqueeze(2).to_broadcast([P, NJ, HD, H]), ALU.mult)\
                           .then_inc(o_normed, 1)
                    if slot == "B_turn_o" and b:
                        dve.wait_ge(oT_hi, g + 1)
                        wait(dve, wo_done, g)
                        dve.tensor_tensor(ot_lo[:, :, :].rearrange("p c s -> p (c s)"), w2[:, :],
                                          f32(ot_hi[:, :, :]).rearrange("p c s -> p (c s)"), ALU.subtract)\
                           .then_inc(oT_lo, 1)
                    if slot == "B_wo" and b:
                        dve.wait_ge(wo_done, g + 1)
                        dve.wait_ge(y_ready, NJ * (g + 1))
                        wait(dve, h2_ready, g)
                        dve.tensor_tensor(x2[:, :, :].rearrange("p j d -> p (j d)"), w1[:, :],
                                          y[:, :, :].rearrange("p j d -> p (j d)"), ALU.add).then_inc(x2_ready, 1)
                        dve.wait_ge(x2_ready, g + 1)
                        stats(ch_b, x2, stat3, g, gbs, gmv)
                    if slot == "X7" and b:
                        dve.wait_ge(x1_kept, g + 1)
                        dve.scalar_tensor_tensor(out=base[:, :, :], in0=x2[:, :, :], scalar=tf_col[:, 0:1],
                                                 in1=x1_old[:, :, :], op0=ALU.mult, op1=ALU.add)\
                           .then_inc(base_ready, 1)
                    if slot == "B_turn_h2" and b:
                        dve.wait_ge(h2T_hi, g + 1)
                        for c in range(NC):
                            ins = dve.scalar_tensor_tensor(out=h2_lo[:, c, :], in0=w0[:, c * S:(c + 1) * S],
                                                           scalar=g2_col[:, c:c + 1], in1=f32(h2_hi[:, c, :]),
                                                           op0=ALU.mult, op1=ALU.subtract)
                        ins.then_inc(h2T_lo, 1)
                    if slot == "B_logits" and b:
                        logits = w1[:, S:S + NJ * P].rearrange("p (j n) -> p j n", j=NJ)[:, :, 0:E]
                        dve.wait_ge(lg_done, g + 1)
                        ch_b.step(dve.tensor_reduce(gmax[:, :], logits, AX.X, ALU.max))
                        dve.tensor_tensor(lg[:, :, :], logits, gmax[:, :].unsqueeze(2).to_broadcast([P, NJ, E]),
                                          ALU.subtract).then_inc(lg_ready, 1)
                        dve.wait_ge(eg_ready, g + 1)
                        ch_b.step(dve.tensor_reduce(gmax[:, :], lg[:, :, :], AX.X, ALU.add))
                        ch_b.step(dve.reciprocal(gmax[:, :], gmax[:, :]))
                        ch_b.step(dve.tensor_scalar(gmax[:, :], gmax[:, :], tf_col[:, 0:1], None, ALU.mult))
                        dve.tensor_tensor(gate[:, :, :], lg[:, :, :],
                                          gmax[:, :].unsqueeze(2).to_broadcast([P, NJ, E]), ALU.mult)\
                           .then_inc(gate_ready, 1)
                        assert ch_b.n == B_CHAIN
                    if slot[0] == "X" and x_on:
                        k = int(slot[1:])
                        j, n = divmod(k, E // EC)
                        if k == 0:
                            wait(dve, stored, 16 * e)
                            dve.wait_ge(gate_ready, e + 1)
                            dve.wait_ge(base_ready, e + 1)
                        dve.wait_ge(mix_done, NX * e + k + 1)
                        for u in range(EC):
                            ex = EC * n + u
                            dve.scalar_tensor_tensor(out=acc[:, j, :], in0=bank_x[k % 2][:, u * D:(u + 1) * D],
                                                     scalar=gate[:, j, ex:ex + 1],
                                                     in1=(base if ex == 0 else acc)[:, j, :],
                                                     op0=ALU.mult, op1=ALU.add).then_inc(mix_acc, 1)
                            dve.wait_ge(mix_acc, NX * EC * e + EC * k + u + 1)

            for h in range(NH):
                part_lo(0, h)
            steps(dve, run)

        @block.tensor
        def _(pe):
            def split_mm(dst, a_hi, a_lo, b_hi, b_lo, start, stop):
                pe.matmul(dst, a_hi, b_hi, start=start, stop=False, skip_group_check=True)
                pe.matmul(dst, a_hi, b_lo, start=False, stop=False, skip_group_check=True)
                return pe.matmul(dst, a_lo, b_hi, start=False, stop=stop, skip_group_check=True)

            def bias_mm(dst, name):
                off, size = BIAS[name]
                return pe.matmul(dst, ones3[:, :], bias3[:, off:off + size], start=False, stop=True,
                                 skip_group_check=True)

            pe.wait_ge(ident_ready, 1)
            pe.wait_ge(gwload, 32)
            pe.wait_ge(gw_sum, 1)
            for k in range(2 * NC):
                src = gw_raw[:, k * P:(k + 1) * P] if k < NC else gw_kv[:, (k - NC) * P:(k - NC + 1) * P]
                ins = pe.transpose(bank_x0[:, k * GP:(k + 1) * GP], src, ident[0:GP, 0:GP])
            ins.then_inc(gw_turned, 1)
            pe.wait_ge(gw_ready, 1)

            def first_pass(i):
                for p in range(2):
                    pe.wait_ge(cin[p], 16 * (i + 1))
                    wait(pe, p_ce[p], i)
                    for c in range(NC):
                        for j in range(NJ):
                            ins = pe.transpose(turned[p][1][:, c * S + j * P:c * S + (j + 1) * P],
                                               cb[p][:, j, c * P:(c + 1) * P], ident[:, :])
                    ins.then_inc(p_cT[p], 1)
                for p in range(2):
                    pe.wait_ge(p_xn[p], i + 1)
                    wait(pe, p_qe[p], i)
                    for c in range(NC):
                        for j in range(NJ):
                            ins = pe.transpose(turned[p][0][:, c * S + j * P:c * S + (j + 1) * P],
                                               xn[p][:, j, c * P:(c + 1) * P], ident[:, :])
                    ins.then_inc(p_qT[p], 1)
                for p in range(2):
                    pe.wait_ge(p_qe[p], i + 1)
                    pe.wait_ge(p_ce[p], i + 1)
                    wait(pe, p_ge[p], i)
                    cols = bass.ds((2 * i + p) * S, S)
                    for k in range(2 * NC):
                        src = (qt_all if k < NC else ct_all)[:, k % NC, cols]
                        ins = pe.matmul(turned[p][2][0:GP, 0:S], gw_t[:, k, :], src,
                                        start=(k == 0), stop=(k == 2 * NC - 1))
                    ins.then_inc(p_g[p], 1)

            first_steps(pe, first_pass)

            pe.wait_ge(row_act, 3)
            pe.wait_ge(p_qe[0], B // 2)
            for k, src in enumerate((row_c, en_row)):
                for j in range(NJ):
                    ins = pe.transpose(w0[:, (k * NJ + j) * R:(k * NJ + j + 1) * R], src[:, j * P:(j + 1) * P],
                                       ident[0:R, 0:R])
            ins.then_inc(rows_turned, 1)

            def run(s, m, a, b, x_on):
                f, g, e = s - 1, s - 2, s - 3
                for slot in SLOTS:
                    if slot == "A_turn" and a:
                        pe.wait_ge(hn_ready, f + 1)
                        if b:
                            pe.wait_ge(o_ready, g + 1)
                        for c in range(NC):
                            for j in range(NJ):
                                ins = pe.transpose(w0[:, c * S + j * P:c * S + (j + 1) * P],
                                                   hn[:, j, c * P:(c + 1) * P], ident[:, :])
                        ins.then_inc(hT, 1)
                    if slot == "A_down" and a:
                        if at(s, 1):
                            pe.wait_ge(w_lo_ready, 1)
                            pe.wait_ge(bload, 16)
                        pe.wait_ge(hT_lo, f + 1)
                        if b:
                            pe.wait_ge(sum_ready, g + 1)
                        for c in range(NC):
                            ins = split_mm(w1[:, 0:S], wd_hi[:, c, :, :].rearrange("p a l -> p (a l)"),
                                           wd_lo[:, c, :, :].rearrange("p a l -> p (a l)"),
                                           ht_hi[:, c, :], ht_lo[:, c, :], c == 0, c == NC - 1)
                        ins.then_inc(dn, 1)
                    if slot == "A_q" and a:
                        if b:
                            pe.wait_ge(e_hi, g + 1)
                        for j in range(NJ):
                            dst = w2[:, j * D:(j + 1) * D]
                            for c in range(NC):
                                split_mm(dst, ht_hi[:, c, j * P:(j + 1) * P], ht_lo[:, c, j * P:(j + 1) * P],
                                         wq_hi[:, c, :], wq_lo[:, c, :], c == 0, False)
                            ins = bias_mm(dst, "q")
                        ins.then_inc(q_done, 1)
                    if slot == "A_kv" and a:
                        pe.wait_ge(dn_lo, f + 1)
                        for j in range(NJ):
                            dst = (w0, w1)[j][:, :]
                            tk = slice(j * P, (j + 1) * P)
                            pe.matmul(dst, dt[:, tk], wu_hi[:, :], start=True, stop=False, skip_group_check=True)
                            pe.matmul(dst, dt[0:L, tk], wu_lo[:, :], start=False, stop=False, skip_group_check=True)
                            bias_mm(dst, "up").then_inc(kv_done, 1)
                    if slot[0] == "M" and m:
                        h = int(slot[1:])
                        if h == 0:
                            pe.wait_ge(mload, 16 * (s + 1))
                        if h < NH:
                            wait(pe, d_ready, NH * s + h)
                            sel = head_sel[:, h, :]
                            pe.matmul(bank_m[:, 0:S], sel, m_rows[:, :], start=True, stop=False, skip_group_check=True)
                            pe.matmul(bank_m[:, S:TRI], sel, m_rows[:, P:S], start=False, stop=False,
                                      skip_group_check=True)
                            pe.matmul(bank_m[:, 0:P], ident_bf[:, :], mask_bf[:, :], start=False, stop=False,
                                      skip_group_check=True)
                            pe.matmul(bank_m[:, S:TRI], ident_bf[:, :], mask_bf[:, :], start=False, stop=True,
                                      skip_group_check=True).then_inc(mb_ready, 1)
                            wait(pe, c_ready, NH * s + h)
                            pe.wait_ge(qk_lo, NH * s + h + 1)
                            pe.matmul(bank_s[:, 0:S], k_parts[:, h, 0:P], q_parts[:, h, :], start=True,
                                      stop=False, skip_group_check=True)
                            pe.matmul(bank_s[:, S:TRI], k_parts[:, h, P:S], q_parts[:, h, P:S], start=False,
                                      stop=True, skip_group_check=True).then_inc(s_ready, 1)
                        if h > 0:
                            done = h - 1
                            if h == 1:
                                pe.wait_ge(vload, 16 * NJ * (s + 1))
                            pe.wait_ge(c_ready, NH * s + h)
                            if done % (NH // 2) == 0:
                                wait(pe, o_evict, 2 * s + done // (NH // 2))
                            for j in range(NJ):
                                col = (j * NH // 2 + done % (NH // 2)) * VW
                                dst = bank_o[:, col:col + VW]
                                if j == 0:
                                    pe.matmul(dst, cell[:, done % 2, 0:P], vals[:, 0, done, :], start=True, stop=True)
                                else:
                                    pe.matmul(dst, cell[:, done % 2, P:S], vals[:, 0, done, :], start=True, stop=False)
                                    pe.matmul(dst, cell[:, done % 2, S:TRI], vals[:, 1, done, :], start=False, stop=True)\
                                      .then_inc(pv_done, 1)
                    if slot == "B_scores" and b:
                        if at(s, 2):
                            pe.wait_ge(grp_zeroed, 1)
                        pe.wait_ge(grp_loaded, 16 * NKV * (g + 1))
                        wait(pe, oT_lo, g)
                        pe.wait_ge(q_lo, g + 1)
                        for i in range(NG):
                            dst = w2[:, i * H:(i + 1) * H]
                            ins = split_mm(dst, k_hi[i], k_lo[i], q_grp[:, i, 0:H], q_grp[:, i, H:2 * H],
                                           i == 0, i == NG - 1)
                        ins.then_inc(sc_done, 1)
                    if slot == "B_max" and b:
                        pe.wait_ge(sc_copied, g + 1)
                        wait(pe, h2T_lo, g)
                        pe.wait_ge(kv_lo, NJ * (g + 1))
                        for col in range(4):
                            ins = pe.transpose(w0[:, col * P:(col + 1) * P], sc_sb[:, col * P:(col + 1) * P], ident[:, :])
                        ins.then_inc(scT, 1)
                    if slot == "B_shift" and b:
                        pe.wait_ge(max_ready, g + 1)
                        for col in range(4):
                            ins = pe.matmul(w2[:, col * P:(col + 1) * P],
                                            smax_x[:, col * T8:(col + 1) * T8, :].rearrange("p t g -> p (t g)"), neg_ident[:, :],
                                            start=False, stop=(col == 3), skip_group_check=True)
                        ins.then_inc(shifted, 1)
                    if slot == "B_values" and b:
                        pe.wait_ge(e_hi, g + 1)
                        pe.wait_ge(e_lo, g + 1)
                        wait(pe, lg_ready, g)
                        pe.matmul(w1[0:T8, :], block_ones[:, 0:P:H], prob_hi[:, :], start=True, stop=False)
                        pe.matmul(w1[0:T8, :], block_ones[:, 0:P:H], prob_lo[:, :], start=False, stop=True)\
                          .then_inc(sums, 1)
                        for i in range(NG):
                            c = slice(i * H, (i + 1) * H)
                            ins = split_mm(w0[:, c], v_hi[i], v_lo[i], prob_hi[:, c], prob_lo[:, c],
                                           i == 0, i == NG - 1)
                        ins.then_inc(values, 1)
                    if slot == "B_turn_o" and b:
                        pe.wait_ge(o_normed, g + 1)
                        if a:
                            pe.wait_ge(q_lo, f + 1)
                        for c in range(NC):
                            for j in range(NJ):
                                ins = pe.transpose(w2[:, c * S + j * P:c * S + (j + 1) * P],
                                                   o_nat[:, j, c * P:(c + 1) * P], ident[:, :])
                        ins.then_inc(oT, 1)
                    if slot == "B_wo" and b:
                        pe.wait_ge(oT_lo, g + 1)
                        if a:
                            pe.wait_ge(kv_lo, NJ * (f + 1))
                        for j in range(NJ):
                            dst = w1[:, j * D:(j + 1) * D]
                            for c in range(NC):
                                ins = split_mm(dst, ot_hi[:, c, j * P:(j + 1) * P], ot_lo[:, c, j * P:(j + 1) * P],
                                               wo_hi[:, c, :], wo_lo[:, c, :], c == 0, c == NC - 1)
                        ins.then_inc(wo_done, 1)
                    if slot == "B_turn_h2" and b:
                        pe.wait_ge(h2_ready, g + 1)
                        if a:
                            pe.wait_ge(kv_lo, NJ * (f + 1))
                        for c in range(NC):
                            for j in range(NJ):
                                ins = pe.transpose(w0[:, c * S + j * P:c * S + (j + 1) * P],
                                                   h2[:, j, c * P:(c + 1) * P], ident[:, :])
                        ins.then_inc(h2T, 1)
                    if slot == "B_gate" and b:
                        pe.wait_ge(h2T_lo, g + 1)
                        pe.wait_ge(x2_ready, g + 1)
                        for c in range(NC):
                            ins = split_mm(w1[0:32, 0:S], wg_hi[:, c, :], wg_lo[:, c, :], h2_hi[:, c, :],
                                           h2_lo[:, c, :], c == 0, c == NC - 1)
                        ins.then_inc(lgT, 1)
                    if slot == "B_logits" and b:
                        pe.wait_ge(lgT_ready, g + 1)
                        for j in range(NJ):
                            ins = pe.transpose(w1[:, S + j * P:S + (j + 1) * P], lg_t[:, j * P:(j + 1) * P],
                                               ident[:, :])
                        ins.then_inc(lg_done, 1)
                    if slot[0] == "X" and x_on:
                        k = int(slot[1:])
                        j, n = divmod(k, E // EC)
                        if k < 2:
                            if at(s, 3):
                                pe.wait_ge(e_lo_ready, 1)
                            wait(pe, mix_acc, NX * EC * e)
                        else:
                            pe.wait_ge(mix_acc, NX * EC * e + EC * (k - 1))
                        cols = slice(n * 512, (n + 1) * 512)
                        for c in range(NC):
                            ins = split_mm(bank_x[k % 2][:, :], h2_hi[:, c, j * P:(j + 1) * P],
                                           h2_lo[:, c, j * P:(j + 1) * P], we_hi[:, c, cols], we_lo[:, c, cols],
                                           c == 0, c == NC - 1)
                        ins.then_inc(mix_done, 1)

            pe.wait_ge(rows_ready, 2)
            pe.wait_ge(consts, 1)
            pe.wait_ge(parts_zeroed, 1)
            for p in range(2):
                pe.wait_ge(p_ge[p], B // 2)
                pe.wait_ge(p_ce[p], B // 2)
            steps(pe, run)


_INS = ["x", "ctx_1024", "g_xattn", "g_ffn", "L0_xattn_igate_w", "L0_xattn_igate_b", "L0_xattn_fgate_w",
        "L0_xattn_fgate_b", "L0_xattn_ln_scale", "L0_ffn_gamma1", "L0_ffn_Wq", "L0_ffn_bq", "L0_ffn_Wdown",
        "L0_ffn_bdown", "L0_ffn_Wup", "L0_ffn_bup", "L0_ffn_Wo", "L0_ffn_bo", "L0_ffn_gamma2", "L0_ffn_Wg",
        "L0_ffn_bg", "L0_ffn_We"]


def kernel(**inputs):
    import numpy as np
    import concourse.bacc as bacc
    from concourse.bass_utils import run_bass_kernel_spmd

    nc = bacc.Bacc("TRN2", target_bir_lowering=False, num_devices=1)
    arrays, args = {}, []
    for name in _INS:
        a = np.ascontiguousarray(inputs[name])
        arrays[f"in_{name}"] = a
        args.append(nc.dram_tensor(f"in_{name}", a.shape, mybir.dt.from_np(a.dtype), kind="ExternalInput").ap())
    out = nc.dram_tensor("out", arrays["in_x"].shape, F32, kind="ExternalOutput").ap()
    build(nc, *args, out)
    r = run_bass_kernel_spmd(nc, [arrays], core_ids=[0])
    return r.results[0]["out"]
```
